# Optimizing a Trainium2 kernel written in Bass

```python
import numpy as np
import jax
import jax.numpy as jnp

def _softmax(x, axis=-1):
    return jax.nn.softmax(x, axis=axis)

def _gelu(x):
    return jax.nn.gelu(x, approximate=True)

def _silu(x):
    return jax.nn.silu(x)

def _sigmoid(x):
    return jax.nn.sigmoid(x)

def _layernorm(x, axis=-1, eps=1e-05):
    m = jnp.mean(x, axis=axis, keepdims=True)
    v = jnp.var(x, axis=axis, keepdims=True)
    return (x - m) / jnp.sqrt(v + eps)

def _scatter_add(tgt, idx, src, axis=0):
    return tgt.at[idx].add(src)

def _segment_sum(src, seg, n):
    return jax.ops.segment_sum(src, seg, n)
kernel_name = 'mk_seq_postln_d2_jaxref_r8_0a75c8'

def setup_inputs(seed: int=0):
    np.random.seed(seed)
    _w = jnp.asarray

    def _L0_attn_setup():
        import jax, jax.numpy as jnp
        import numpy as np
        N_HEAD = 16
        LATENT = 32

        def _rotate_half(x):
            xe = x[..., ::2]
            xo = x[..., 1::2]
            return jnp.stack((-xo, xe), axis=-1).reshape(x.shape)

        def _rope_tables(T, latent_dim, dtype):
            inv_freq = 1.0 / 10000.0 ** (jnp.arange(0, latent_dim, 2, dtype=jnp.float32) / latent_dim)
            t = jnp.arange(T, dtype=jnp.float32)
            freqs = jnp.outer(t, inv_freq)
            cos = jnp.repeat(jnp.cos(freqs), 2, axis=-1)[:, :latent_dim]
            sin = jnp.repeat(jnp.sin(freqs), 2, axis=-1)[:, :latent_dim]
            return (cos.astype(dtype), sin.astype(dtype))
        key = jax.random.key(seed)
        ks = jax.random.split(key, 14)
        C = 128
        hd = C // N_HEAD
        L = LATENT
        s = 0.02
        return {'x': jax.random.normal(ks[0], (4, 256, C), jnp.float32), 'c_attn_w': jax.random.normal(ks[1], (3 * C, C), jnp.float32) * s, 'c_attn_b': jnp.zeros((3 * C,), jnp.float32), 'q2l_w': jax.random.normal(ks[2], (L, hd), jnp.float32) * s, 'q2l_b': jnp.zeros((L,), jnp.float32), 'kv2l_w': jax.random.normal(ks[3], (L, hd), jnp.float32) * s, 'kv2l_b': jnp.zeros((L,), jnp.float32), 'l2o_w': jax.random.normal(ks[4], (hd, L), jnp.float32) * s, 'l2o_b': jnp.zeros((hd,), jnp.float32), 'wqk_w': jax.random.normal(ks[5], (L, L), jnp.float32) * s, 'wqk_b': jnp.zeros((L,), jnp.float32), 'cproj_w': jax.random.normal(ks[6], (C, C), jnp.float32) * s, 'cproj_b': jnp.zeros((C,), jnp.float32)}
    _L0_attn_in = _L0_attn_setup()

    def _L0_ffn_setup():
        import jax, jax.numpy as jnp
        import numpy as np
        H = 128
        E = 8
        B, S = (4, 256)
        key = jax.random.key(seed)
        k1, k2, k3, k4 = jax.random.split(key, 4)
        x = jax.random.normal(k1, (B, S, H), dtype=jnp.float32)
        wg = jax.random.normal(k2, (H, E), dtype=jnp.float32) * 0.02
        W = jax.random.normal(k3, (E, H, H), dtype=jnp.float32) * 0.02
        b = jax.random.normal(k4, (E, H), dtype=jnp.float32) * 0.02
        return {'x': x, 'wg': wg, 'W': W, 'b': b}
    _L0_ffn_in = _L0_ffn_setup()

    def _L1_attn_setup():
        import jax, jax.numpy as jnp
        import numpy as np
        import math
        DIM = 128
        NUM_HEADS = 16
        HEAD_DIM = DIM // NUM_HEADS
        B, S = (2, 256)
        key = jax.random.key(seed)
        ks = jax.random.split(key, 9)
        sc = 0.02
        return {'x': jax.random.normal(ks[0], (B, S, DIM), jnp.float32), 'Wq': jax.random.normal(ks[1], (DIM, DIM), jnp.float32) * sc, 'bq': jax.random.normal(ks[2], (DIM,), jnp.float32) * sc, 'Wk': jax.random.normal(ks[3], (DIM, DIM), jnp.float32) * sc, 'bk': jax.random.normal(ks[4], (DIM,), jnp.float32) * sc, 'Wv': jax.random.normal(ks[5], (DIM, DIM), jnp.float32) * sc, 'bv': jax.random.normal(ks[6], (DIM,), jnp.float32) * sc, 'Wo': jax.random.normal(ks[7], (DIM, DIM), jnp.float32) * sc, 'bo': jax.random.normal(ks[8], (DIM,), jnp.float32) * sc}
    _L1_attn_in = _L1_attn_setup()

    def _L1_ffn_setup():
        import jax, jax.numpy as jnp
        import numpy as np
        EPS = 1e-05

        def _quantize(W):
            gamma = jnp.mean(jnp.abs(W))
            return jnp.clip(jnp.round(W / (gamma + EPS)), -1.0, 1.0)
        key = jax.random.key(seed)
        k_x, k_w1, k_b1, k_w2, k_b2 = jax.random.split(key, 5)
        n_embd = 128
        d_ff = 4 * n_embd
        B, S = (4, 512)
        bound1 = 1.0 / np.sqrt(n_embd)
        bound2 = 1.0 / np.sqrt(d_ff)
        x = jax.random.normal(k_x, (B, S, n_embd), dtype=jnp.float32)
        W1 = jax.random.uniform(k_w1, (d_ff, n_embd), jnp.float32, -bound1, bound1)
        b1 = jax.random.uniform(k_b1, (d_ff,), jnp.float32, -bound1, bound1)
        W2 = jax.random.uniform(k_w2, (n_embd, d_ff), jnp.float32, -bound2, bound2)
        b2 = jax.random.uniform(k_b2, (n_embd,), jnp.float32, -bound2, bound2)
        return {'x': x, 'W1': W1, 'b1': b1, 'W2': W2, 'b2': b2}
    _L1_ffn_in = _L1_ffn_setup()
    _d = {'L0_attn_x': _L0_attn_in['x'], 'L0_attn_c_attn_w': _L0_attn_in['c_attn_w'], 'L0_attn_c_attn_b': _L0_attn_in['c_attn_b'], 'L0_attn_q2l_w': _L0_attn_in['q2l_w'], 'L0_attn_q2l_b': _L0_attn_in['q2l_b'], 'L0_attn_kv2l_w': _L0_attn_in['kv2l_w'], 'L0_attn_kv2l_b': _L0_attn_in['kv2l_b'], 'L0_attn_l2o_w': _L0_attn_in['l2o_w'], 'L0_attn_l2o_b': _L0_attn_in['l2o_b'], 'L0_attn_wqk_w': _L0_attn_in['wqk_w'], 'L0_attn_wqk_b': _L0_attn_in['wqk_b'], 'L0_attn_cproj_w': _L0_attn_in['cproj_w'], 'L0_attn_cproj_b': _L0_attn_in['cproj_b'], 'L0_ffn_wg': _L0_ffn_in['wg'], 'L0_ffn_W': _L0_ffn_in['W'], 'L0_ffn_b': _L0_ffn_in['b'], 'L1_attn_Wq': _L1_attn_in['Wq'], 'L1_attn_bq': _L1_attn_in['bq'], 'L1_attn_Wk': _L1_attn_in['Wk'], 'L1_attn_bk': _L1_attn_in['bk'], 'L1_attn_Wv': _L1_attn_in['Wv'], 'L1_attn_bv': _L1_attn_in['bv'], 'L1_attn_Wo': _L1_attn_in['Wo'], 'L1_attn_bo': _L1_attn_in['bo'], 'L1_ffn_W1': _L1_ffn_in['W1'], 'L1_ffn_b1': _L1_ffn_in['b1'], 'L1_ffn_W2': _L1_ffn_in['W2'], 'L1_ffn_b2': _L1_ffn_in['b2']}
    _x0 = _d['L0_attn_x']
    _d['L0_attn_x'] = jax.random.normal(jax.random.fold_in(jax.random.key(seed), 1), (8, 256, 128), dtype=_x0.dtype)
    del _x0
    return _d

def reference(L0_attn_x, L0_attn_c_attn_w, L0_attn_c_attn_b, L0_attn_q2l_w, L0_attn_q2l_b, L0_attn_kv2l_w, L0_attn_kv2l_b, L0_attn_l2o_w, L0_attn_l2o_b, L0_attn_wqk_w, L0_attn_wqk_b, L0_attn_cproj_w, L0_attn_cproj_b, L0_ffn_wg, L0_ffn_W, L0_ffn_b, L1_attn_Wq, L1_attn_bq, L1_attn_Wk, L1_attn_bk, L1_attn_Wv, L1_attn_bv, L1_attn_Wo, L1_attn_bo, L1_ffn_W1, L1_ffn_b1, L1_ffn_W2, L1_ffn_b2):

    def _L0_attn_ref(x, c_attn_w, c_attn_b, q2l_w, q2l_b, kv2l_w, kv2l_b, l2o_w, l2o_b, wqk_w, wqk_b, cproj_w, cproj_b):
        import jax, jax.numpy as jnp
        import numpy as np
        N_HEAD = 16
        LATENT = 32

        def _rotate_half(x):
            xe = x[..., ::2]
            xo = x[..., 1::2]
            return jnp.stack((-xo, xe), axis=-1).reshape(x.shape)

        def _rope_tables(T, latent_dim, dtype):
            inv_freq = 1.0 / 10000.0 ** (jnp.arange(0, latent_dim, 2, dtype=jnp.float32) / latent_dim)
            t = jnp.arange(T, dtype=jnp.float32)
            freqs = jnp.outer(t, inv_freq)
            cos = jnp.repeat(jnp.cos(freqs), 2, axis=-1)[:, :latent_dim]
            sin = jnp.repeat(jnp.sin(freqs), 2, axis=-1)[:, :latent_dim]
            return (cos.astype(dtype), sin.astype(dtype))
        B, T, C = x.shape
        H = N_HEAD
        hd = C // H
        L = q2l_w.shape[0]
        qkv = x @ c_attn_w.T + c_attn_b
        q, k, v = jnp.split(qkv, 3, axis=2)

        def heads(t):
            return t.reshape(B, T, H, hd).transpose(0, 2, 1, 3)
        q, k, v = (heads(q), heads(k), heads(v))
        q_lat = q @ q2l_w.T + q2l_b
        k_lat = k @ kv2l_w.T + kv2l_b
        v_lat = v @ kv2l_w.T + kv2l_b
        cos, sin = _rope_tables(T, L, x.dtype)
        cos = cos[None, None]
        sin = sin[None, None]
        q_lat = q_lat * cos + _rotate_half(q_lat) * sin
        k_lat = k_lat * cos + _rotate_half(k_lat) * sin
        q_for_k = q_lat @ wqk_w.T + wqk_b
        att = jnp.einsum('bhql,bhkl->bhqk', q_for_k, k_lat) * L ** (-0.5)
        causal = jnp.tril(jnp.ones((T, T), dtype=bool))
        att = jnp.where(causal[None, None], att, -jnp.inf)
        att = jax.nn.softmax(att, axis=-1)
        y_lat = jnp.einsum('bhqk,bhkl->bhql', att, v_lat)
        y = y_lat @ l2o_w.T + l2o_b
        y = y.transpose(0, 2, 1, 3).reshape(B, T, C)
        return y @ cproj_w.T + cproj_b

    def _L0_ffn_ref(x, wg, W, b):
        import jax, jax.numpy as jnp
        import numpy as np
        H = 128
        E = 8
        B, S = (4, 256)
        Bb, Ss, Hh = x.shape
        Ee = wg.shape[1]
        T = Bb * Ss
        C = T // Ee
        xt = x.reshape(T, Hh)
        logits = xt @ wg
        probs = jax.nn.softmax(logits, axis=-1)
        idx = jnp.argmax(probs, axis=-1)
        mask = jax.nn.one_hot(idx, Ee, dtype=xt.dtype)
        locations = jnp.cumsum(mask, axis=0) - mask
        mask = mask * (locations < C).astype(xt.dtype)
        gate = jnp.sum(probs * mask, axis=-1)
        loc_s = jnp.sum(locations * mask, axis=-1).astype(jnp.int32)
        loc_oh = jax.nn.one_hot(loc_s, C, dtype=xt.dtype)
        dispatch = mask[:, :, None] * loc_oh[:, None, :]
        combine = gate[:, None, None] * dispatch
        exp_in = jnp.einsum('tec,th->ech', dispatch, xt)
        exp_out = jnp.einsum('ech,efh->ecf', exp_in, W) + b[:, None, :]
        out = jnp.einsum('tec,ecf->tf', combine, exp_out)
        return out.reshape(Bb, Ss, Hh)

    def _L1_attn_ref(x, Wq, bq, Wk, bk, Wv, bv, Wo, bo):
        import jax, jax.numpy as jnp
        import numpy as np
        import math
        DIM = 128
        NUM_HEADS = 16
        HEAD_DIM = DIM // NUM_HEADS
        B, S = (2, 256)
        b, s, d = x.shape
        h, hd = (NUM_HEADS, HEAD_DIM)

        def split_heads(t):
            return t.reshape(b, s, h, hd).transpose(0, 2, 1, 3)
        q = split_heads(x @ Wq + bq)
        k = split_heads(x @ Wk + bk)
        v = split_heads(x @ Wv + bv)
        scores = jnp.einsum('bhqd,bhkd->bhqk', q, k) / math.sqrt(hd)
        causal = jnp.tril(jnp.ones((s, s), dtype=bool))
        scores = jnp.where(causal[None, None], scores, jnp.asarray(-10000.0, scores.dtype))
        probs = jax.nn.softmax(scores, axis=-1)
        ctx = jnp.einsum('bhqk,bhkd->bhqd', probs, v)
        ctx = ctx.transpose(0, 2, 1, 3).reshape(b, s, d)
        return ctx @ Wo + bo

    def _L1_ffn_ref(x, W1, b1, W2, b2):
        import jax, jax.numpy as jnp
        import numpy as np
        EPS = 1e-05

        def _quantize(W):
            gamma = jnp.mean(jnp.abs(W))
            return jnp.clip(jnp.round(W / (gamma + EPS)), -1.0, 1.0)
        Wq1 = _quantize(W1)
        Wq2 = _quantize(W2)
        h = jax.nn.relu(jnp.einsum('bsd,fd->bsf', x, Wq1) + b1)
        out = jnp.einsum('bsf,df->bsd', h, Wq2) + b2
        return out
    x = L0_attn_x
    x = _layernorm(x + _L0_attn_ref(x, L0_attn_c_attn_w, L0_attn_c_attn_b, L0_attn_q2l_w, L0_attn_q2l_b, L0_attn_kv2l_w, L0_attn_kv2l_b, L0_attn_l2o_w, L0_attn_l2o_b, L0_attn_wqk_w, L0_attn_wqk_b, L0_attn_cproj_w, L0_attn_cproj_b), axis=-1)
    x = _layernorm(x + _L0_ffn_ref(x, L0_ffn_wg, L0_ffn_W, L0_ffn_b), axis=-1)
    x = _layernorm(x + _L1_attn_ref(x, L1_attn_Wq, L1_attn_bq, L1_attn_Wk, L1_attn_bk, L1_attn_Wv, L1_attn_bv, L1_attn_Wo, L1_attn_bo), axis=-1)
    x = _layernorm(x + _L1_ffn_ref(x, L1_ffn_W1, L1_ffn_b1, L1_ffn_W2, L1_ffn_b2), axis=-1)
    return x

_drawn_inputs = setup_inputs


def setup_inputs(seed=0):
    import zlib

    import numpy as np

    out = dict(_drawn_inputs(seed))
    spreads = {'L0_attn_c_attn_b': (0.0, 0.8),
     'L0_attn_q2l_b': (0.0, 0.8),
     'L0_attn_kv2l_b': (0.0, 0.8),
     'L0_attn_l2o_b': (0.0, 0.279),
     'L0_attn_wqk_b': (0.0, 0.8),
     'L0_attn_cproj_b': (0.0, 0.1)}
    factors = {'L0_attn_c_attn_w': 8.0,
     'L0_attn_q2l_w': 8.0,
     'L0_attn_kv2l_w': 8.0,
     'L0_attn_l2o_w': 8.0,
     'L0_attn_wqk_w': 8.0,
     'L0_ffn_b': 8.0,
     'L1_attn_Wq': 8.0,
     'L1_attn_bq': 8.0,
     'L1_attn_Wk': 8.0,
     'L1_attn_bk': 200.0,
     'L1_attn_Wv': 6.712,
     'L1_attn_bv': 8.0,
     'L1_attn_Wo': 5.687,
     'L1_ffn_b1': 8.0,
     'L1_ffn_b2': 200.0,
     'L1_attn_bo': 3.734}
    for name, (base, spread) in spreads.items():
        noise = np.random.default_rng([zlib.crc32(name.encode()), seed]).standard_normal(out[name].shape)
        drawn = base * np.exp(spread * noise) if base else spread * noise
        out[name] = jnp.asarray(drawn.astype(out[name].dtype))
    for name, factor in factors.items():
        out[name] = (out[name] * factor).astype(out[name].dtype)
    return out
```

```python
from contextlib import ExitStack

import concourse.bass as bass
from concourse import mybir

F32 = mybir.dt.float32
BF16 = mybir.dt.bfloat16
ALU = mybir.AluOpType
ACT = mybir.ActivationFunctionType
AX = mybir.AxisListType

C = 128
T = 256
TILE = 128
NT = T // TILE
NB = 8
NH = 16
HD = C // NH
L = 32
NG = 4
NE = 8
CAP = NB * T // NE
NF = 4
EPS = 1e-5
MASKED = -1.0e30
MAXROW = 96
MAXROWS = 16
STACKED = MAXROW + MAXROWS
OW = 32
NP = 6

SLOTS = 12
ITEMS = 2 * NB

S1 = (0, 1)
S2 = (2, 3)
PB = (4, 5)
OB = 6
FB = 7

CI = 0
CCOS = CI + 128
CSIN = CCOS + T
CHM = CSIN + T
CJM = CHM + NH
CR = CJM + 4
CE = CR + 2 * L
CE8 = CE + 2 * C
CSEL = CE8 + C
CU = CSEL + NH
CW = CU + 128
CONE = CW + NE
NC = CONE + 128


def constants():
    import numpy as np
    c = np.zeros((128, NC), np.float32)
    c[:, CI:CI + 128] = np.eye(128)
    inv = (np.float32(1.0) / np.power(np.float32(10000.0), np.arange(0, L, 2, dtype=np.float32) / np.float32(L)))
    fr = np.outer(np.arange(T, dtype=np.float32), inv.astype(np.float32)).astype(np.float32)
    p = np.arange(128)
    half, lat, jl = p // 64, (p % 64) // 2, p % 2
    c[:, CCOS:CCOS + T] = np.cos(fr)[:, lat // 2].T
    c[:, CSIN:CSIN + T] = np.sin(fr)[:, lat // 2].T
    c[p, CHM + p // HD] = 1.0
    c[p, CJM + 2 * half + jl] = float(L) ** -0.5
    c[np.arange(L), CR + np.arange(L)] = 1.0
    rot = np.zeros((L, L), np.float32)
    rot[np.arange(0, L, 2), np.arange(1, L, 2)] = -1.0
    rot[np.arange(1, L, 2), np.arange(0, L, 2)] = 1.0
    c[0:L, CR + L:CR + 2 * L] = rot.T
    c[lat, CE + p] = 1.0
    c[0:L, CE + C:CE + 2 * C] = rot.T[:, lat]
    c[p % HD, CE8 + p] = 1.0
    r = np.arange(MAXROWS)
    for s in range(NH):
        c[MAXROW + r[r % 8 == s % 8], CSEL + s] = 1.0
    c[:, CU:CU + 128] = np.triu(np.ones((128, 128)), 1)
    c[:, CW:CW + NE] = np.arange(NE, 0, -1)
    c[:, CONE:CONE + 128] = 1.0
    return c


class Item:

    def __init__(self, b, i=0):
        self.b, self.i = b, i
        self.n, self.half, self.par = b + 2 * i, b // 2 + i, b % 2
        self.layer = int(b >= NB)
        self.m = self.n - NB if self.layer else self.n
        self.real = 0 <= b < ITEMS

    def before(self, d):
        it = Item(self.b - d, self.i)
        assert isinstance(self.i, int) or (it.real and it.layer == self.layer)
        return it


class Step:

    def __init__(self, base, i=0):
        self.base, self.i = base, i

    def item(self, d):
        return Item(self.base + d, self.i)


FIRST, LAST = -2, ITEMS + 1
LOOPS = {2: 2, 10: 2}


def walk(eng, slots):
    s = FIRST
    while s <= LAST:
        if s in LOOPS:
            with eng.Fori(0, LOOPS[s]) as i:
                for off in range(2):
                    slots(Step(s + off, i))
            s += 2 * LOOPS[s]
        else:
            slots(Step(s))
            s += 1


PJOBS = (11, 3)


def p_job(it, k):
    b = k % 2
    per = [(j + 1 - b) // 2 for j in PJOBS]
    return per[it.layer] * it.m + (per[0] * NB if it.layer else 0) + k // 2


FJOBS = (13, 8)
SETUP_F = 14


def f_job(it, k):
    return FJOBS[it.layer] * it.m + (FJOBS[0] * NB if it.layer else 0) + SETUP_F + k


def m_job(it, k):
    return 8 * it.n + k // 2 + (k // 2 >= 3) if k % 2 == 0 else 7 * it.n + 1 + k // 2


def e_job(it, k):
    return 6 * it.n + k // 2


def mt_job(it, half):
    return 8 * it.n + 3 + 4 * half


def v_job(it):
    return 7 * it.n


def e_piece(k):
    return (-1, k + 3) if k < 9 else (0, k - 9)


def pv_piece(k):
    return (-1, k + 1) if k < 11 else (0, k - 11)


TERMS = (((0, 0), (0, 1), (1, 0)),
         ((0, 0), (0, 1), (1, 0), (0, 2), (2, 0), (1, 1)))


def stacked_count(it):
    per = [2 * 16 * len(t) for t in TERMS]
    return per[0] * NB // 2 + per[1] * (it.half - NB // 2 + 1) if it.layer else per[0] * (it.half + 1)


P_SLOTS = ({1: [0], 2: [1, 2], 3: [3, 4], 4: [5, 6], 5: [7, 8], 8: [9], 9: [10]},
           {1: [0], 2: [1, 2]})
F_JOBS = ({22: 0, 23: 1, 1: 2, 3: 3, 7: 4, 9: 5, 12: 6, 14: 7, 16: 8, 17: 9, 18: 10, 19: 11, 20: 12},
          {22: 0, 23: 1, 1: 2, 3: 3, 7: 4, 9: 5, 11: 6, 14: 7})
POWER = ((1, 10), (1, 7))
NORMAL = ((5, 22), (5, 16))
FD = (30, 9)
SETUP_SLOTS = {0: [0, 1], 1: [2, 3], 2: [4, 5], 3: [6], 4: [7], 5: [8], 6: [9], 7: [10], 8: [11], 9: [12], 10: [13]}
W_DVE = 30
POOL_SETUP = 11


def f_item(st, h):
    return st.item(-1) if h >= 2 * (SLOTS - 1) else st.item(-2)


def f_job_at(st, h):
    it = f_item(st, h)
    return it, F_JOBS[it.layer].get(h) if it.real else None


def until(eng, sem, count):
    if isinstance(count, int) and count <= 0:
        return
    eng.wait_ge(sem, count)


def build(nc, x, cst_d, W, out):
    x2d = nc.dram_tensor("x2_scratch", (NB * T, C), F32, kind="Internal").ap()
    xr_d = x.rearrange("b (n p) c -> b p n c", p=TILE)
    x2_d = x2d.rearrange("(b n p) c -> b p n c", b=NB, p=TILE)
    out_d = out.rearrange("b (n p) c -> b p n c", p=TILE)

    with ExitStack() as ctx:
        def sb(name, shape, dt=F32):
            return ctx.enter_context(nc.sbuf_tensor(name, shape, dt))

        def sem(name):
            return ctx.enter_context(nc.semaphore(name))

        ps = ctx.enter_context(nc.psum_tensor("ps", [128, 8, 512], F32))

        cst = sb("cst", [128, NC])
        cattn = sb("cattn", [128, 3, C])
        cproj = sb("cproj", [128, C])
        q2l = sb("q2l", [L, 2, HD])
        wqk = sb("wqk", [L, L])
        l2o = sb("l2o", [HD, L])
        lbias = sb("lbias", [L, 3])
        l2ob = sb("l2ob", [HD, 1])
        cattnb = sb("cattnb", [128, 3])
        rowb = sb("rowb", [1, 3, C])
        wgate = sb("wgate", [128, NE])
        wexp = sb("wexp", [128, NE, C])
        bexp = sb("bexp", [NE, C])
        w1l = sb("w1l", [128, 4, C])
        b1l = sb("b1l", [128, 3])
        w1n = sb("w1n", [128, NF * C])
        w2n = sb("w2n", [128, NF * C])
        b1h = sb("b1h", [128, NF])
        identb = sb("identb", [128, 128], BF16)
        maskb = sb("maskb", [128, 4, 128], BF16)
        triub = sb("triub", [128, 128], BF16)
        onesb = sb("onesb", [128, 128], BF16)
        neghalf = sb("neghalf", [128, 2])
        q2lrep = sb("q2lrep", [L, 2, NH, HD])
        wqkrep = sb("wqkrep", [L, 2, L, 2])
        l2orep = sb("l2orep", [L, NH, HD])
        WL = sb("WL", [128, 4, NG * C])
        BDW = sb("BDW", [128, C])
        BDM = sb("BDM", [128, C])
        perm = sb("perm", [128, C])
        cprojT = sb("cprojT", [128, C])
        wv = sb("wv", [128, 2, C])
        wo = sb("wo", [128, 2, C])
        obias = sb("obias", [128, 2, C])
        lb = sb("lb", [128, 16])
        wqkbc = sb("wqkbc", [128, 1])
        ybc = sb("ybc", [128, 1])
        rep = sb("rep", [128, 3, C])
        wexpT = sb("wexpT", [128, NE, C])
        wq1 = sb("wq1", [128, 2, C])
        bq1 = sb("bq1", [128, 2])
        w1T = sb("w1T", [128, NF, C])
        w2T = sb("w2T", [128, NF, C])
        b2row = sb("b2row", [128, C])
        gam = sb("gam", [128, 8])
        xin = sb("xin", [128, 2, NT, C])
        xT = sb("xT", [128, 2, T])
        t1 = sb("t1", [128, 2, 2 * T])
        tb = sb("tb", [128, 2, 2 * T])
        t2 = sb("t2", [128, 2, 2 * T])
        rq = sb("rq", [128, NG * T])
        rk = sb("rk", [128, NG * T])
        parts = sb("parts", [128, 2, 4, NG * T], BF16)
        rest = sb("rest", [128, 2, T])
        parts1 = sb("parts1", [128, 2, 2, 3, T], BF16)
        QS = [[sb(f"QS{l}{p}", [128, NH, T], BF16) for p in range(2)] for l in range(2)]
        KS = [[sb(f"KS{l}{p}", [128, NH, T], BF16) for p in range(2)] for l in range(2)]
        nm = sb("nm", [128, 2, NT, NH])
        nmb = sb("nmb", [128, 2, NT, 2, 2, 8], BF16)
        mT = sb("mT", [MAXROWS, 2, 2, T], BF16)
        vaug = sb("vaug", [128, 2, NT, NH, OW])
        prob = sb("prob", [128, NP, 512])
        BD = prob[:, 0:4, :].rearrange("p k (g c) -> p k g c", g=NG)
        qtmp = prob[:, 0:2, :]
        oT = sb("oT", [128, NG, T])
        rden = sb("rden", [128, NH])
        on = sb("on", [128, NT, C])
        onT = sb("onT", [128, T])
        xf = sb("xf", [128, 2, NT, C])
        xr = sb("xr", [128, NT, C])
        y = sb("y", [128, NT, C])
        stats = sb("stats", [128, NT, 6])
        mv = sb("mv", [128, NT, 2])
        ve = sb("ve", [128, NT])
        rstd = sb("rstd", [128, NT])
        x1 = sb("x1", [128, NT, C])
        x1T = sb("x1T", [128, T])
        lmax = sb("lmax", [128, NT])
        lsh = sb("lsh", [128, NT, NE])
        lex = sb("lex", [128, NT, NE])
        lsum = sb("lsum", [128, NT])
        lrec = sb("lrec", [128, NT])
        pr = sb("pr", [128, NT, NE])
        pmax = sb("pmax", [128, NT])
        peq = sb("peq", [128, NT, NE])
        pk = sb("pk", [128, NT, NE])
        pkm = sb("pkm", [128, NT])
        oh = sb("oh", [128, NT, NE], BF16)
        seen = sb("seen", [128, NE], BF16)
        ohs = sb("ohs", [128, NE], BF16)
        kept = sb("kept", [128, NT, NE])
        gate = sb("gate", [128, NT, NE])
        gT = sb("gT", [NE, T])
        acc = sb("acc", [128, NT, C])
        hT = sb("hT", [128, NF, T])
        xo = sb("xo", [128, 2, NT, C])

        w_in = sem("w_in")
        w2_in = sem("w2_in")
        w_pool = sem("w_pool")
        w_pe = sem("w_pe")
        w_dve = sem("w_dve")
        w_act = sem("w_act")
        x_in = [sem(f"x_in{p}") for p in range(2)]
        xf_in = [sem(f"xf_in{p}") for p in range(2)]
        xo_stored = [sem(f"xo_stored{p}") for p in range(2)]
        p_full = [sem(f"p_full{b}") for b in range(2)]
        p_out = [sem(f"p_out{b}") for b in range(2)]
        rope_mul = sem("rope_mul")
        rope_sum = sem("rope_sum")
        q_high = sem("q_high")
        k_high = sem("k_high")
        k_low = sem("k_low")
        split_a = sem("split_a")
        split_m = sem("split_m")
        split_l = sem("split_l")
        stacked = [[sem(f"stacked{h}{p}") for p in range(2)] for h in range(2)]
        s1_full = [sem(f"s1_full{b}") for b in range(2)]
        s1_out = [sem(f"s1_out{b}") for b in range(2)]
        nm_part = sem("nm_part")
        max_in = [[sem(f"max_in{h}{p}") for p in range(2)] for h in range(2)]
        s2_full = [sem(f"s2_full{b}") for b in range(2)]
        exp_done = sem("exp_done")
        clear_begun = sem("clear_begun")
        stats_seen = sem("stats_seen")
        causal = sem("causal")
        pv_done = sem("pv_done")
        o_out = sem("o_out")
        f_full = sem("f_full")
        f_out = sem("f_out")
        f_dve = [sem(f"f_dve{l}") for l in range(2)]
        var_ready = sem("var_ready")
        nm_high = sem("nm_high")
        w2_dve = sem("w2_dve")
        onehot_ready = sem("onehot_ready")
        gate_ready = sem("gate_ready")
        x1_ready = sem("x1_ready")
        xo_ready = sem("xo_ready")
        xr_done = sem("xr_done")
        rstd_done = sem("rstd_done")
        lexp_done = sem("lexp_done")

        block = ctx.enter_context(nc.Block())

        ident = cst[:, CI:CI + 128]
        hm = cst[:, CHM:CHM + NH]
        ones = cst[:, CONE:CONE + 128]

        NW, NW2 = 13, 20

        @block.sync
        def _(sp):
            def load(dst, src, s):
                sp.dma_start(dst, src).then_inc(s, 16)

            load(cst[:, :], cst_d, w_in)
            load(cattn[:, :, :], W["c_attn_w"].rearrange("(a p) c -> p a c", p=128), w_in)
            load(q2l[:, 0, :], W["q2l_w"], w_in)
            load(q2l[:, 1, :], W["kv2l_w"], w_in)
            load(wqk[:, :], W["wqk_w"], w_in)
            load(l2o[:, :], W["l2o_w"], w_in)
            load(lbias[:, 0:1], W["q2l_b"].rearrange("(p a) -> p a", a=1), w_in)
            load(lbias[:, 1:2], W["kv2l_b"].rearrange("(p a) -> p a", a=1), w_in)
            load(lbias[:, 2:3], W["wqk_b"].rearrange("(p a) -> p a", a=1), w_in)
            load(l2ob[:, :], W["l2o_b"].rearrange("(p a) -> p a", a=1), w_in)
            for n in range(3):
                load(cattnb[:, n:n + 1], W["c_attn_b"][n * C:(n + 1) * C].rearrange("(p a) -> p a", a=1), w_in)

            def other_weights():
                load(cproj[:, :], W["cproj_w"], w2_in)
                load(rowb[:, 0, :], W["cproj_b"].rearrange("(a p) -> a p", a=1), w2_in)
                load(rowb[:, 1, :], W["bo"].rearrange("(a p) -> a p", a=1), w2_in)
                load(rowb[:, 2, :], W["b2"].rearrange("(a p) -> a p", a=1), w2_in)
                load(wgate[:, :], W["wg"], w2_in)
                load(wexp[:, :, :], W["W"].rearrange("e f h -> f e h"), w2_in)
                load(bexp[:, :], W["b"], w2_in)
                for n, name in enumerate(("Wq", "Wk", "Wv", "Wo")):
                    load(w1l[:, n, :], W[name], w2_in)
                for n, name in enumerate(("bq", "bk", "bv")):
                    load(b1l[:, n:n + 1], W[name].rearrange("(p a) -> p a", a=1), w2_in)
                load(w1n[:, :].rearrange("p (a c) -> p a c", a=NF), W["W1"].rearrange("(a p) c -> p a c", p=128), w2_in)
                load(w2n[:, :], W["W2"], w2_in)
                for n in range(NF):
                    load(b1h[:, n:n + 1], W["b1"][n * C:(n + 1) * C].rearrange("(p a) -> p a", a=1), w2_in)

            def value(v):
                return v if isinstance(v, int) else sp.snap(v)

            def load_x(it):
                row, mine = value(it.m), value(16 * (it.half - NB // 2) + 32)
                if it.before(2).real:
                    read = value(p_job(it.before(2), 0) + 1)
                    sp.wait_ge(p_full[0], read)
                if it.layer:
                    sp.wait_ge(xo_stored[it.par], mine)
                src = x2_d if it.layer else xr_d
                sp.dma_start(xin[:, it.par, :, :], src[row]).then_inc(x_in[it.par], 16)

            def load_xf(it):
                row = value(it.m)
                until(sp, xr_done, it.n)
                src = x2_d if it.layer else xr_d
                sp.dma_start(xf[:, it.par, :, :], src[row]).then_inc(xf_in[it.par], 16)

            def stack(it, half):
                rows = slice(64 * half, 64 * half + 64)
                heads = slice(8 * half, 8 * half + 8)
                read = value(e_job(it.before(2), 6 * half + 5) + 1)
                q_parts, k_parts, low_parts = value(p_job(it, 10) + 1), value(it.m + 1), value(2 * it.m + 2)
                if it.before(2).real:
                    sp.wait_ge(s2_full[1], read)
                done = stacked[half][it.par]
                if it.layer == 0:
                    sp.wait_ge(p_out[0], q_parts)
                    sp.wait_ge(k_low, k_parts)
                    for r, (qp, kp) in enumerate(TERMS[0]):
                        for dst, part in ((QS[0], qp), (KS[0], 2 + kp)):
                            sp.dma_start(dst[it.par][L * r:L * r + L, heads, :],
                                         parts[rows, it.par, part, :]).then_inc(done, 16)
                else:
                    sp.wait_ge(split_l, low_parts)
                    sp.wait_ge(w_pool, POOL_SETUP)
                    for r, (qp, kp) in enumerate(TERMS[1]):
                        for o, dst, part in ((0, QS[1], qp), (1, KS[1], kp)):
                            sp.dma_start(dst[it.par][HD * r:HD * r + HD, heads, :],
                                         parts1[rows, it.par, o, part, :]).then_inc(done, 16)

            def max_rows(it, half):
                sp.wait_ge(s1_out[0], mt_job(it, half) + 1)
                src = mT[:, it.par, half:half + 1, :].broadcast_to([MAXROWS, 8, T])
                sp.dma_start(QS[it.layer][it.par][MAXROW:STACKED, 8 * half:8 * half + 8, :], src)\
                    .then_inc(max_in[half][it.par], 16)

            def store(it):
                row, ready = value(it.m), value(it.n + 1)
                sp.wait_ge(xo_ready, ready)
                if it.layer == 0:
                    sp.dma_start(x2_d[row], xo[:, it.par, :, :]).then_inc(xo_stored[it.par], 16)
                else:
                    sp.dma_start(out_d[row], xo[:, it.par, :, :]).then_inc(xo_stored[it.par], 16)

            def slots(st):
                for k in range(SLOTS):
                    if k == 0:
                        if st.item(-1).real:
                            max_rows(st.item(-1), 1)
                        if st.item(2).real:
                            load_x(st.item(2))
                        if st.item(-1).real:
                            load_xf(st.item(-1))
                    if k == 3 and st.item(1).real:
                        stack(st.item(1), 0)
                    if k == 6 and st.item(0).real:
                        max_rows(st.item(0), 0)
                    if k == 9 and st.item(1).real:
                        stack(st.item(1), 1)
                    if k == 11 and st.item(-2).real:
                        store(st.item(-2))
                if st.base == FIRST:
                    other_weights()

            walk(sp, slots)
            for p in range(2):
                sp.wait_ge(xo_stored[p], 16 * ITEMS // 2 + 16)

        @block.gpsimd
        def _(pool):
            g = nc.gpsimd
            g.memset(neghalf[:, :], -0.5).then_inc(w_pool, 1)
            g.memset(maskb[:, :, :], 0.0).then_inc(w_pool, 1)
            for p in range(2):
                g.memset(vaug[:, p, :, :, :], 0.0).then_inc(w_pool, 1)
            pool.wait_ge(w_pool, 4)
            g.affine_select(out=maskb[:, :, :], in_=maskb[:, :, :], compare_op=ALU.is_ge, fill=MASKED, base=0,
                            pattern=[[0, 4], [-1, 128]], channel_multiplier=1).then_inc(w_pool, 1)
            for p in range(2):
                g.memset(vaug[:, p, :, :, HD:HD + 1], 1.0).then_inc(w_pool, 1)
            pool.wait_ge(w_in, 16 * NW)

            def clear_stacks():
                for p in range(2):
                    g.memset(QS[1][p][0:MAXROW, :, :], 0.0).then_inc(w_pool, 1)
                    g.memset(KS[1][p][0:MAXROW, :, :], 0.0).then_inc(w_pool, 1)

            def rope(it, a):
                ja, jb = 1 + 2 * a, 2 + 2 * a
                pool.wait_ge(p_out[jb % 2], p_job(it, jb) + 1)
                until(pool, rope_sum, 4 * it.m + a - 1)
                sin = cst[:, CSIN:CSIN + T].rearrange("p (a t) -> p a t", a=1).broadcast_to([128, 2, T])
                g.tensor_tensor(t2[:, a % 2, :].rearrange("p (a t) -> p a t", a=2),
                                tb[:, a % 2, :].rearrange("p (a t) -> p a t", a=2), sin, ALU.mult).then_inc(rope_mul, 1)
                pool.wait_ge(p_out[ja % 2], p_job(it, ja) + 1)
                pool.wait_ge(rope_mul, 4 * it.m + a + 1)
                if a < 2 and it.before(1).real:
                    pool.wait_ge(p_full[a % 2 ^ 1], p_job(it.before(1), 9 + a) + 1)
                if a >= 2:
                    until(pool, k_low, it.m)
                dst = (rq if a < 2 else rk)[:, (a % 2) * 2 * T:(a % 2 + 1) * 2 * T]
                g.tensor_tensor(dst, t1[:, a % 2, :], t2[:, a % 2, :], ALU.add).then_inc(rope_sum, 1)

            def clear(it, k):
                pool.wait_ge(exp_done, 12 * it.n + k + 1)
                pool.sem_inc(clear_begun, 1)
                heads = 2 if k % 3 < 2 else 4
                v = prob[:, k % NP, :].rearrange("p (h t) -> p h t", h=heads)[:, :, 0:TILE]
                g.affine_select(out=v, in_=v, compare_op=ALU.is_ge, fill=0.0, base=0,
                                pattern=[[0, heads], [1, TILE]], channel_multiplier=-1).then_inc(causal, 1)

            def power(it, which):
                pool.wait_ge(var_ready, 2 * it.n + which + 1)
                g.tensor_tensor(rstd[:, :], ve[:, :], neghalf[:, :], ALU.pow).then_inc(rstd_done, 1)

            def residual(it):
                pool.wait_ge(f_out, SETUP_F)
                pool.wait_ge(xf_in[it.par], 16 * it.half + 16)
                if it.before(1).real:
                    pool.wait_ge(f_out, f_job(it.before(1), 3) + 1)
                ob = obias[:, it.layer:it.layer + 1, :].broadcast_to([128, NT, C])
                g.tensor_tensor(xr[:, :, :], xf[:, it.par, :, :], ob, ALU.add).then_inc(xr_done, 1)

            def slots(st):
                for k in range(SLOTS):
                    p = st.item(2)
                    d, piece = e_piece(k)
                    if st.item(d).real:
                        clear(st.item(d), piece)
                    if p.real and p.layer == 0 and 3 <= k < 7:
                        rope(p, k - 3)
                    if k == 11 and st.item(-1).real:
                        residual(st.item(-1))
                    if k == 11 and st.base == -1:
                        clear_stacks()
                    f = st.item(-2)
                    if f.real and k in POWER[f.layer]:
                        power(f, POWER[f.layer].index(k))

            walk(pool, slots)

        @block.scalar
        def _(act):
            a_ = nc.scalar

            def setup():
                for kind in range(4):
                    act.wait_ge(w_pe, 2 + kind)
                    a_.activation(WL[:, kind, :], ps[:, kind, :], ACT.Copy).then_inc(w_act, 1)
                act.wait_ge(w_pe, 7)
                a_.activation(wv[:, 0, :], ps[:, 5, 0:C], ACT.Copy).then_inc(w_act, 1)
                act.wait_ge(w_dve, W_DVE)

            def p_evac(it, k):
                b = k % 2
                if k == 0:
                    act.wait_ge(p_full[0], p_job(it, 0) + 1)
                    if it.before(2).real:
                        act.wait_ge(s1_full[1], v_job(it.before(2)) + 1)
                    a_.activation(xT[:, it.par, :], ps[:, PB[0], 0:T], ACT.Copy).then_inc(p_out[0], 1)
                elif it.layer == 0 and k <= 8:
                    a = (k - 2) // 2
                    act.wait_ge(p_full[b], p_job(it, k) + 1)
                    until(act, rope_mul, 4 * it.m + a - 1)
                    for g in range(2):
                        col = (1, 3)[a // 2] * NG + 2 * (a % 2) + g
                        ins = a_.activation(tb[:, a % 2, g * T:(g + 1) * T], ps[:, PB[b], g * T:(g + 1) * T],
                                            ACT.Identity, bias=lb[:, col:col + 1])
                    ins.then_inc(p_out[b], 1)
                elif it.layer == 0:
                    act.wait_ge(p_full[b], p_job(it, k) + 1)
                    parts_free(it)
                    a_.activation(parts[:, it.par, 0, (k - 9) * 512:(k - 8) * 512], ps[:, PB[b], :], ACT.Identity,
                                  bias=wqkbc[:, 0:1]).then_inc(q_high, 1)
                else:
                    o = k - 1
                    act.wait_ge(p_full[b], p_job(it, k) + 1)
                    if it.before(2).layer:
                        parts_free(it)
                    a_.activation(parts1[:, it.par, o, 0, :], ps[:, PB[b], 0:T], ACT.Identity,
                                  bias=bq1[:, o:o + 1]).then_inc(split_a, 1)

            def parts_free(it):
                if it.before(2).real:
                    for h in range(2):
                        act.wait_ge(stacked[h][it.par], stacked_count(it.before(2)))

            def k_parts(it):
                act.wait_ge(rope_sum, 4 * it.m + 4)
                parts_free(it)
                a_.activation(parts[:, it.par, 2, :], rk[:, :], ACT.Copy).then_inc(k_high, 1)

            def split_middle(it):
                for o in range(2):
                    act.wait_ge(p_out[(o + 1) % 2], p_job(it, o + 1) + 1)
                    a_.activation(parts1[:, it.par, o, 1, :], rest[:, o, :], ACT.Copy).then_inc(split_m, 1)

            def values(it):
                act.wait_ge(s1_full[1], v_job(it) + 1)
                if it.before(2).real:
                    act.wait_ge(pv_done, 12 * it.before(2).n + 12)
                else:
                    act.wait_ge(w_pool, 7)
                a_.activation(vaug[:, it.par, :, :, 0:HD],
                              ps[:, S1[1], 0:T].rearrange("p (n h d) -> p n h d", n=NT, h=NH), ACT.Copy)\
                    .then_inc(s1_out[1], 1)

            def exp(it, k):
                act.wait_ge(s2_full[k % 2], e_job(it, k) + 1)
                until(act, pv_done, 12 * it.n + k - NP + 1)
                a_.activation(prob[:, k % NP, :], ps[:, S2[k % 2], :], ACT.Exp).then_inc(exp_done, 1)

            def o_evac(it, h):
                act.wait_ge(pv_done, 12 * it.n + 6 * h + 6)
                if h == 0 and it.before(1).real:
                    act.wait_ge(f_full, f_job(it.before(1), 1) + 1)
                a_.activation(oT[:, 2 * h:2 * h + 2, :].rearrange("p a t -> p (a t)"), ps[:, OB, :], ACT.Copy)\
                    .then_inc(o_out, 1)

            def f_evac(it, k):
                if k in (2, 4):
                    act.wait_ge(f_full, f_job(it, k) + 1)
                    a_.activation((onT if k == 2 else x1T)[:, :], ps[:, FB, 0:T], ACT.Copy).then_inc(f_out, 1)
                elif it.layer == 0 and k == 5:
                    act.wait_ge(f_out, f_job(it, 5) + 1)
                    a_.activation(lex[:, :, :], lsh[:, :, :], ACT.Exp).then_inc(lexp_done, 1)
                elif it.layer == 0 and k == 7:
                    act.wait_ge(f_full, f_job(it, k) + 1)
                    a_.activation(gT[:, :], ps[0:NE, FB, 0:T], ACT.Copy).then_inc(f_out, 1)
                elif it.layer == 1 and k in (5, 6):
                    act.wait_ge(f_full, f_job(it, k) + 1)
                    for c in range(2):
                        ch = 2 * (k - 5) + c
                        ins = a_.activation(hT[:, ch, :], ps[:, FB, c * T:(c + 1) * T], ACT.Relu, bias=b1h[:, ch:ch + 1])
                    ins.then_inc(f_out, 1)

            def half_slot(st, h):
                it, j = f_job_at(st, h)
                if j is not None:
                    f_evac(it, j)

            def slots(st):
                if st.base == FIRST:
                    setup()
                for k in range(SLOTS):
                    half_slot(st, 2 * k)
                    d, piece = e_piece(k)
                    if st.item(d).real:
                        exp(st.item(d), piece)
                    d, piece = pv_piece(k)
                    if st.item(d).real and piece in (5, 11):
                        o_evac(st.item(d), piece // 6)
                    p = st.item(2)
                    if p.real:
                        for j in P_SLOTS[p.layer].get(k, []):
                            if j == 0 or (j % 2 == 0 if p.layer == 0 and j < 9 else True):
                                p_evac(p, j)
                        if p.layer == 0 and k == 7:
                            k_parts(p)
                        if p.layer == 1 and k == 3:
                            split_middle(p)
                    if k == 11 and st.item(1).real:
                        values(st.item(1))
                    half_slot(st, 2 * k + 1)

            walk(act, slots)

        @block.tensor
        def _(pe):
            mm, tr = nc.tensor.matmul, nc.tensor.transpose

            def setup():
                pe.wait_ge(w_in, 16 * NW)
                pe.wait_ge(w_dve, 2)
                for kind in range(2):
                    mm(ps[:, FB, 64 * kind:64 * kind + 64], q2lrep[:, kind, :, :].rearrange("p h d -> p (h d)"),
                       cst[0:L, CR:CR + 2 * L], start=True, stop=True)
                mm(ps[:, FB, 128:128 + L], wqkrep[:, :, :, :].rearrange("p a l b -> p (a l b)"),
                   cst[0:L, CR:CR + L], start=True, stop=True)
                mm(ps[:, FB, 160:161], cst[0:L, CE:CE + C], lbias[:, 2:3], start=True, stop=True).then_inc(w_pe, 1)
                for kind in range(4):
                    pe.wait_ge(w_dve, 2 + 4 * (kind + 1))
                    mm(ps[:, kind, :], cattn[:, kind // 2, :], BD[:, kind, :, :].rearrange("p g c -> p (g c)"),
                       start=True, stop=True).then_inc(w_pe, 1)
                for kind in range(4):
                    for g in range(NG):
                        col = ps[:, 4, kind * NG + g:kind * NG + g + 1]
                        mm(col, BD[:, kind, g, :], cattnb[:, kind // 2:kind // 2 + 1], start=True, stop=False)
                        last = mm(col, cst[0:L, CE + C * (kind % 2):CE + C * (kind % 2) + C],
                                  lbias[:, kind // 2:kind // 2 + 1], start=False, stop=True)
                last.then_inc(w_pe, 1)
                tr(ps[:, 5, 0:C], cattn[:, 2, :], ident).then_inc(w_pe, 1)
                pe.wait_ge(w_act, 5)
                pe.wait_ge(w_dve, W_DVE)
                pe.wait_ge(w_pool, 5)

            def setup_f(j):
                if j == 0:
                    pe.wait_ge(w2_in, 16 * NW2)
                    pe.wait_ge(w2_dve, 4)
                else:
                    pe.wait_ge(f_out, j)
                bank = ps[:, FB, :]
                if j == 0:
                    last = tr(bank[:, 0:C], cproj[:, :], ident)
                elif j == 1:
                    last = tr(ps[0:L, FB, 0:HD], l2o[:, :], cst[0:HD, CI:CI + HD])
                elif j == 2:
                    last = mm(bank[:, 0:HD], l2orep[:, :, :].rearrange("p h e -> p (h e)"), q2l[:, 1, :],
                              start=True, stop=True)
                elif j == 3:
                    mm(bank[:, 0:1], l2orep[:, :, :].rearrange("p h e -> p (h e)"), lbias[:, 1:2], start=True, stop=False)
                    last = mm(bank[:, 0:1], cst[0:HD, CE8:CE8 + C], l2ob[:, :], start=False, stop=True)
                elif j == 4:
                    last = mm(bank[:, 0:C], BDM[:, :], cprojT[:, :], start=True, stop=True)
                elif j == 5:
                    mm(bank[:, 0:C], rep[:, 0, :], wo[:, 0, :], start=True, stop=False)
                    mm(bank[:, 0:C], rep[:, 1, :], cprojT[:, :], start=False, stop=False)
                    last = mm(bank[:, 0:C], cst[0:1, CONE:CONE + 128], rowb[:, 0, :], start=False, stop=True)
                elif j in (6, 7):
                    for e in range(4):
                        last = tr(bank[:, e * C:(e + 1) * C], wexp[:, 4 * (j - 6) + e, :], ident)
                elif j == 8:
                    last = mm(bank[:, 0:2], ones, gam[:, 0:2], start=True, stop=True)
                elif j in (9, 10):
                    pe.wait_ge(w2_dve, 11)
                    for a in range(NF):
                        last = tr(bank[:, a * C:(a + 1) * C], (w1n, w2n)[j - 9][:, a * C:(a + 1) * C], ident)
                elif j == 11:
                    for o in range(2):
                        last = mm(bank[:, o:o + 1], perm[:, :], b1l[:, o:o + 1], start=True, stop=True)
                elif j == 12:
                    mm(bank[:, 0:C], rep[:, 2, :], w1l[:, 3, :], start=True, stop=False)
                    last = mm(bank[:, 0:C], cst[0:1, CONE:CONE + 128], rowb[:, 1, :], start=False, stop=True)
                else:
                    last = mm(bank[:, 0:C], cst[0:1, CONE:CONE + 128], rowb[:, 2, :], start=True, stop=True)
                last.then_inc(f_full, 1)

            def projection(it, k):
                b = k % 2
                until(pe, p_out[b], p_job(it, k))
                bank = ps[:, PB[b], :]
                if k == 0:
                    pe.wait_ge(x_in[it.par], 16 * it.half + 16)
                    for n in range(NT):
                        last = tr(bank[:, n * TILE:(n + 1) * TILE], xin[:, it.par, n, :], ident)
                elif it.layer == 0 and k < 9:
                    pe.wait_ge(p_out[0], p_job(it, 0) + 1)
                    a = (k - 1) // 2
                    kind, g0 = 2 * (a // 2) + (k - 1) % 2, 2 * (a % 2)
                    for g in range(2):
                        last = mm(bank[:, g * T:(g + 1) * T], WL[:, kind, (g0 + g) * C:(g0 + g + 1) * C],
                                  xT[:, it.par, :], start=True, stop=True)
                elif it.layer == 0:
                    pe.wait_ge(rope_sum, 4 * it.m + 2)
                    last = mm(bank, BDW[:, :], rq[:, (k - 9) * 512:(k - 8) * 512], start=True, stop=True)
                else:
                    pe.wait_ge(p_out[0], p_job(it, 0) + 1)
                    last = mm(bank[:, 0:T], wq1[:, k - 1, :], xT[:, it.par, :], start=True, stop=True)
                last.then_inc(p_full[b], 1)

            def values(it):
                until(pe, s1_out[1], v_job(it))
                pe.wait_ge(p_out[0], p_job(it, 0) + 1)
                w = w1l[:, 2, :] if it.layer else wv[:, 0, :]
                for n in range(NT):
                    last = mm(ps[:, S1[1], n * C:(n + 1) * C], xT[:, it.par, n * TILE:(n + 1) * TILE], w,
                              start=True, stop=True)
                last.then_inc(s1_full[1], 1)

            def scores_for_max(it, k):
                b, u, r = k % 2, k // 3, k % 3
                q, kk = QS[it.layer][it.par], KS[it.layer][it.par]
                if k in (0, 6):
                    pe.wait_ge(stacked[k // 6][it.par], stacked_count(it))
                until(pe, s1_out[b], m_job(it, k))
                bank = ps[:, S1[b], :]
                if r == 0:
                    for j in range(4):
                        mm(bank[:, j * TILE:(j + 1) * TILE], q[0:MAXROW, 4 * u + j, 0:TILE],
                           kk[0:MAXROW, 4 * u + j, 0:TILE], start=(j == 0), stop=False)
                    last = mm(bank, identb[:, :], maskb[:, :, :].rearrange("p h t -> p (h t)"), start=False, stop=True)
                else:
                    for j in range(2):
                        h = 4 * u + 2 * (r - 1) + j
                        mm(bank[:, j * T:(j + 1) * T], q[0:MAXROW, h, TILE:T], kk[0:MAXROW, h, :],
                           start=(j == 0), stop=False)
                    last = mm(bank.rearrange("p (h t) -> p h t", h=2)[:, :, TILE:T], identb[:, :], maskb[:, 0:2, :],
                              start=False, stop=True)
                last.then_inc(s1_full[b], 1)

            def transpose_max(it, half):
                pe.wait_ge(nm_part, 2 * it.n + half + 1)
                until(pe, s1_out[0], mt_job(it, half))
                bank = ps[0:MAXROWS, S1[0], :].bitcast(BF16)
                for n in range(NT):
                    last = tr(bank[:, n * TILE:(n + 1) * TILE],
                              nmb[:, it.par, n, half, :, :].rearrange("p a h -> p (a h)"), identb[:, :])
                last.then_inc(s1_full[0], 1)

            def scores_for_exp(it, k):
                b, u, r = k % 2, k // 3, k % 3
                q, kk = QS[it.layer][it.par], KS[it.layer][it.par]
                if k in (0, 6):
                    pe.wait_ge(max_in[k // 6][it.par], 16 * it.half + 16)
                until(pe, exp_done, 12 * it.n + k - 1)
                bank = ps[:, S2[b], :]
                if r < 2:
                    for j in range(2):
                        h = 4 * u + 2 * r + j
                        last = mm(bank[:, j * T:(j + 1) * T], kk[0:STACKED, h, 0:TILE], q[0:STACKED, h, :],
                                  start=True, stop=True)
                else:
                    for j in range(4):
                        h = 4 * u + j
                        last = mm(bank[:, j * TILE:(j + 1) * TILE], kk[0:STACKED, h, TILE:T], q[0:STACKED, h, TILE:T],
                                  start=True, stop=True)
                last.then_inc(s2_full[b], 1)

            def times_values(it, k):
                u, r = k // 3, k % 3
                pe.wait_ge(causal, 12 * it.n + k + 1)
                if k == 0:
                    pe.wait_ge(s1_out[1], v_job(it) + 1)
                if k % 6 == 0:
                    until(pe, o_out, 2 * it.n + k // 6)
                base = (u % 2) * T
                for i in range(2 if r < 2 else 4):
                    j = 2 * r + i if r < 2 else i
                    rows = slice(32 * j, 32 * j + OW)
                    if r < 2:
                        last = mm(ps[rows, OB, base:base + T], vaug[:, it.par, 0, 4 * u + j, :],
                                  prob[:, k % NP, i * T:(i + 1) * T], start=True, stop=False)
                    else:
                        last = mm(ps[rows, OB, base + TILE:base + T], vaug[:, it.par, 1, 4 * u + j, :],
                                  prob[:, k % NP, i * TILE:(i + 1) * TILE], start=False, stop=True)
                last.then_inc(pv_done, 1)

            def f_product(it, k):
                pe.wait_ge(f_out, f_job(it, k))
                bank = ps[:, FB, :]
                if k < 2:
                    pe.wait_ge(o_out, 2 * it.n + 2)
                    for u in range(NG):
                        last = tr(bank[:, u * TILE:(u + 1) * TILE], oT[:, u, k * TILE:(k + 1) * TILE], ident)
                elif k == 2:
                    for n in range(NT):
                        last = tr(bank[:, n * TILE:(n + 1) * TILE], on[:, n, :], ident)
                elif k == 3:
                    w = w1l[:, 3, :] if it.layer else wo[:, 0, :]
                    for n in range(NT):
                        last = mm(bank[:, n * C:(n + 1) * C], onT[:, n * TILE:(n + 1) * TILE], w, start=True, stop=True)
                elif k == 4:
                    pe.wait_ge(x1_ready, it.n + 1)
                    for n in range(NT):
                        last = tr(bank[:, n * TILE:(n + 1) * TILE], x1[:, n, :], ident)
                elif it.layer == 0:
                    last = moe(it, k, bank)
                else:
                    last = mlp(k, bank)
                last.then_inc(f_full, 1)

            def moe(it, k, bank):
                if k == 5:
                    for n in range(NT):
                        last = mm(bank[:, n * NE:(n + 1) * NE], x1T[:, n * TILE:(n + 1) * TILE], wgate[:, :],
                                  start=True, stop=True)
                elif k == 6:
                    pe.wait_ge(onehot_ready, it.m + 1)
                    for n in range(NT):
                        dst = bank[:, n * NE:(n + 1) * NE]
                        mm(dst, triub[:, :], oh[:, n, :], start=True, stop=False)
                        if n:
                            mm(dst, onesb[:, :], oh[:, 0, :], start=False, stop=False)
                        last = mm(dst, onesb[:, :], seen[:, :], start=False, stop=True)
                elif k == 7:
                    pe.wait_ge(gate_ready, it.m + 1)
                    for n in range(NT):
                        last = tr(ps[0:NE, FB, n * TILE:(n + 1) * TILE], gate[:, n, :], ident)
                elif k == 8:
                    for n in range(NT):
                        last = mm(bank[:, n * C:(n + 1) * C], gT[:, n * TILE:(n + 1) * TILE], bexp[:, :],
                                  start=True, stop=True)
                else:
                    n, half = (k - 9) // 2, (k - 9) % 2
                    last = mm(bank, x1T[:, n * TILE:(n + 1) * TILE],
                              wexpT[:, 4 * half:4 * half + 4, :].rearrange("p e c -> p (e c)"), start=True, stop=True)
                return last

            def mlp(k, bank):
                if k in (5, 6):
                    for c in range(2):
                        last = mm(bank[:, c * T:(c + 1) * T], w1T[:, 2 * (k - 5) + c, :], x1T[:, :], start=True, stop=True)
                else:
                    for n in range(NT):
                        for c in range(NF):
                            last = mm(bank[:, n * C:(n + 1) * C], hT[:, c, n * TILE:(n + 1) * TILE], w2T[:, c, :],
                                      start=(c == 0), stop=(c == NF - 1))
                return last

            def half_slot(st, h):
                it, j = f_job_at(st, h)
                if j is not None:
                    f_product(it, j)

            def slots(st):
                if st.base == FIRST:
                    setup()
                for k in range(SLOTS):
                    half_slot(st, 2 * k)
                    m = st.item(0)
                    if m.real:
                        scores_for_max(m, k)
                    d, piece = e_piece(k)
                    if st.item(d).real:
                        scores_for_exp(st.item(d), piece)
                    d, piece = pv_piece(k)
                    if st.item(d).real:
                        times_values(st.item(d), piece)
                    p = st.item(2)
                    if p.real:
                        for j in P_SLOTS[p.layer].get(k, []):
                            projection(p, j)
                    if st.base == -1:
                        for j in SETUP_SLOTS.get(k, []):
                            setup_f(j)
                    if k == 11 and st.item(1).real:
                        values(st.item(1))
                    half_slot(st, 2 * k + 1)
                    if k in (5, 11) and m.real:
                        transpose_max(m, k // 6)

            walk(pe, slots)

        @block.vector
        def _(dve):
            v = nc.vector

            def setup():
                for p in range(2):
                    dve.sem_inc(xo_stored[p], 16)
                dve.wait_ge(w_in, 16 * NW)
                v.tensor_copy(q2lrep[:, :, :, :],
                              q2l[:, :, :].rearrange("p k (a d) -> p k a d", a=1).broadcast_to([L, 2, NH, HD]))\
                    .then_inc(w_dve, 1)
                v.tensor_copy(wqkrep[:, :, :, :],
                              wqk[:, :].rearrange("p (a l b) -> p a l b", a=1, b=1).broadcast_to([L, 2, L, 2]))\
                    .then_inc(w_dve, 1)
                dve.wait_ge(w_pe, 1)
                for kind in range(4):
                    src = ps[:, FB, L * kind:L * kind + L].rearrange("p (a l b) -> p a l b", a=1, b=1)
                    for g in range(NG):
                        own = hm.rearrange("p (a b g) -> p a b g", a=2, g=NG)[:, :, :, g]
                        own = own.rearrange("p a (x b) -> p a x b", x=1)
                        v.tensor_tensor(BD[:, kind, g, :].rearrange("p (a l b) -> p a l b", a=2, b=2),
                                        src.broadcast_to([128, 2, L, 2]), own.broadcast_to([128, 2, L, 2]), ALU.mult)\
                            .then_inc(w_dve, 1)
                src = ps[:, FB, 128:128 + L].rearrange("p (a l b) -> p a l b", a=1, b=1).broadcast_to([128, 2, L, 2])
                own = cst[:, CJM:CJM + 4].rearrange("p (a x b) -> p a x b", a=2, x=1).broadcast_to([128, 2, L, 2])
                v.tensor_tensor(BDW[:, :].rearrange("p (a l b) -> p a l b", a=2, b=2), src, own, ALU.mult)\
                    .then_inc(w_dve, 1)
                v.tensor_scalar(wqkbc[:, :], ps[:, FB, 160:161], float(L) ** -0.5, None, ALU.mult).then_inc(w_dve, 1)
                v.tensor_copy(identb[:, :], ident).then_inc(w_dve, 1)
                v.tensor_copy(triub[:, :], cst[:, CU:CU + 128]).then_inc(w_dve, 1)
                v.tensor_copy(onesb[:, :], ones).then_inc(w_dve, 1)
                v.memset(seen[:, :], 0.0).then_inc(w_dve, 1)
                sel = cst[MAXROW:STACKED, CSEL:CSEL + NH].rearrange("p (h a) -> p h a", a=1).broadcast_to([MAXROWS, NH, T])
                for l in range(2):
                    for p in range(2):
                        v.tensor_copy(KS[l][p][MAXROW:STACKED, :, :], sel).then_inc(w_dve, 1)
                dve.wait_ge(w_pe, 6)
                v.tensor_copy(lb[:, :], ps[:, 4, 0:16]).then_inc(w_dve, 1)
                v.tensor_copy(perm[:, :].rearrange("p (a d b) -> p a d b", a=2, d=HD),
                              ident.rearrange("p (a b d) -> p a d b", a=2, d=HD)).then_inc(w_dve, 1)

            def setup_2():
                dve.wait_ge(w2_in, 16 * NW2)
                v.tensor_copy(rep[:, 0, :], cattnb[:, 2:3].broadcast_to([128, C])).then_inc(w2_dve, 1)
                v.tensor_copy(rep[:, 2, :], b1l[:, 2:3].broadcast_to([128, C])).then_inc(w2_dve, 1)
                v.tensor_reduce(gam[:, 0:1], w1n[:, :], AX.X, ALU.add, apply_absolute_value=True).then_inc(w2_dve, 1)
                v.tensor_reduce(gam[:, 1:2], w2n[:, :], AX.X, ALU.add, apply_absolute_value=True).then_inc(w2_dve, 1)
                for o in range(2):
                    v.tensor_scalar(wq1[:, o, :].rearrange("p (a d b) -> p a d b", a=2, d=HD),
                                    w1l[:, o, :].rearrange("p (a b d) -> p a d b", a=2, d=HD),
                                    (float(HD) ** -0.5, 1.0)[o], None, ALU.mult).then_inc(w2_dve, 1)

            def setup_f(j):
                dve.wait_ge(f_full, j + 1)
                bank = ps[:, FB, :]
                if j == 0:
                    last = v.tensor_copy(cprojT[:, :], bank[:, 0:C])
                elif j == 1:
                    last = v.tensor_copy(l2orep[:, :, :], ps[0:L, FB, 0:HD].rearrange("p (a e) -> p a e", a=1)
                                         .broadcast_to([L, NH, HD]))
                elif j == 2:
                    last = v.tensor_tensor(BDM[:, :].rearrange("p (h d) -> p h d", h=NH),
                                           bank[:, 0:HD].rearrange("p (a d) -> p a d", a=1).broadcast_to([128, NH, HD]),
                                           hm.rearrange("p (h a) -> p h a", a=1).broadcast_to([128, NH, HD]), ALU.mult)
                elif j == 3:
                    last = v.tensor_copy(rep[:, 1, :], bank[:, 0:1].broadcast_to([128, C]))
                elif j == 4:
                    last = v.tensor_copy(wo[:, 0, :], bank[:, 0:C])
                elif j == 5:
                    last = v.tensor_copy(obias[:, 0, :], bank[:, 0:C])
                elif j in (6, 7):
                    last = v.tensor_copy(wexpT[:, 4 * (j - 6):4 * (j - 6) + 4, :].rearrange("p e c -> p (e c)"), bank)
                elif j == 8:
                    last = v.tensor_scalar(gam[:, 2:4], bank[:, 0:2], 1.0 / (NF * C * C), EPS, ALU.mult, ALU.add)
                elif j in (9, 10):
                    last = v.tensor_copy((w1T, w2T)[j - 9][:, :, :].rearrange("p a c -> p (a c)"), bank)
                elif j == 11:
                    v.tensor_scalar(bq1[:, 0:1], bank[:, 0:1], float(HD) ** -0.5, None, ALU.mult)
                    last = v.tensor_copy(bq1[:, 1:2], bank[:, 1:2])
                elif j == 12:
                    last = v.tensor_copy(obias[:, 1, :], bank[:, 0:C])
                else:
                    last = v.tensor_copy(b2row[:, :], bank[:, 0:C])
                last.then_inc(f_out, 1)
                if j == 8:
                    dve.wait_ge(f_out, 9)
                    v.tensor_scalar(gam[:, 4:6], gam[:, 2:4], 0.5, None, ALU.mult)
                    v.tensor_scalar(gam[:, 6:8], gam[:, 2:4], -0.5, None, ALU.mult).then_inc(w2_dve, 1)
                    dve.wait_ge(w2_dve, 7)
                    for n, w in enumerate((w1n, w2n)):
                        v.tensor_scalar(qtmp[:, n, :], w[:, :], gam[:, 6 + n:7 + n], None, ALU.is_lt).then_inc(w2_dve, 1)
                    dve.wait_ge(w2_dve, 9)
                    for n, w in enumerate((w1n, w2n)):
                        v.scalar_tensor_tensor(out=w[:, :], in0=w[:, :], scalar=gam[:, 4 + n:5 + n],
                                               in1=qtmp[:, n, :], op0=ALU.is_gt, op1=ALU.subtract).then_inc(w2_dve, 1)

            def p_evac(it, k):
                b = k % 2
                if it.layer == 0 and k <= 8:
                    a = (k - 1) // 2
                    dve.wait_ge(p_full[b], p_job(it, k) + 1)
                    until(dve, rope_sum, 4 * it.m + a - 1)
                    for g in range(2):
                        col = (0, 2)[a // 2] * NG + 2 * (a % 2) + g
                        last = v.scalar_tensor_tensor(out=t1[:, a % 2, g * T:(g + 1) * T],
                                                      in0=ps[:, PB[b], g * T:(g + 1) * T], scalar=lb[:, col:col + 1],
                                                      in1=cst[:, CCOS:CCOS + T], op0=ALU.add, op1=ALU.mult)
                    last.then_inc(p_out[b], 1)
                elif it.layer == 0:
                    dve.wait_ge(q_high, 2 * it.m + k - 8)
                    cols = slice((k - 9) * 512, (k - 8) * 512)
                    v.scalar_tensor_tensor(out=parts[:, it.par, 1, cols], in0=ps[:, PB[b], :], scalar=wqkbc[:, 0:1],
                                           in1=parts[:, it.par, 0, cols], op0=ALU.add, op1=ALU.subtract)\
                        .then_inc(p_out[b], 1)
                else:
                    o = k - 1
                    dve.wait_ge(split_a, 2 * it.m + o + 1)
                    until(dve, split_l, 2 * it.m)
                    v.scalar_tensor_tensor(out=rest[:, o, :], in0=ps[:, PB[b], 0:T], scalar=bq1[:, o:o + 1],
                                           in1=parts1[:, it.par, o, 0, :], op0=ALU.add, op1=ALU.subtract)\
                        .then_inc(p_out[b], 1)

            def k_parts(it):
                dve.wait_ge(k_high, it.m + 1)
                v.tensor_tensor(parts[:, it.par, 3, :], rk[:, :], parts[:, it.par, 2, :], ALU.subtract).then_inc(k_low, 1)

            def split_low(it):
                for o in range(2):
                    dve.wait_ge(split_m, 2 * it.m + o + 1)
                    v.tensor_tensor(parts1[:, it.par, o, 2, :], rest[:, o, :], parts1[:, it.par, o, 1, :], ALU.subtract)\
                        .then_inc(split_l, 1)

            def row_max(it, k):
                b, u, r = k % 2, k // 3, k % 3
                dve.wait_ge(s1_full[b], m_job(it, k) + 1)
                if r == 0:
                    v.tensor_reduce(nm[:, it.par, 0, 4 * u:4 * u + 4], ps[:, S1[b], :].rearrange("p (h t) -> p h t", h=4),
                                    AX.X, ALU.max, negate=True).then_inc(s1_out[b], 1)
                else:
                    h = 4 * u + 2 * (r - 1)
                    v.tensor_reduce(nm[:, it.par, 1, h:h + 2], ps[:, S1[b], :].rearrange("p (h t) -> p h t", h=2),
                                    AX.X, ALU.max, negate=True).then_inc(s1_out[b], 1)

            def max_parts(it, half):
                src = nm[:, it.par, :, 8 * half:8 * half + 8]
                dve.wait_ge(s1_out[1], m_job(it, 6 * half + 5) + 1)
                dve.wait_ge(s1_out[0], m_job(it, 6 * half + 4) + 1)
                v.tensor_copy(nmb[:, it.par, :, half, 0, :], src).then_inc(nm_high, 1)
                dve.wait_ge(nm_high, 2 * it.n + half + 1)
                v.tensor_tensor(nmb[:, it.par, :, half, 1, :], src, nmb[:, it.par, :, half, 0, :], ALU.subtract)\
                    .then_inc(nm_part, 1)

            def max_evac(it, half):
                dve.wait_ge(s1_full[0], mt_job(it, half) + 1)
                v.tensor_copy(mT[:, it.par, half, :], ps[0:MAXROWS, S1[0], :].bitcast(BF16)[:, 0:T]).then_inc(s1_out[0], 1)

            def f_chain(it, start):
                count = [FD[it.layer] * it.m + start]

                def link(ins):
                    count[0] += 1
                    ins.then_inc(f_dve[it.layer], 1)
                    dve.wait_ge(f_dve[it.layer], count[0])
                return link

            def statistics(src, link):
                for n in range(NT):
                    link(v.bn_stats(stats[:, n, :], src[:, n, :]))
                dve.sem_inc(stats_seen, 1)
                v.bn_aggr(mv[:, 0, :], stats[:, 0, :])
                link(v.bn_aggr(mv[:, 1, :], stats[:, 1, :]))
                v.tensor_scalar(ve[:, :], mv[:, :, 1], EPS, None, ALU.add).then_inc(var_ready, 1)

            def normalise(it, which):
                dve.wait_ge(rstd_done, 2 * it.n + which + 1)
                src = y if which == 0 or it.layer else acc
                if which == 0:
                    dst, signal = x1, x1_ready
                else:
                    dst, signal = xo[:, it.par, :, :], xo_ready
                    dve.wait_ge(xo_stored[it.par], 16 * it.half + 16)
                for n in range(NT):
                    last = v.tensor_scalar(dst[:, n, :], src[:, n, :], mv[:, n, 0:1], rstd[:, n:n + 1],
                                           ALU.subtract, ALU.mult)
                last.then_inc(signal, 1)

            def f_step(it, k):
                bank = ps[:, FB, :]
                if k in (0, 1, 3) or (it.layer == 0 and k in (5, 6, 8, 9, 10, 11, 12)) or (it.layer == 1 and k == 7):
                    dve.wait_ge(f_full, f_job(it, k) + 1)
                if k < 2:
                    link = f_chain(it, k)
                    heads = bank.rearrange("p (h w) -> p h w", w=OW)
                    link(v.reciprocal(rden[:, :], heads[:, :, HD]))
                    v.tensor_tensor(on[:, k, :].rearrange("p (h d) -> p h d", d=HD), heads[:, :, 0:HD],
                                    rden[:, :].rearrange("p (h a) -> p h a", a=1).broadcast_to([128, NH, HD]), ALU.mult)\
                        .then_inc(f_out, 1)
                elif k == 3:
                    dve.wait_ge(xr_done, it.n + 1)
                    v.tensor_tensor(y[:, :, :].rearrange("p n c -> p (n c)"), bank[:, 0:T],
                                    xr[:, :, :].rearrange("p n c -> p (n c)"), ALU.add).then_inc(f_out, 1)
                    dve.wait_ge(f_out, f_job(it, 3) + 1)
                    statistics(y, f_chain(it, 2))
                elif it.layer == 0:
                    moe_step(it, k, bank)
                elif k == 4:
                    dve.wait_ge(x1_ready, it.n + 1)
                    link = f_chain(it, 5)
                    link(v.tensor_tensor(acc[:, :, :], x1[:, :, :],
                                         b2row[:, :].rearrange("p (a c) -> p a c", a=1).broadcast_to([128, NT, C]), ALU.add))
                elif k == 7:
                    v.tensor_tensor(y[:, :, :].rearrange("p n c -> p (n c)"), bank[:, 0:T],
                                    acc[:, :, :].rearrange("p n c -> p (n c)"), ALU.add).then_inc(f_out, 1)
                    dve.wait_ge(f_out, f_job(it, 7) + 1)
                    statistics(y, f_chain(it, 6))

            def moe_step(it, k, bank):
                two = [128, NT, NE]

                def wide(ap):
                    return ap.rearrange("p (n a) -> p n a", a=1).broadcast_to(two)

                if k == 5:
                    logits = bank[:, 0:NT * NE].rearrange("p (n e) -> p n e", e=NE)
                    link = f_chain(it, 5)
                    link(v.tensor_reduce(lmax[:, :], logits, AX.X, ALU.max))
                    v.tensor_tensor(lsh[:, :, :], logits, wide(lmax[:, :]), ALU.subtract).then_inc(f_out, 1)
                    dve.wait_ge(lexp_done, it.m + 1)
                    link(v.tensor_reduce(lsum[:, :], lex[:, :, :], AX.X, ALU.add))
                    link(v.reciprocal(lrec[:, :], lsum[:, :]))
                    link(v.tensor_tensor(pr[:, :, :], lex[:, :, :], wide(lrec[:, :]), ALU.mult))
                    link(v.tensor_reduce(pmax[:, :], pr[:, :, :], AX.X, ALU.max))
                    link(v.tensor_tensor(peq[:, :, :], pr[:, :, :], wide(pmax[:, :]), ALU.is_equal))
                    order = cst[:, CW:CW + NE].rearrange("p (a e) -> p a e", a=1).broadcast_to(two)
                    link(v.tensor_tensor(pk[:, :, :], peq[:, :, :], order, ALU.mult))
                    link(v.tensor_reduce(pkm[:, :], pk[:, :, :], AX.X, ALU.max))
                    v.tensor_tensor(oh[:, :, :], pk[:, :, :], wide(pkm[:, :]), ALU.is_equal).then_inc(onehot_ready, 1)
                elif k == 6:
                    link = f_chain(it, 13)
                    before = bank[:, 0:NT * NE].rearrange("p (n e) -> p n e", e=NE)
                    v.scalar_tensor_tensor(out=kept[:, :, :], in0=before, scalar=float(CAP), in1=oh[:, :, :],
                                           op0=ALU.is_lt, op1=ALU.mult).then_inc(f_out, 1)
                    dve.wait_ge(f_out, f_job(it, 6) + 1)
                    v.tensor_tensor(gate[:, :, :], kept[:, :, :], wide(pmax[:, :]), ALU.mult).then_inc(gate_ready, 1)
                    link(v.tensor_tensor(ohs[:, :], oh[:, 0, :], oh[:, 1, :], ALU.add))
                    link(v.tensor_tensor(seen[:, :], seen[:, :], ohs[:, :], ALU.add))
                elif k == 8:
                    dve.wait_ge(x1_ready, it.n + 1)
                    v.tensor_tensor(acc[:, :, :].rearrange("p n c -> p (n c)"), bank[:, 0:T],
                                    x1[:, :, :].rearrange("p n c -> p (n c)"), ALU.add).then_inc(f_out, 1)
                    dve.wait_ge(f_out, f_job(it, 8) + 1)
                elif k >= 9:
                    n, half = (k - 9) // 2, (k - 9) % 2
                    link = f_chain(it, 15 + 3 * (k - 9))
                    for e in range(4):
                        ins = v.scalar_tensor_tensor(out=acc[:, n, :], in0=bank[:, e * C:(e + 1) * C],
                                                     scalar=gate[:, n, 4 * half + e:4 * half + e + 1], in1=acc[:, n, :],
                                                     op0=ALU.mult, op1=ALU.add)
                        if e < 3:
                            link(ins)
                    ins.then_inc(f_out, 1)
                    dve.wait_ge(f_out, f_job(it, k) + 1)
                    if k == 12:
                        statistics(acc, f_chain(it, 27))

            def half_slot(st, h):
                n2 = st.item(-2)
                if n2.real and h in NORMAL[n2.layer]:
                    normalise(n2, NORMAL[n2.layer].index(h))
                it, j = f_job_at(st, h)
                if j is not None:
                    f_step(it, j)

            def slots(st):
                if st.base == FIRST:
                    setup()
                if st.base == -1:
                    setup_2()
                for k in range(SLOTS):
                    half_slot(st, 2 * k)
                    m = st.item(0)
                    if m.real:
                        row_max(m, k)
                        if k in (5, 11):
                            max_parts(m, k // 6)
                    p = st.item(2)
                    if p.real:
                        for j in P_SLOTS[p.layer].get(k, []):
                            if j % 2 == 1 and j < 9 if p.layer == 0 else j > 0:
                                p_evac(p, j)
                        if p.layer == 0 and k in (9, 10):
                            p_evac(p, k)
                        if p.layer == 0 and k == 8:
                            k_parts(p)
                        if p.layer == 1 and k == 3:
                            split_low(p)
                    if st.base == -1:
                        for j in SETUP_SLOTS.get(k, []):
                            setup_f(j)
                    half_slot(st, 2 * k + 1)
                    if m.real and k in (5, 11):
                        max_evac(m, k // 6)

            walk(dve, slots)


_W = (("c_attn_w", "L0_attn_c_attn_w"), ("c_attn_b", "L0_attn_c_attn_b"), ("q2l_w", "L0_attn_q2l_w"),
      ("q2l_b", "L0_attn_q2l_b"), ("kv2l_w", "L0_attn_kv2l_w"), ("kv2l_b", "L0_attn_kv2l_b"),
      ("l2o_w", "L0_attn_l2o_w"), ("l2o_b", "L0_attn_l2o_b"), ("wqk_w", "L0_attn_wqk_w"),
      ("wqk_b", "L0_attn_wqk_b"), ("cproj_w", "L0_attn_cproj_w"), ("cproj_b", "L0_attn_cproj_b"),
      ("wg", "L0_ffn_wg"), ("W", "L0_ffn_W"), ("b", "L0_ffn_b"), ("Wq", "L1_attn_Wq"), ("bq", "L1_attn_bq"),
      ("Wk", "L1_attn_Wk"), ("bk", "L1_attn_bk"), ("Wv", "L1_attn_Wv"), ("bv", "L1_attn_bv"),
      ("Wo", "L1_attn_Wo"), ("bo", "L1_attn_bo"), ("W1", "L1_ffn_W1"), ("b1", "L1_ffn_b1"),
      ("W2", "L1_ffn_W2"), ("b2", "L1_ffn_b2"))


def kernel(**inputs):
    import numpy as np
    import concourse.bacc as bacc
    from concourse.bass_utils import run_bass_kernel_spmd

    nc = bacc.Bacc("TRN2", target_bir_lowering=False, num_devices=1)
    arrays = {}

    def dram(name, a):
        a = np.ascontiguousarray(a)
        arrays[name] = a
        return nc.dram_tensor(name, a.shape, mybir.dt.from_np(a.dtype), kind="ExternalInput").ap()

    x = dram("x", inputs["L0_attn_x"])
    c = dram("shape_constants", constants())
    w = {short: dram(long, inputs[long]) for short, long in _W}
    out = nc.dram_tensor("out", (NB, T, C), F32, kind="ExternalOutput").ap()
    build(nc, x, c, w, out)
    r = run_bass_kernel_spmd(nc, [arrays], core_ids=[0])
    return r.results[0]["out"]
```

```python
from contextlib import ExitStack

import concourse.bass as bass
from concourse import mybir

F32 = mybir.dt.float32
BF16 = mybir.dt.bfloat16
ALU = mybir.AluOpType
ACT = mybir.ActivationFunctionType
AX = mybir.AxisListType

C = 128
T = 256
TILE = 128
NT = T // TILE
NB = 8
NH = 16
HD = C // NH
L = 32
NG = 4
NE = 8
CAP = NB * T // NE
NF = 4
EPS = 1e-5
MASKED = -1.0e30
MAXROW = 96
MAXROWS = 16
STACKED = MAXROW + MAXROWS
OW = 32
NP = 6

ITEMS = 2 * NB

S1 = (0, 1)
S2 = (2, 3)
PB = 4
OB = 6
FB = (5, 7)

CI = 0
CCOS = CI + 128
CSIN = CCOS + T
CHM = CSIN + T
CJM = CHM + NH
CE = CJM + 4
CE8 = CE + C
CSEL = CE8 + C
CU = CSEL + NH
CW = CU + 128
CONE = CW + NE
NC = CONE + 128


def constants():
    import numpy as np
    c = np.zeros((128, NC), np.float32)
    c[:, CI:CI + 128] = np.eye(128)
    inv = (np.float32(1.0) / np.power(np.float32(10000.0), np.arange(0, L, 2, dtype=np.float32) / np.float32(L)))
    fr = np.outer(np.arange(T, dtype=np.float32), inv.astype(np.float32)).astype(np.float32)
    p = np.arange(128)
    lat, j = 2 * (p % 64 // 4) + p // 64, p % 4
    c[:, CCOS:CCOS + T] = np.cos(fr)[:, lat // 2].T
    c[:, CSIN:CSIN + T] = np.sin(fr)[:, lat // 2].T * np.where(p < 64, -1.0, 1.0)[:, None]
    c[p, CHM + p // HD] = 1.0
    c[p, CJM + j] = float(L) ** -0.5
    c[lat, CE + p] = 1.0
    c[p % HD, CE8 + p] = 1.0
    r = np.arange(MAXROWS)
    for s in range(NH):
        c[MAXROW + r[r % 8 == s % 8], CSEL + s] = 1.0
    c[:, CU:CU + 128] = np.triu(np.ones((128, 128)), 1)
    c[:, CW:CW + NE] = np.arange(NE, 0, -1)
    c[:, CONE:CONE + 128] = 1.0
    return c


class Item:

    def __init__(self, b, i=0):
        self.b, self.i = b, i
        self.n, self.half, self.par = b + 2 * i, b // 2 + i, b % 2
        self.layer = int(b >= NB)
        self.m = self.n - NB if self.layer else self.n
        self.real = 0 <= b < ITEMS

    def before(self, d):
        it = Item(self.b - d, self.i)
        assert isinstance(self.i, int) or (it.real and it.layer == self.layer)
        return it


class Step:

    def __init__(self, base, i=0):
        self.base, self.i = base, i

    def item(self, d):
        return Item(self.base + d, self.i)


FIRST, LAST = -1, ITEMS + 1
LOOPS = {2: 2, 10: 2}


def walk(eng, slots):
    s = FIRST
    while s <= LAST:
        if s in LOOPS:
            with eng.Fori(0, LOOPS[s]) as i:
                for off in range(2):
                    slots(Step(s + off, i))
            s += 2 * LOOPS[s]
        else:
            slots(Step(s))
            s += 1


PJOBS = (7, 3)


def p_job(it, k):
    return PJOBS[it.layer] * it.m + (PJOBS[0] * NB if it.layer else 0) + k


FJOBS = (13, 8)
SETUP_F = (0, 14)


def f_job(it, k):
    per = [(j + 1 - k % 2) // 2 for j in FJOBS]
    return per[it.layer] * it.m + (per[0] * NB if it.layer else 0) + SETUP_F[k % 2] + k // 2


def m_job(it, k):
    return 8 * it.n + k // 2 + (k // 2 >= 3) if k % 2 == 0 else 7 * it.n + 1 + k // 2


def e_job(it, k):
    return 6 * it.n + k // 2


def mt_job(it, half):
    return 8 * it.n + 3 + 4 * half


def v_job(it):
    return 7 * it.n


TICKS = 48


def every(first, gap=4, count=12):
    return [first + gap * k for k in range(count)]


PE_P = ([-48, -44, -37, -28, -24, -18, -9], [-50, -45, -36])
ACT_P = ([-47, -43, -36, -27, -24, -18, -9], [-52, -44, -32])
DVE_P = ([None, -42, -35, -27, -22, -16, -7], [None, -43, -28])
POOL_ROPE = ([-43, -26, -19, -11], [])
ACT_K = ([-23, -7], [])
DVE_K = ([-22, 0], [])
ACT_SPLIT = ([], [-27])
DVE_SPLIT = ([], [-26])
PE_V = ([-1], [-2])
ACT_V = ([-4], [-8])
PE_M = (every(1), every(1))
DVE_M = (every(1), every(1))
DVE_PARTS = ([22, 46], [22, 47])
PE_MT = ([23, 47], [24, 48])
DVE_MT = ([23, 47], [23, 47])
PE_E = (every(36), every(33))
ACT_E = (every(36), every(36))
POOL_E = (every(40), every(37))
PE_PV = (every(47), every(44))
ACT_O = ([68, 84], [64, 85])
PE_F = ([92, 94, 99, 102, 110, 114, 120, 123, 128, 129, 131, 134, 137], [97, 98, 103, 108, 115, 118, 124, 132])
ACT_F = ([92, 94, 99, 103, 110, 114, 120, 126, 128, 129, 131, 135, 136], [97, 99, 101, 114, 115, 118, 124, 139])
DVE_F = ([92, 94, 99, 103, 107, 114, 120, 123, 128, 129, 131, 134, 135], [97, 98, 103, 108, 115, 118, 124, 133])
POOL_POW = ([101, 139], [109, 136])
DVE_NORM = ([106, 138], [112, 142])
POOL_XR = ([93], [93])
SP_MAX = ([22, 46], [18, 47])
SP_STACK = ([-16, 1], [-24, 1])
SP_X = ([-85], [-93])
SP_XF = ([41], [52])
SP_STORE = ([130], [136])
SETUP_TIMES = [0, 2, 4, 6, 9, 10, 12, 15, 23, 24, 28, 32, 37, 46]
POOL_CLEAR = 32


def due(st, tick, times):
    for layer in range(2):
        for k, t in enumerate(times[layer]):
            if t is not None and t % TICKS == tick:
                it = st.item(-(t // TICKS))
                if it.real and it.layer == layer:
                    yield it, k


TERMS = (((0, 0), (0, 1), (1, 0)),
         ((0, 0), (0, 1), (1, 0), (0, 2), (2, 0), (1, 1)))


def stacked_count(it):
    per = [2 * 16 * len(t) for t in TERMS]
    return per[0] * NB // 2 + per[1] * (it.half - NB // 2 + 1) if it.layer else per[0] * (it.half + 1)


W_DVE = 22
SETUP_STEP = 0
POOL_SETUP = 11


def until(eng, sem, count):
    if isinstance(count, int) and count <= 0:
        return
    eng.wait_ge(sem, count)


def build(nc, x, cst_d, W, out):
    x2d = nc.dram_tensor("x2_scratch", (NB * T, C), F32, kind="Internal").ap()
    xr_d = x.rearrange("b (n p) c -> b p n c", p=TILE)
    x2_d = x2d.rearrange("(b n p) c -> b p n c", b=NB, p=TILE)
    out_d = out.rearrange("b (n p) c -> b p n c", p=TILE)

    with ExitStack() as ctx:
        def sb(name, shape, dt=F32):
            return ctx.enter_context(nc.sbuf_tensor(name, shape, dt))

        def sem(name):
            return ctx.enter_context(nc.semaphore(name))

        ps = ctx.enter_context(nc.psum_tensor("ps", [128, 8, 512], F32))

        cst = sb("cst", [128, NC])
        cattn = sb("cattn", [128, 3, C])
        cproj = sb("cproj", [128, C])
        q2l = sb("q2l", [L, 2, HD])
        wqk = sb("wqk", [L, L])
        l2o = sb("l2o", [HD, L])
        lbias = sb("lbias", [L, 3])
        l2ob = sb("l2ob", [HD, 1])
        cattnb = sb("cattnb", [128, 3])
        rowb = sb("rowb", [1, 3, C])
        wgate = sb("wgate", [128, NE])
        wexp = sb("wexp", [128, NE, C])
        bexp = sb("bexp", [NE, C])
        w1l = sb("w1l", [128, 4, C])
        b1l = sb("b1l", [128, 3])
        w1n = sb("w1n", [128, NF * C])
        w2n = sb("w2n", [128, NF * C])
        b1h = sb("b1h", [128, NF])
        identb = sb("identb", [128, 128], BF16)
        maskb = sb("maskb", [128, 4, 128], BF16)
        triub = sb("triub", [128, 128], BF16)
        onesb = sb("onesb", [128, 128], BF16)
        neghalf = sb("neghalf", [128, 2])
        q2lrep = sb("q2lrep", [L, 2, NH, HD])
        wqkrep = sb("wqkrep", [L, 2, L // 2, 4])
        l2orep = sb("l2orep", [L, NH, HD])
        WL = sb("WL", [128, 2, NG * C])
        BDW = sb("BDW", [128, C])
        BDM = sb("BDM", [128, C])
        perm = sb("perm", [128, C])
        cprojT = sb("cprojT", [128, C])
        wv = sb("wv", [128, 2, C])
        wo = sb("wo", [128, 2, C])
        obias = sb("obias", [128, 2, C])
        lb = sb("lb", [128, 8])
        wqkbc = sb("wqkbc", [128, 1])
        ybc = sb("ybc", [128, 1])
        rep = sb("rep", [128, 3, C])
        wexpT = sb("wexpT", [128, NE, C])
        wq1 = sb("wq1", [128, 2, C])
        bq1 = sb("bq1", [128, 2])
        w1T = sb("w1T", [128, NF, C])
        w2T = sb("w2T", [128, NF, C])
        b2row = sb("b2row", [128, C])
        gam = sb("gam", [128, 8])
        xin = sb("xin", [128, 2, NT, C])
        xT = sb("xT", [128, 2, T])
        t1 = sb("t1", [128, 2, 2 * T])
        tb = sb("tb", [128, 2, 2 * T])
        t2 = sb("t2", [128, 2, 2 * T])
        rq = sb("rq", [128, NG * T])
        rk = sb("rk", [128, NG * T])
        parts = sb("parts", [128, 2, 4, NG * T], BF16)
        rest = sb("rest", [128, 2, T])
        parts1 = sb("parts1", [128, 2, 2, 3, T], BF16)
        QS = [[sb(f"QS{l}{p}", [128, NH, T], BF16) for p in range(2)] for l in range(2)]
        KS = [[sb(f"KS{l}{p}", [128, NH, T], BF16) for p in range(2)] for l in range(2)]
        nm = sb("nm", [128, 2, NT, NH])
        nmb = sb("nmb", [128, 2, NT, 2, 2, 8], BF16)
        mT = sb("mT", [MAXROWS, 2, 2, T], BF16)
        vaug = sb("vaug", [128, 2, NT, NH, OW])
        prob = sb("prob", [128, NP, 512])
        BD = prob[:, 0:2, :].rearrange("p k (g c) -> p k g c", g=NG)
        qtmp = sb("qtmp", [128, 2, NF * C])
        oT = sb("oT", [128, NG, T])
        rden = sb("rden", [128, NT, NH])
        on = sb("on", [128, NT, C])
        onT = sb("onT", [128, T])
        xf = sb("xf", [128, 2, NT, C])
        xr = sb("xr", [128, NT, C])
        y = sb("y", [128, NT, C])
        stats = sb("stats", [128, NT, 6])
        mv = sb("mv", [128, NT, 2])
        ve = sb("ve", [128, NT])
        rstd = sb("rstd", [128, NT])
        x1 = sb("x1", [128, NT, C])
        x1T = sb("x1T", [128, T])
        lmax = sb("lmax", [128, NT])
        lsh = sb("lsh", [128, NT, NE])
        lex = sb("lex", [128, NT, NE])
        lsum = sb("lsum", [128, NT])
        lrec = sb("lrec", [128, NT])
        pr = sb("pr", [128, NT, NE])
        pmax = sb("pmax", [128, NT])
        peq = sb("peq", [128, NT, NE])
        pk = sb("pk", [128, NT, NE])
        pkm = sb("pkm", [128, NT])
        oh = sb("oh", [128, NT, NE], BF16)
        seen = sb("seen", [128, NE], BF16)
        ohs = sb("ohs", [128, NE], BF16)
        kept = sb("kept", [128, NT, NE])
        gate = sb("gate", [128, NT, NE])
        gT = sb("gT", [NE, T])
        acc = sb("acc", [128, NT, C])
        hT = sb("hT", [128, NF, T])
        xo = sb("xo", [128, 2, NT, C])

        w_in = sem("w_in")
        w2_in = sem("w2_in")
        w_pool = sem("w_pool")
        w_pe = sem("w_pe")
        w_dve = sem("w_dve")
        w_act = sem("w_act")
        x_in = [sem(f"x_in{p}") for p in range(2)]
        xf_in = [sem(f"xf_in{p}") for p in range(2)]
        xo_stored = [sem(f"xo_stored{p}") for p in range(2)]
        p_full = sem("p_full")
        p_out = sem("p_out")
        swapped = sem("swapped")
        rope_mul = sem("rope_mul")
        rope_sum = sem("rope_sum")
        q_high = sem("q_high")
        k_high = sem("k_high")
        k_low = sem("k_low")
        split_a = sem("split_a")
        split_m = sem("split_m")
        split_l = sem("split_l")
        stacked = [[sem(f"stacked{h}{p}") for p in range(2)] for h in range(2)]
        s1_full = [sem(f"s1_full{b}") for b in range(2)]
        s1_out = [sem(f"s1_out{b}") for b in range(2)]
        nm_part = sem("nm_part")
        max_in = [[sem(f"max_in{h}{p}") for p in range(2)] for h in range(2)]
        s2_full = [sem(f"s2_full{b}") for b in range(2)]
        exp_done = sem("exp_done")
        clear_begun = sem("clear_begun")
        stats_seen = sem("stats_seen")
        causal = sem("causal")
        pv_done = sem("pv_done")
        o_out = sem("o_out")
        f_full = [sem(f"f_full{b}") for b in range(2)]
        f_out = [sem(f"f_out{b}") for b in range(2)]
        f_dve = sem("f_dve")
        var_ready = sem("var_ready")
        nm_high = sem("nm_high")
        w2_dve = sem("w2_dve")
        onehot_ready = sem("onehot_ready")
        gate_ready = sem("gate_ready")
        x1_ready = sem("x1_ready")
        xo_ready = sem("xo_ready")
        xr_done = sem("xr_done")
        rstd_done = sem("rstd_done")
        lexp_done = sem("lexp_done")

        block = ctx.enter_context(nc.Block())

        ident = cst[:, CI:CI + 128]
        hm = cst[:, CHM:CHM + NH]
        ones = cst[:, CONE:CONE + 128]

        NW, NW2 = 13, 20

        @block.sync
        def _(sp):
            def load(dst, src, s):
                sp.dma_start(dst, src).then_inc(s, 16)

            load(cst[:, :], cst_d, w_in)
            load(cattn[:, :, :], W["c_attn_w"].rearrange("(a p) c -> p a c", p=128), w_in)
            load(q2l[:, 0, :], W["q2l_w"], w_in)
            load(q2l[:, 1, :], W["kv2l_w"], w_in)
            load(wqk[:, :], W["wqk_w"], w_in)
            load(l2o[:, :], W["l2o_w"], w_in)
            load(lbias[:, 0:1], W["q2l_b"].rearrange("(p a) -> p a", a=1), w_in)
            load(lbias[:, 1:2], W["kv2l_b"].rearrange("(p a) -> p a", a=1), w_in)
            load(lbias[:, 2:3], W["wqk_b"].rearrange("(p a) -> p a", a=1), w_in)
            load(l2ob[:, :], W["l2o_b"].rearrange("(p a) -> p a", a=1), w_in)
            for n in range(3):
                load(cattnb[:, n:n + 1], W["c_attn_b"][n * C:(n + 1) * C].rearrange("(p a) -> p a", a=1), w_in)

            def other_weights():
                load(cproj[:, :], W["cproj_w"], w2_in)
                load(rowb[:, 0, :], W["cproj_b"].rearrange("(a p) -> a p", a=1), w2_in)
                load(rowb[:, 1, :], W["bo"].rearrange("(a p) -> a p", a=1), w2_in)
                load(rowb[:, 2, :], W["b2"].rearrange("(a p) -> a p", a=1), w2_in)
                load(wgate[:, :], W["wg"], w2_in)
                load(wexp[:, :, :], W["W"].rearrange("e f h -> f e h"), w2_in)
                load(bexp[:, :], W["b"], w2_in)
                for n, name in enumerate(("Wq", "Wk", "Wv", "Wo")):
                    load(w1l[:, n, :], W[name], w2_in)
                for n, name in enumerate(("bq", "bk", "bv")):
                    load(b1l[:, n:n + 1], W[name].rearrange("(p a) -> p a", a=1), w2_in)
                load(w1n[:, :].rearrange("p (a c) -> p a c", a=NF), W["W1"].rearrange("(a p) c -> p a c", p=128), w2_in)
                load(w2n[:, :], W["W2"], w2_in)
                for n in range(NF):
                    load(b1h[:, n:n + 1], W["b1"][n * C:(n + 1) * C].rearrange("(p a) -> p a", a=1), w2_in)

            def value(v):
                return v if isinstance(v, int) else sp.snap(v)

            def load_x(it):
                row, mine = value(it.m), value(16 * (it.half - NB // 2) + 32)
                if it.before(2).real:
                    read = value(p_job(it.before(2), 0) + 1)
                    sp.wait_ge(p_full, read)
                if it.layer:
                    sp.wait_ge(xo_stored[it.par], mine)
                src = x2_d if it.layer else xr_d
                sp.dma_start(xin[:, it.par, :, :], src[row]).then_inc(x_in[it.par], 16)

            def load_xf(it):
                row = value(it.m)
                until(sp, xr_done, it.n)
                src = x2_d if it.layer else xr_d
                sp.dma_start(xf[:, it.par, :, :], src[row]).then_inc(xf_in[it.par], 16)

            def stack(it, half):
                rows = slice(64 * half, 64 * half + 64)
                heads = slice(8 * half, 8 * half + 8)
                read = value(e_job(it.before(2), 6 * half + 5) + 1)
                ready = value(2 * it.m + (2 if it.layer else half + 1))
                if it.before(2).real and half == 0:
                    sp.wait_ge(s2_full[1], read)
                done = stacked[half][it.par]
                if it.layer == 0:
                    sp.wait_ge(k_low, ready)
                    for r, (qp, kp) in enumerate(TERMS[0]):
                        for dst, part in ((QS[0], qp), (KS[0], 2 + kp)):
                            sp.dma_start(dst[it.par][L * r:L * r + L, heads, :],
                                         parts[:, it.par, part, 512 * half:512 * half + 512]).then_inc(done, 16)
                else:
                    sp.wait_ge(split_l, ready)
                    sp.wait_ge(w_pool, POOL_SETUP)
                    for r, (qp, kp) in enumerate(TERMS[1]):
                        for o, dst, part in ((0, QS[1], qp), (1, KS[1], kp)):
                            sp.dma_start(dst[it.par][HD * r:HD * r + HD, heads, :],
                                         parts1[rows, it.par, o, part, :]).then_inc(done, 16)

            def max_rows(it, half):
                sp.wait_ge(s1_out[0], mt_job(it, half) + 1)
                src = mT[:, it.par, half:half + 1, :].broadcast_to([MAXROWS, 8, T])
                sp.dma_start(QS[it.layer][it.par][MAXROW:STACKED, 8 * half:8 * half + 8, :], src)\
                    .then_inc(max_in[half][it.par], 16)

            def store(it):
                row, ready = value(it.m), value(it.n + 1)
                sp.wait_ge(xo_ready, ready)
                if it.layer == 0:
                    sp.dma_start(x2_d[row], xo[:, it.par, :, :]).then_inc(xo_stored[it.par], 16)
                else:
                    sp.dma_start(out_d[row], xo[:, it.par, :, :]).then_inc(xo_stored[it.par], 16)

            def slots(st):
                for tick in range(TICKS):
                    for it, half in due(st, tick, SP_MAX):
                        max_rows(it, half)
                    for it, half in due(st, tick, SP_STACK):
                        stack(it, half)
                    for it, _ in due(st, tick, SP_X):
                        load_x(it)
                    for it, _ in due(st, tick, SP_XF):
                        load_xf(it)
                    for it, _ in due(st, tick, SP_STORE):
                        store(it)

            load_x(Item(0))
            other_weights()
            walk(sp, slots)
            for p in range(2):
                sp.wait_ge(xo_stored[p], 16 * ITEMS // 2 + 16)

        @block.gpsimd
        def _(pool):
            g = nc.gpsimd
            g.memset(neghalf[:, :], -0.5).then_inc(w_pool, 1)
            g.memset(maskb[:, :, :], 0.0).then_inc(w_pool, 1)
            for p in range(2):
                g.memset(vaug[:, p, :, :, :], 0.0).then_inc(w_pool, 1)
            pool.wait_ge(w_pool, 4)
            g.affine_select(out=maskb[:, :, :], in_=maskb[:, :, :], compare_op=ALU.is_ge, fill=MASKED, base=0,
                            pattern=[[0, 4], [-1, 128]], channel_multiplier=1).then_inc(w_pool, 1)
            for p in range(2):
                g.memset(vaug[:, p, :, :, HD:HD + 1], 1.0).then_inc(w_pool, 1)
            pool.wait_ge(w_in, 16 * NW)

            def clear_stacks():
                for p in range(2):
                    g.memset(QS[1][p][0:MAXROW, :, :], 0.0).then_inc(w_pool, 1)
                    g.memset(KS[1][p][0:MAXROW, :, :], 0.0).then_inc(w_pool, 1)

            def rope(it, a):
                pair, kind = a // 2, a % 2
                pool.wait_ge(swapped, 4 * it.m + a + 1)
                until(pool, rope_sum, 4 * it.m + a - 1)
                sin = cst[:, CSIN:CSIN + T].rearrange("p (a t) -> p a t", a=1).broadcast_to([128, 2, T])
                g.tensor_tensor(t2[:, a % 2, :].rearrange("p (a t) -> p a t", a=2),
                                tb[:, a % 2, :].rearrange("p (a t) -> p a t", a=2), sin, ALU.mult).then_inc(rope_mul, 1)
                pool.wait_ge(p_out, p_job(it, 1 + 3 * pair + kind) + 1)
                pool.wait_ge(rope_mul, 4 * it.m + a + 1)
                if kind == 0 and it.before(1).real:
                    pool.wait_ge(p_full, p_job(it.before(1), 3 + 3 * pair) + 1)
                if kind == 1:
                    until(pool, k_low, 2 * it.m + pair - 1)
                dst = (rq, rk)[kind][:, pair * 2 * T:(pair + 1) * 2 * T]
                g.tensor_tensor(dst, t1[:, a % 2, :], t2[:, a % 2, :], ALU.add).then_inc(rope_sum, 1)

            def clear(it, k):
                pool.wait_ge(exp_done, 12 * it.n + k + 1)
                pool.sem_inc(clear_begun, 1)
                heads = 2 if k % 3 < 2 else 4
                v = prob[:, k % NP, :].rearrange("p (h t) -> p h t", h=heads)[:, :, 0:TILE]
                g.affine_select(out=v, in_=v, compare_op=ALU.is_ge, fill=0.0, base=0,
                                pattern=[[0, heads], [1, TILE]], channel_multiplier=-1).then_inc(causal, 1)

            def power(it, which):
                pool.wait_ge(var_ready, 2 * it.n + which + 1)
                g.tensor_tensor(rstd[:, :], ve[:, :], neghalf[:, :], ALU.pow).then_inc(rstd_done, 1)

            def residual(it):
                pool.wait_ge(f_out[1], SETUP_F[1])
                pool.wait_ge(xf_in[it.par], 16 * it.half + 16)
                if it.before(1).real:
                    pool.wait_ge(f_out[1], f_job(it.before(1), 3) + 1)
                ob = obias[:, it.layer:it.layer + 1, :].broadcast_to([128, NT, C])
                g.tensor_tensor(xr[:, :, :], xf[:, it.par, :, :], ob, ALU.add).then_inc(xr_done, 1)

            def slots(st):
                for tick in range(TICKS):
                    for it, k in due(st, tick, POOL_E):
                        clear(it, k)
                    for it, a in due(st, tick, POOL_ROPE):
                        rope(it, a)
                    for it, _ in due(st, tick, POOL_XR):
                        residual(it)
                    if st.base == SETUP_STEP and tick == POOL_CLEAR:
                        clear_stacks()
                    for it, which in due(st, tick, POOL_POW):
                        power(it, which)

            walk(pool, slots)

        @block.scalar
        def _(act):
            a_ = nc.scalar

            def setup():
                for kind in range(2):
                    act.wait_ge(w_pe, 2 + kind)
                    a_.activation(WL[:, kind, :], ps[:, kind, :], ACT.Copy).then_inc(w_act, 1)
                act.wait_ge(w_pe, 5)
                a_.activation(wv[:, 0, :], ps[:, 5, 0:C], ACT.Copy).then_inc(w_act, 1)
                act.wait_ge(w_dve, W_DVE)

            def p_evac(it, k):
                act.wait_ge(p_full, p_job(it, k) + 1)
                if k == 0:
                    if it.before(2).real:
                        act.wait_ge(s1_full[1], v_job(it.before(2)) + 1)
                    a_.activation(xT[:, it.par, :], ps[:, PB, 0:T], ACT.Copy).then_inc(p_out, 1)
                elif it.layer == 0 and k % 3:
                    pair, kind = k // 3, k % 3 - 1
                    a = 2 * pair + kind
                    until(act, rope_mul, 4 * it.m + a - 1)
                    for g in range(2):
                        col = kind * NG + 2 * pair + g
                        for src, dst in ((slice(0, 64), slice(64, 128)), (slice(64, 128), slice(0, 64))):
                            ins = a_.activation(tb[dst, a % 2, g * T:(g + 1) * T], ps[src, PB, g * T:(g + 1) * T],
                                                ACT.Identity, bias=lb[src, col:col + 1])
                    ins.then_inc(swapped, 1)
                elif it.layer == 0:
                    pair = k // 3 - 1
                    parts_free(it)
                    a_.activation(parts[:, it.par, 0, pair * 512:(pair + 1) * 512], ps[:, PB, :], ACT.Identity,
                                  bias=wqkbc[:, 0:1]).then_inc(q_high, 1)
                else:
                    o = k - 1
                    if it.before(2).layer:
                        parts_free(it)
                    a_.activation(parts1[:, it.par, o, 0, :], ps[:, PB, 0:T], ACT.Identity,
                                  bias=bq1[:, o:o + 1]).then_inc(split_a, 1)

            def parts_free(it):
                if it.before(2).real:
                    for h in range(2):
                        act.wait_ge(stacked[h][it.par], stacked_count(it.before(2)))

            def k_parts(it, pair):
                act.wait_ge(rope_sum, 4 * it.m + 2 * pair + 2)
                parts_free(it)
                cols = slice(pair * 512, (pair + 1) * 512)
                a_.activation(parts[:, it.par, 2, cols], rk[:, cols], ACT.Copy).then_inc(k_high, 1)

            def split_middle(it):
                for o in range(2):
                    act.wait_ge(p_out, p_job(it, o + 1) + 1)
                    a_.activation(parts1[:, it.par, o, 1, :], rest[:, o, :], ACT.Copy).then_inc(split_m, 1)

            def values(it):
                act.wait_ge(s1_full[1], v_job(it) + 1)
                if it.before(2).real:
                    act.wait_ge(pv_done, 12 * it.before(2).n + 12)
                else:
                    act.wait_ge(w_pool, 7)
                a_.activation(vaug[:, it.par, :, :, 0:HD],
                              ps[:, S1[1], 0:T].rearrange("p (n h d) -> p n h d", n=NT, h=NH), ACT.Copy)\
                    .then_inc(s1_out[1], 1)

            def exp(it, k):
                act.wait_ge(s2_full[k % 2], e_job(it, k) + 1)
                until(act, pv_done, 12 * it.n + k - NP + 1)
                a_.activation(prob[:, k % NP, :], ps[:, S2[k % 2], :], ACT.Exp).then_inc(exp_done, 1)

            def o_evac(it, h):
                act.wait_ge(pv_done, 12 * it.n + 6 * h + 6)
                if h == 0 and it.before(1).real:
                    act.wait_ge(f_full[1], f_job(it.before(1), 1) + 1)
                a_.activation(oT[:, 2 * h:2 * h + 2, :].rearrange("p a t -> p (a t)"), ps[:, OB, :], ACT.Copy)\
                    .then_inc(o_out, 1)

            def f_evac(it, k):
                if k in (2, 4):
                    act.wait_ge(f_full[k % 2], f_job(it, k) + 1)
                    a_.activation((onT if k == 2 else x1T)[:, :], ps[:, FB[k % 2], 0:T], ACT.Copy).then_inc(f_out[k % 2], 1)
                elif it.layer == 0 and k == 5:
                    act.wait_ge(f_out[1], f_job(it, 5) + 1)
                    a_.activation(lex[:, :, :], lsh[:, :, :], ACT.Exp).then_inc(lexp_done, 1)
                elif it.layer == 0 and k == 7:
                    act.wait_ge(f_full[k % 2], f_job(it, k) + 1)
                    a_.activation(gT[:, :], ps[0:NE, FB[k % 2], 0:T], ACT.Copy).then_inc(f_out[k % 2], 1)
                elif it.layer == 1 and k in (5, 6):
                    act.wait_ge(f_full[k % 2], f_job(it, k) + 1)
                    for c in range(2):
                        ch = 2 * (k - 5) + c
                        ins = a_.activation(hT[:, ch, :], ps[:, FB[k % 2], c * T:(c + 1) * T], ACT.Relu, bias=b1h[:, ch:ch + 1])
                    ins.then_inc(f_out[k % 2], 1)

            def slots(st):
                if st.base == FIRST:
                    setup()
                for tick in range(TICKS):
                    for it, k in due(st, tick, ACT_E):
                        exp(it, k)
                    for it, half in due(st, tick, ACT_O):
                        o_evac(it, half)
                    for it, k in due(st, tick, ACT_F):
                        f_evac(it, k)
                    for it, k in due(st, tick, ACT_P):
                        p_evac(it, k)
                    for it, pair in due(st, tick, ACT_K):
                        k_parts(it, pair)
                    for it, _ in due(st, tick, ACT_SPLIT):
                        split_middle(it)
                    for it, _ in due(st, tick, ACT_V):
                        values(it)

            walk(act, slots)

        @block.tensor
        def _(pe):
            mm, tr = nc.tensor.matmul, nc.tensor.transpose

            def setup():
                pe.wait_ge(w_in, 16 * NW)
                pe.wait_ge(w_dve, 2)
                for kind in range(2):
                    mm(ps[:, FB[1], L * kind:L * kind + L], q2lrep[:, kind, :, :].rearrange("p h d -> p (h d)"),
                       cst[0:L, CI:CI + L], start=True, stop=True)
                mm(ps[:, FB[1], 64:64 + L], wqkrep[:, :, :, :].rearrange("p a l b -> p (a l b)"),
                   cst[0:L, CI:CI + L], start=True, stop=True)
                mm(ps[:, FB[1], 96:97], cst[0:L, CE:CE + C], lbias[:, 2:3], start=True, stop=True).then_inc(w_pe, 1)
                for kind in range(2):
                    pe.wait_ge(w_dve, 2 + 4 * (kind + 1))
                    mm(ps[:, kind, :], cattn[:, kind, :], BD[:, kind, :, :].rearrange("p g c -> p (g c)"),
                       start=True, stop=True).then_inc(w_pe, 1)
                for kind in range(2):
                    for g in range(NG):
                        col = ps[:, 4, kind * NG + g:kind * NG + g + 1]
                        mm(col, BD[:, kind, g, :], cattnb[:, kind:kind + 1], start=True, stop=False)
                        last = mm(col, cst[0:L, CE:CE + C], lbias[:, kind:kind + 1], start=False, stop=True)
                last.then_inc(w_pe, 1)
                tr(ps[:, 5, 0:C], cattn[:, 2, :], ident).then_inc(w_pe, 1)
                pe.wait_ge(w_act, 3)
                pe.wait_ge(w_dve, W_DVE)
                pe.wait_ge(w_pool, 5)

            def setup_f(j):
                if j == 0:
                    pe.wait_ge(w2_in, 16 * NW2)
                    pe.wait_ge(w2_dve, 4)
                else:
                    pe.wait_ge(f_out[1], j)
                bank = ps[:, FB[1], :]
                if j == 0:
                    last = tr(bank[:, 0:C], cproj[:, :], ident)
                elif j == 1:
                    last = tr(ps[0:L, FB[1], 0:HD], l2o[:, :], cst[0:HD, CI:CI + HD])
                elif j == 2:
                    last = mm(bank[:, 0:HD], l2orep[:, :, :].rearrange("p h e -> p (h e)"), q2l[:, 1, :],
                              start=True, stop=True)
                elif j == 3:
                    mm(bank[:, 0:1], l2orep[:, :, :].rearrange("p h e -> p (h e)"), lbias[:, 1:2], start=True, stop=False)
                    last = mm(bank[:, 0:1], cst[0:HD, CE8:CE8 + C], l2ob[:, :], start=False, stop=True)
                elif j == 4:
                    last = mm(bank[:, 0:C], BDM[:, :], cprojT[:, :], start=True, stop=True)
                elif j == 5:
                    mm(bank[:, 0:C], rep[:, 0, :], wo[:, 0, :], start=True, stop=False)
                    mm(bank[:, 0:C], rep[:, 1, :], cprojT[:, :], start=False, stop=False)
                    last = mm(bank[:, 0:C], cst[0:1, CONE:CONE + 128], rowb[:, 0, :], start=False, stop=True)
                elif j in (6, 7):
                    for e in range(4):
                        last = tr(bank[:, e * C:(e + 1) * C], wexp[:, 4 * (j - 6) + e, :], ident)
                elif j == 8:
                    last = mm(bank[:, 0:2], ones, gam[:, 0:2], start=True, stop=True)
                elif j in (9, 10):
                    pe.wait_ge(w2_dve, 11)
                    for a in range(NF):
                        last = tr(bank[:, a * C:(a + 1) * C], (w1n, w2n)[j - 9][:, a * C:(a + 1) * C], ident)
                elif j == 11:
                    for o in range(2):
                        last = mm(bank[:, o:o + 1], perm[:, :], b1l[:, o:o + 1], start=True, stop=True)
                elif j == 12:
                    mm(bank[:, 0:C], rep[:, 2, :], w1l[:, 3, :], start=True, stop=False)
                    last = mm(bank[:, 0:C], cst[0:1, CONE:CONE + 128], rowb[:, 1, :], start=False, stop=True)
                else:
                    last = mm(bank[:, 0:C], cst[0:1, CONE:CONE + 128], rowb[:, 2, :], start=True, stop=True)
                last.then_inc(f_full[1], 1)

            def projection(it, k):
                until(pe, p_out, p_job(it, k))
                bank = ps[:, PB, :]
                if k == 0:
                    pe.wait_ge(x_in[it.par], 16 * it.half + 16)
                    for n in range(NT):
                        last = tr(bank[:, n * TILE:(n + 1) * TILE], xin[:, it.par, n, :], ident)
                elif it.layer == 0 and k % 3:
                    pair, kind = k // 3, k % 3 - 1
                    for g in range(2):
                        last = mm(bank[:, g * T:(g + 1) * T], WL[:, kind, (2 * pair + g) * C:(2 * pair + g + 1) * C],
                                  xT[:, it.par, :], start=True, stop=True)
                elif it.layer == 0:
                    pair = k // 3 - 1
                    pe.wait_ge(rope_sum, 4 * it.m + 2 * pair + 1)
                    last = mm(bank, BDW[:, :], rq[:, pair * 512:(pair + 1) * 512], start=True, stop=True)
                else:
                    last = mm(bank[:, 0:T], wq1[:, k - 1, :], xT[:, it.par, :], start=True, stop=True)
                last.then_inc(p_full, 1)

            def values(it):
                until(pe, s1_out[1], v_job(it))
                pe.wait_ge(p_out, p_job(it, 0) + 1)
                w = w1l[:, 2, :] if it.layer else wv[:, 0, :]
                for n in range(NT):
                    last = mm(ps[:, S1[1], n * C:(n + 1) * C], xT[:, it.par, n * TILE:(n + 1) * TILE], w,
                              start=True, stop=True)
                last.then_inc(s1_full[1], 1)

            def scores_for_max(it, k):
                b, u, r = k % 2, k // 3, k % 3
                q, kk = QS[it.layer][it.par], KS[it.layer][it.par]
                if k in (0, 6):
                    pe.wait_ge(stacked[k // 6][it.par], stacked_count(it))
                until(pe, s1_out[b], m_job(it, k))
                bank = ps[:, S1[b], :]
                if r == 0:
                    for j in range(4):
                        mm(bank[:, j * TILE:(j + 1) * TILE], q[0:MAXROW, 4 * u + j, 0:TILE],
                           kk[0:MAXROW, 4 * u + j, 0:TILE], start=(j == 0), stop=False)
                    last = mm(bank, identb[:, :], maskb[:, :, :].rearrange("p h t -> p (h t)"), start=False, stop=True)
                else:
                    for j in range(2):
                        h = 4 * u + 2 * (r - 1) + j
                        mm(bank[:, j * T:(j + 1) * T], q[0:MAXROW, h, TILE:T], kk[0:MAXROW, h, :],
                           start=(j == 0), stop=False)
                    last = mm(bank.rearrange("p (h t) -> p h t", h=2)[:, :, TILE:T], identb[:, :], maskb[:, 0:2, :],
                              start=False, stop=True)
                last.then_inc(s1_full[b], 1)

            def transpose_max(it, half):
                pe.wait_ge(nm_part, 2 * it.n + half + 1)
                until(pe, s1_out[0], mt_job(it, half))
                bank = ps[0:MAXROWS, S1[0], :].bitcast(BF16)
                for n in range(NT):
                    last = tr(bank[:, n * TILE:(n + 1) * TILE],
                              nmb[:, it.par, n, half, :, :].rearrange("p a h -> p (a h)"), identb[:, :])
                last.then_inc(s1_full[0], 1)

            def scores_for_exp(it, k):
                b, u, r = k % 2, k // 3, k % 3
                q, kk = QS[it.layer][it.par], KS[it.layer][it.par]
                if k in (0, 6):
                    pe.wait_ge(max_in[k // 6][it.par], 16 * it.half + 16)
                until(pe, exp_done, 12 * it.n + k - 1)
                bank = ps[:, S2[b], :]
                if r < 2:
                    for j in range(2):
                        h = 4 * u + 2 * r + j
                        last = mm(bank[:, j * T:(j + 1) * T], kk[0:STACKED, h, 0:TILE], q[0:STACKED, h, :],
                                  start=True, stop=True)
                else:
                    for j in range(4):
                        h = 4 * u + j
                        last = mm(bank[:, j * TILE:(j + 1) * TILE], kk[0:STACKED, h, TILE:T], q[0:STACKED, h, TILE:T],
                                  start=True, stop=True)
                last.then_inc(s2_full[b], 1)

            def times_values(it, k):
                u, r = k // 3, k % 3
                pe.wait_ge(causal, 12 * it.n + k + 1)
                if k == 0:
                    pe.wait_ge(s1_out[1], v_job(it) + 1)
                if k % 6 == 0:
                    until(pe, o_out, 2 * it.n + k // 6)
                base = (u % 2) * T
                for i in range(2 if r < 2 else 4):
                    j = 2 * r + i if r < 2 else i
                    rows = slice(32 * j, 32 * j + OW)
                    if r < 2:
                        last = mm(ps[rows, OB, base:base + T], vaug[:, it.par, 0, 4 * u + j, :],
                                  prob[:, k % NP, i * T:(i + 1) * T], start=True, stop=False)
                    else:
                        last = mm(ps[rows, OB, base + TILE:base + T], vaug[:, it.par, 1, 4 * u + j, :],
                                  prob[:, k % NP, i * TILE:(i + 1) * TILE], start=False, stop=True)
                last.then_inc(pv_done, 1)

            def f_product(it, k):
                until(pe, f_out[k % 2], f_job(it, k))
                if k in (2, 3, 5, 6, 8) and (it.layer == 0 or k != 8):
                    pe.wait_ge(f_out[(k - 1) % 2], f_job(it, k - 1) + 1)
                if k == 7 and it.layer:
                    pe.wait_ge(f_out[0], f_job(it, 6) + 1)
                bank = ps[:, FB[k % 2], :]
                if k < 2:
                    pe.wait_ge(o_out, 2 * it.n + 2)
                    for u in range(NG):
                        last = tr(bank[:, u * TILE:(u + 1) * TILE], oT[:, u, k * TILE:(k + 1) * TILE], ident)
                elif k == 2:
                    for n in range(NT):
                        last = tr(bank[:, n * TILE:(n + 1) * TILE], on[:, n, :], ident)
                elif k == 3:
                    w = w1l[:, 3, :] if it.layer else wo[:, 0, :]
                    for n in range(NT):
                        last = mm(bank[:, n * C:(n + 1) * C], onT[:, n * TILE:(n + 1) * TILE], w, start=True, stop=True)
                elif k == 4:
                    pe.wait_ge(x1_ready, it.n + 1)
                    for n in range(NT):
                        last = tr(bank[:, n * TILE:(n + 1) * TILE], x1[:, n, :], ident)
                elif it.layer == 0:
                    last = moe(it, k, bank)
                else:
                    last = mlp(k, bank)
                last.then_inc(f_full[k % 2], 1)

            def moe(it, k, bank):
                if k == 5:
                    for n in range(NT):
                        last = mm(bank[:, n * NE:(n + 1) * NE], x1T[:, n * TILE:(n + 1) * TILE], wgate[:, :],
                                  start=True, stop=True)
                elif k == 6:
                    pe.wait_ge(onehot_ready, it.m + 1)
                    for n in range(NT):
                        dst = bank[:, n * NE:(n + 1) * NE]
                        mm(dst, triub[:, :], oh[:, n, :], start=True, stop=False)
                        if n:
                            mm(dst, onesb[:, :], oh[:, 0, :], start=False, stop=False)
                        last = mm(dst, onesb[:, :], seen[:, :], start=False, stop=True)
                elif k == 7:
                    pe.wait_ge(gate_ready, it.m + 1)
                    for n in range(NT):
                        last = tr(ps[0:NE, FB[1], n * TILE:(n + 1) * TILE], gate[:, n, :], ident)
                elif k == 8:
                    for n in range(NT):
                        last = mm(bank[:, n * C:(n + 1) * C], gT[:, n * TILE:(n + 1) * TILE], bexp[:, :],
                                  start=True, stop=True)
                else:
                    n, half = (k - 9) // 2, (k - 9) % 2
                    last = mm(bank, x1T[:, n * TILE:(n + 1) * TILE],
                              wexpT[:, 4 * half:4 * half + 4, :].rearrange("p e c -> p (e c)"), start=True, stop=True)
                return last

            def mlp(k, bank):
                if k in (5, 6):
                    for c in range(2):
                        last = mm(bank[:, c * T:(c + 1) * T], w1T[:, 2 * (k - 5) + c, :], x1T[:, :], start=True, stop=True)
                else:
                    for n in range(NT):
                        for c in range(NF):
                            last = mm(bank[:, n * C:(n + 1) * C], hT[:, c, n * TILE:(n + 1) * TILE], w2T[:, c, :],
                                      start=(c == 0), stop=(c == NF - 1))
                return last

            def slots(st):
                if st.base == FIRST:
                    setup()
                for tick in range(TICKS):
                    for it, k in due(st, tick, PE_F):
                        f_product(it, k)
                    for it, k in due(st, tick, PE_M):
                        scores_for_max(it, k)
                    for it, k in due(st, tick, PE_E):
                        scores_for_exp(it, k)
                    for it, k in due(st, tick, PE_PV):
                        times_values(it, k)
                    for it, k in due(st, tick, PE_P):
                        projection(it, k)
                    if st.base == SETUP_STEP and tick in SETUP_TIMES:
                        setup_f(SETUP_TIMES.index(tick))
                    for it, _ in due(st, tick, PE_V):
                        values(it)
                    for it, half in due(st, tick, PE_MT):
                        transpose_max(it, half)

            walk(pe, slots)

        @block.vector
        def _(dve):
            v = nc.vector

            def setup():
                for p in range(2):
                    dve.sem_inc(xo_stored[p], 16)
                dve.wait_ge(w_in, 16 * NW)
                v.tensor_copy(q2lrep[:, :, :, :],
                              q2l[:, :, :].rearrange("p k (a d) -> p k a d", a=1).broadcast_to([L, 2, NH, HD]))\
                    .then_inc(w_dve, 1)
                v.tensor_copy(wqkrep[:, :, :, :],
                              wqk[:, :].rearrange("p (l a b) -> p a l b", a=2, b=1).broadcast_to([L, 2, L // 2, 4]))\
                    .then_inc(w_dve, 1)
                dve.wait_ge(w_pe, 1)
                shape = [128, 2, L // 2, 4]
                for kind in range(2):
                    src = ps[:, FB[1], L * kind:L * kind + L].rearrange("p (l a b) -> p a l b", a=2, b=1)
                    for g in range(NG):
                        own = hm.rearrange("p (h j b) -> p h j b", h=2, j=4)[:, g // 2, :, g % 2]
                        own = own.rearrange("p (a l j) -> p a l j", a=1, l=1)
                        v.tensor_tensor(BD[:, kind, g, :].rearrange("p (a l b) -> p a l b", a=2, b=4),
                                        src.broadcast_to(shape), own.broadcast_to(shape), ALU.mult).then_inc(w_dve, 1)
                src = ps[:, FB[1], 64:64 + L].rearrange("p (l a b) -> p a l b", a=2, b=1).broadcast_to(shape)
                own = cst[:, CJM:CJM + 4].rearrange("p (a l j) -> p a l j", a=1, l=1).broadcast_to(shape)
                v.tensor_tensor(BDW[:, :].rearrange("p (a l b) -> p a l b", a=2, b=4), src, own, ALU.mult)\
                    .then_inc(w_dve, 1)
                v.tensor_scalar(wqkbc[:, :], ps[:, FB[1], 96:97], float(L) ** -0.5, None, ALU.mult).then_inc(w_dve, 1)
                v.tensor_copy(identb[:, :], ident).then_inc(w_dve, 1)
                v.tensor_copy(triub[:, :], cst[:, CU:CU + 128]).then_inc(w_dve, 1)
                v.tensor_copy(onesb[:, :], ones).then_inc(w_dve, 1)
                v.memset(seen[:, :], 0.0).then_inc(w_dve, 1)
                sel = cst[MAXROW:STACKED, CSEL:CSEL + NH].rearrange("p (h a) -> p h a", a=1).broadcast_to([MAXROWS, NH, T])
                for l in range(2):
                    for p in range(2):
                        v.tensor_copy(KS[l][p][MAXROW:STACKED, :, :], sel).then_inc(w_dve, 1)
                dve.wait_ge(w_pe, 4)
                v.tensor_copy(lb[:, :], ps[:, 4, 0:8]).then_inc(w_dve, 1)
                v.tensor_copy(perm[:, :].rearrange("p (a d b) -> p a d b", a=2, d=HD),
                              ident.rearrange("p (a b d) -> p a d b", a=2, d=HD)).then_inc(w_dve, 1)

            def setup_2():
                dve.wait_ge(w2_in, 16 * NW2)
                v.tensor_copy(rep[:, 0, :], cattnb[:, 2:3].broadcast_to([128, C])).then_inc(w2_dve, 1)
                v.tensor_copy(rep[:, 2, :], b1l[:, 2:3].broadcast_to([128, C])).then_inc(w2_dve, 1)
                v.tensor_reduce(gam[:, 0:1], w1n[:, :], AX.X, ALU.add, apply_absolute_value=True).then_inc(w2_dve, 1)
                v.tensor_reduce(gam[:, 1:2], w2n[:, :], AX.X, ALU.add, apply_absolute_value=True).then_inc(w2_dve, 1)
                for o in range(2):
                    v.tensor_scalar(wq1[:, o, :].rearrange("p (a d b) -> p a d b", a=2, d=HD),
                                    w1l[:, o, :].rearrange("p (a b d) -> p a d b", a=2, d=HD),
                                    (float(HD) ** -0.5, 1.0)[o], None, ALU.mult).then_inc(w2_dve, 1)

            def setup_f(j):
                dve.wait_ge(f_full[1], j + 1)
                bank = ps[:, FB[1], :]
                if j == 0:
                    last = v.tensor_copy(cprojT[:, :], bank[:, 0:C])
                elif j == 1:
                    last = v.tensor_copy(l2orep[:, :, :], ps[0:L, FB[1], 0:HD].rearrange("p (a e) -> p a e", a=1)
                                         .broadcast_to([L, NH, HD]))
                elif j == 2:
                    last = v.tensor_tensor(BDM[:, :].rearrange("p (h d) -> p h d", h=NH),
                                           bank[:, 0:HD].rearrange("p (a d) -> p a d", a=1).broadcast_to([128, NH, HD]),
                                           hm.rearrange("p (h a) -> p h a", a=1).broadcast_to([128, NH, HD]), ALU.mult)
                elif j == 3:
                    last = v.tensor_copy(rep[:, 1, :], bank[:, 0:1].broadcast_to([128, C]))
                elif j == 4:
                    last = v.tensor_copy(wo[:, 0, :], bank[:, 0:C])
                elif j == 5:
                    last = v.tensor_copy(obias[:, 0, :], bank[:, 0:C])
                elif j in (6, 7):
                    last = v.tensor_copy(wexpT[:, 4 * (j - 6):4 * (j - 6) + 4, :].rearrange("p e c -> p (e c)"), bank)
                elif j == 8:
                    last = v.tensor_scalar(gam[:, 2:4], bank[:, 0:2], 1.0 / (NF * C * C), EPS, ALU.mult, ALU.add)
                elif j in (9, 10):
                    last = v.tensor_copy((w1T, w2T)[j - 9][:, :, :].rearrange("p a c -> p (a c)"), bank)
                elif j == 11:
                    v.tensor_scalar(bq1[:, 0:1], bank[:, 0:1], float(HD) ** -0.5, None, ALU.mult)
                    last = v.tensor_copy(bq1[:, 1:2], bank[:, 1:2])
                elif j == 12:
                    last = v.tensor_copy(obias[:, 1, :], bank[:, 0:C])
                else:
                    last = v.tensor_copy(b2row[:, :], bank[:, 0:C])
                last.then_inc(f_out[1], 1)
                if j == 8:
                    dve.wait_ge(f_out[1], 9)
                    v.tensor_scalar(gam[:, 4:6], gam[:, 2:4], 0.5, None, ALU.mult)
                    v.tensor_scalar(gam[:, 6:8], gam[:, 2:4], -0.5, None, ALU.mult).then_inc(w2_dve, 1)
                    dve.wait_ge(w2_dve, 7)
                    for n, w in enumerate((w1n, w2n)):
                        v.tensor_scalar(qtmp[:, n, :], w[:, :], gam[:, 6 + n:7 + n], None, ALU.is_lt).then_inc(w2_dve, 1)
                    dve.wait_ge(w2_dve, 9)
                    for n, w in enumerate((w1n, w2n)):
                        v.scalar_tensor_tensor(out=w[:, :], in0=w[:, :], scalar=gam[:, 4 + n:5 + n],
                                               in1=qtmp[:, n, :], op0=ALU.is_gt, op1=ALU.subtract).then_inc(w2_dve, 1)

            def p_evac(it, k):
                if it.layer == 0 and k % 3:
                    pair, kind = k // 3, k % 3 - 1
                    a = 2 * pair + kind
                    dve.wait_ge(swapped, 4 * it.m + a + 1)
                    until(dve, rope_sum, 4 * it.m + a - 1)
                    for g in range(2):
                        col = kind * NG + 2 * pair + g
                        last = v.scalar_tensor_tensor(out=t1[:, a % 2, g * T:(g + 1) * T],
                                                      in0=ps[:, PB, g * T:(g + 1) * T], scalar=lb[:, col:col + 1],
                                                      in1=cst[:, CCOS:CCOS + T], op0=ALU.add, op1=ALU.mult)
                    last.then_inc(p_out, 1)
                elif it.layer == 0:
                    pair = k // 3 - 1
                    dve.wait_ge(q_high, 2 * it.m + pair + 1)
                    cols = slice(pair * 512, (pair + 1) * 512)
                    v.scalar_tensor_tensor(out=parts[:, it.par, 1, cols], in0=ps[:, PB, :], scalar=wqkbc[:, 0:1],
                                           in1=parts[:, it.par, 0, cols], op0=ALU.add, op1=ALU.subtract)\
                        .then_inc(p_out, 1)
                else:
                    o = k - 1
                    dve.wait_ge(split_a, 2 * it.m + o + 1)
                    until(dve, split_l, 2 * it.m)
                    v.scalar_tensor_tensor(out=rest[:, o, :], in0=ps[:, PB, 0:T], scalar=bq1[:, o:o + 1],
                                           in1=parts1[:, it.par, o, 0, :], op0=ALU.add, op1=ALU.subtract)\
                        .then_inc(p_out, 1)

            def k_parts(it, pair):
                dve.wait_ge(k_high, 2 * it.m + pair + 1)
                cols = slice(pair * 512, (pair + 1) * 512)
                v.tensor_tensor(parts[:, it.par, 3, cols], rk[:, cols], parts[:, it.par, 2, cols], ALU.subtract)\
                    .then_inc(k_low, 1)

            def split_low(it):
                for o in range(2):
                    dve.wait_ge(split_m, 2 * it.m + o + 1)
                    v.tensor_tensor(parts1[:, it.par, o, 2, :], rest[:, o, :], parts1[:, it.par, o, 1, :], ALU.subtract)\
                        .then_inc(split_l, 1)

            def row_max(it, k):
                b, u, r = k % 2, k // 3, k % 3
                dve.wait_ge(s1_full[b], m_job(it, k) + 1)
                if r == 0:
                    v.tensor_reduce(nm[:, it.par, 0, 4 * u:4 * u + 4], ps[:, S1[b], :].rearrange("p (h t) -> p h t", h=4),
                                    AX.X, ALU.max, negate=True).then_inc(s1_out[b], 1)
                else:
                    h = 4 * u + 2 * (r - 1)
                    v.tensor_reduce(nm[:, it.par, 1, h:h + 2], ps[:, S1[b], :].rearrange("p (h t) -> p h t", h=2),
                                    AX.X, ALU.max, negate=True).then_inc(s1_out[b], 1)

            def max_parts(it, half):
                src = nm[:, it.par, :, 8 * half:8 * half + 8]
                dve.wait_ge(s1_out[1], m_job(it, 6 * half + 5) + 1)
                dve.wait_ge(s1_out[0], m_job(it, 6 * half + 4) + 1)
                v.tensor_copy(nmb[:, it.par, :, half, 0, :], src).then_inc(nm_high, 1)
                dve.wait_ge(nm_high, 2 * it.n + half + 1)
                v.tensor_tensor(nmb[:, it.par, :, half, 1, :], src, nmb[:, it.par, :, half, 0, :], ALU.subtract)\
                    .then_inc(nm_part, 1)

            def max_evac(it, half):
                dve.wait_ge(s1_full[0], mt_job(it, half) + 1)
                v.tensor_copy(mT[:, it.par, half, :], ps[0:MAXROWS, S1[0], :].bitcast(BF16)[:, 0:T]).then_inc(s1_out[0], 1)

            def f_chain(it, start):
                count = [start]

                def link(ins):
                    count[0] += 1
                    ins.then_inc(f_dve, 1)
                    dve.wait_ge(f_dve, count[0])
                return link

            def statistics(src, link):
                for n in range(NT):
                    link(v.bn_stats(stats[:, n, :], src[:, n, :]))
                dve.sem_inc(stats_seen, 1)
                v.bn_aggr(mv[:, 0, :], stats[:, 0, :])
                link(v.bn_aggr(mv[:, 1, :], stats[:, 1, :]))
                v.tensor_scalar(ve[:, :], mv[:, :, 1], EPS, None, ALU.add).then_inc(var_ready, 1)

            def normalise(it, which):
                dve.wait_ge(rstd_done, 2 * it.n + which + 1)
                src = y if which == 0 or it.layer else acc
                if which == 0:
                    dst, signal = x1, x1_ready
                else:
                    dst, signal = xo[:, it.par, :, :], xo_ready
                    dve.wait_ge(xo_stored[it.par], 16 * it.half + 16)
                for n in range(NT):
                    last = v.tensor_scalar(dst[:, n, :], src[:, n, :], mv[:, n, 0:1], rstd[:, n:n + 1],
                                           ALU.subtract, ALU.mult)
                last.then_inc(signal, 1)

            def f_step(it, k):
                bank = ps[:, FB[k % 2], :]
                if k in (0, 1, 3) or (it.layer == 0 and k in (5, 6, 8, 9, 10, 11, 12)) or (it.layer == 1 and k == 7):
                    dve.wait_ge(f_full[k % 2], f_job(it, k) + 1)
                if k < 2:
                    link = f_chain(it, k)
                    heads = bank.rearrange("p (h w) -> p h w", w=OW)
                    link(v.reciprocal(rden[:, k, :], heads[:, :, HD]))
                    v.tensor_tensor(on[:, k, :].rearrange("p (h d) -> p h d", d=HD), heads[:, :, 0:HD],
                                    rden[:, k, :].rearrange("p (h a) -> p h a", a=1).broadcast_to([128, NH, HD]), ALU.mult)\
                        .then_inc(f_out[k % 2], 1)
                elif k == 3:
                    dve.wait_ge(xr_done, it.n + 1)
                    v.tensor_tensor(y[:, :, :].rearrange("p n c -> p (n c)"), bank[:, 0:T],
                                    xr[:, :, :].rearrange("p n c -> p (n c)"), ALU.add).then_inc(f_out[k % 2], 1)
                    dve.wait_ge(f_out[k % 2], f_job(it, 3) + 1)
                    statistics(y, f_chain(it, 2))
                elif it.layer == 0:
                    moe_step(it, k, bank)
                elif k == 4:
                    dve.wait_ge(x1_ready, it.n + 1)
                    link = f_chain(it, 5)
                    link(v.tensor_tensor(acc[:, :, :], x1[:, :, :],
                                         b2row[:, :].rearrange("p (a c) -> p a c", a=1).broadcast_to([128, NT, C]), ALU.add))
                elif k == 7:
                    v.tensor_tensor(y[:, :, :].rearrange("p n c -> p (n c)"), bank[:, 0:T],
                                    acc[:, :, :].rearrange("p n c -> p (n c)"), ALU.add).then_inc(f_out[k % 2], 1)
                    dve.wait_ge(f_out[k % 2], f_job(it, 7) + 1)
                    statistics(y, f_chain(it, 6))
                    dve.sem_clear(f_dve)

            def moe_step(it, k, bank):
                two = [128, NT, NE]

                def wide(ap):
                    return ap.rearrange("p (n a) -> p n a", a=1).broadcast_to(two)

                if k == 5:
                    logits = bank[:, 0:NT * NE].rearrange("p (n e) -> p n e", e=NE)
                    link = f_chain(it, 5)
                    link(v.tensor_reduce(lmax[:, :], logits, AX.X, ALU.max))
                    v.tensor_tensor(lsh[:, :, :], logits, wide(lmax[:, :]), ALU.subtract).then_inc(f_out[k % 2], 1)
                    dve.wait_ge(lexp_done, it.m + 1)
                    link(v.tensor_reduce(lsum[:, :], lex[:, :, :], AX.X, ALU.add))
                    link(v.reciprocal(lrec[:, :], lsum[:, :]))
                    link(v.tensor_tensor(pr[:, :, :], lex[:, :, :], wide(lrec[:, :]), ALU.mult))
                    link(v.tensor_reduce(pmax[:, :], pr[:, :, :], AX.X, ALU.max))
                    link(v.tensor_tensor(peq[:, :, :], pr[:, :, :], wide(pmax[:, :]), ALU.is_equal))
                    order = cst[:, CW:CW + NE].rearrange("p (a e) -> p a e", a=1).broadcast_to(two)
                    link(v.tensor_tensor(pk[:, :, :], peq[:, :, :], order, ALU.mult))
                    link(v.tensor_reduce(pkm[:, :], pk[:, :, :], AX.X, ALU.max))
                    v.tensor_tensor(oh[:, :, :], pk[:, :, :], wide(pkm[:, :]), ALU.is_equal).then_inc(onehot_ready, 1)
                elif k == 6:
                    link = f_chain(it, 13)
                    before = bank[:, 0:NT * NE].rearrange("p (n e) -> p n e", e=NE)
                    v.scalar_tensor_tensor(out=kept[:, :, :], in0=before, scalar=float(CAP), in1=oh[:, :, :],
                                           op0=ALU.is_lt, op1=ALU.mult).then_inc(f_out[k % 2], 1)
                    dve.wait_ge(f_out[k % 2], f_job(it, 6) + 1)
                    v.tensor_tensor(gate[:, :, :], kept[:, :, :], wide(pmax[:, :]), ALU.mult).then_inc(gate_ready, 1)
                    link(v.tensor_tensor(ohs[:, :], oh[:, 0, :], oh[:, 1, :], ALU.add))
                    link(v.tensor_tensor(seen[:, :], seen[:, :], ohs[:, :], ALU.add))
                elif k == 8:
                    dve.wait_ge(x1_ready, it.n + 1)
                    v.tensor_tensor(acc[:, :, :].rearrange("p n c -> p (n c)"), bank[:, 0:T],
                                    x1[:, :, :].rearrange("p n c -> p (n c)"), ALU.add).then_inc(f_out[k % 2], 1)
                    dve.wait_ge(f_out[k % 2], f_job(it, 8) + 1)
                elif k >= 9:
                    n, half = (k - 9) // 2, (k - 9) % 2
                    link = f_chain(it, 15 + 3 * (k - 9))
                    for e in range(4):
                        ins = v.scalar_tensor_tensor(out=acc[:, n, :], in0=bank[:, e * C:(e + 1) * C],
                                                     scalar=gate[:, n, 4 * half + e:4 * half + e + 1], in1=acc[:, n, :],
                                                     op0=ALU.mult, op1=ALU.add)
                        if e < 3:
                            link(ins)
                    ins.then_inc(f_out[k % 2], 1)
                    dve.wait_ge(f_out[k % 2], f_job(it, k) + 1)
                    if k == 12:
                        statistics(acc, f_chain(it, 27))
                        dve.sem_clear(f_dve)

            def slots(st):
                if st.base == FIRST:
                    setup()
                if st.base == SETUP_STEP:
                    setup_2()
                for tick in range(TICKS):
                    for it, which in due(st, tick, DVE_NORM):
                        normalise(it, which)
                    for it, k in due(st, tick, DVE_F):
                        f_step(it, k)
                    for it, k in due(st, tick, DVE_M):
                        row_max(it, k)
                    for it, half in due(st, tick, DVE_PARTS):
                        max_parts(it, half)
                    for it, k in due(st, tick, DVE_P):
                        p_evac(it, k)
                    for it, pair in due(st, tick, DVE_K):
                        k_parts(it, pair)
                    for it, _ in due(st, tick, DVE_SPLIT):
                        split_low(it)
                    if st.base == SETUP_STEP and tick in SETUP_TIMES:
                        setup_f(SETUP_TIMES.index(tick))
                    for it, half in due(st, tick, DVE_MT):
                        max_evac(it, half)

            walk(dve, slots)


_W = (("c_attn_w", "L0_attn_c_attn_w"), ("c_attn_b", "L0_attn_c_attn_b"), ("q2l_w", "L0_attn_q2l_w"),
      ("q2l_b", "L0_attn_q2l_b"), ("kv2l_w", "L0_attn_kv2l_w"), ("kv2l_b", "L0_attn_kv2l_b"),
      ("l2o_w", "L0_attn_l2o_w"), ("l2o_b", "L0_attn_l2o_b"), ("wqk_w", "L0_attn_wqk_w"),
      ("wqk_b", "L0_attn_wqk_b"), ("cproj_w", "L0_attn_cproj_w"), ("cproj_b", "L0_attn_cproj_b"),
      ("wg", "L0_ffn_wg"), ("W", "L0_ffn_W"), ("b", "L0_ffn_b"), ("Wq", "L1_attn_Wq"), ("bq", "L1_attn_bq"),
      ("Wk", "L1_attn_Wk"), ("bk", "L1_attn_bk"), ("Wv", "L1_attn_Wv"), ("bv", "L1_attn_bv"),
      ("Wo", "L1_attn_Wo"), ("bo", "L1_attn_bo"), ("W1", "L1_ffn_W1"), ("b1", "L1_ffn_b1"),
      ("W2", "L1_ffn_W2"), ("b2", "L1_ffn_b2"))


def kernel(**inputs):
    import numpy as np
    import concourse.bacc as bacc
    from concourse.bass_utils import run_bass_kernel_spmd

    nc = bacc.Bacc("TRN2", target_bir_lowering=False, num_devices=1)
    arrays = {}

    def dram(name, a):
        a = np.ascontiguousarray(a)
        arrays[name] = a
        return nc.dram_tensor(name, a.shape, mybir.dt.from_np(a.dtype), kind="ExternalInput").ap()

    x = dram("x", inputs["L0_attn_x"])
    c = dram("shape_constants", constants())
    w = {short: dram(long, inputs[long]) for short, long in _W}
    out = nc.dram_tensor("out", (NB, T, C), F32, kind="ExternalOutput").ap()
    build(nc, x, c, w, out)
    r = run_bass_kernel_spmd(nc, [arrays], core_ids=[0])
    return r.results[0]["out"]
```

```python
from contextlib import ExitStack

import concourse.bass as bass
from concourse import mybir

F32 = mybir.dt.float32
BF16 = mybir.dt.bfloat16
ALU = mybir.AluOpType
ACT = mybir.ActivationFunctionType
AX = mybir.AxisListType

C = 128
T = 256
TILE = 128
NT = T // TILE
NB = 8
NH = 16
HD = C // NH
L = 32
NG = 4
NE = 8
CAP = NB * T // NE
NF = 4
EPS = 1e-5
MASKED = -1.0e30
MAXROW = 96
MAXROWS = 16
STACKED = MAXROW + MAXROWS
OW = 32
NP = 8

ITEMS = 2 * NB

S1 = (0, 1)
S2 = (2, 3)
PB = 4
OB = 6
FB = (5, 7)

CI = 0
CCOS = CI + 128
CSIN = CCOS + T
CHM = CSIN + T
CJM = CHM + NH
CJ = CJM + 4
CE = CJ + 4
CE8 = CE + C
CSEL = CE8 + C
CU = CSEL + NH
CW = CU + 128
CONE = CW + NE
NC = CONE + 128


def constants():
    import numpy as np
    c = np.zeros((128, NC), np.float32)
    c[:, CI:CI + 128] = np.eye(128)
    inv = (np.float32(1.0) / np.power(np.float32(10000.0), np.arange(0, L, 2, dtype=np.float32) / np.float32(L)))
    fr = np.outer(np.arange(T, dtype=np.float32), inv.astype(np.float32)).astype(np.float32)
    p = np.arange(128)
    lat, j = 2 * (p % 64 // 4) + p // 64, p % 4
    c[:, CCOS:CCOS + T] = np.cos(fr)[:, lat // 2].T
    c[:, CSIN:CSIN + T] = np.sin(fr)[:, lat // 2].T * np.where(p < 64, -1.0, 1.0)[:, None]
    c[p, CHM + p // HD] = 1.0
    c[p, CJM + j] = float(L) ** -0.5
    c[p, CJ + j] = 1.0
    c[lat, CE + p] = 1.0
    c[p % HD, CE8 + p] = 1.0
    r = np.arange(MAXROWS)
    for s in range(NH):
        c[MAXROW + r[r % 8 == s % 8], CSEL + s] = 1.0
    c[:, CU:CU + 128] = np.triu(np.ones((128, 128)), 1)
    c[:, CW:CW + NE] = np.arange(NE, 0, -1)
    c[:, CONE:CONE + 128] = 1.0
    return c


class Item:

    def __init__(self, b, i=0):
        self.b, self.i = b, i
        self.n, self.half, self.par = b + 2 * i, b // 2 + i, b % 2
        self.layer = int(b >= NB)
        self.m = self.n - NB if self.layer else self.n
        self.real = 0 <= b < ITEMS

    def before(self, d):
        it = Item(self.b - d, self.i)
        assert isinstance(self.i, int) or (it.real and it.layer == self.layer)
        return it


class Step:

    def __init__(self, base, i=0):
        self.base, self.i = base, i

    def item(self, d):
        return Item(self.base + d, self.i)


FIRST, LAST = -1, ITEMS + 1
LOOPS = {2: 2, 10: 2}


def walk(eng, step):
    s = FIRST
    while s <= LAST:
        if s in LOOPS:
            with eng.Fori(0, LOOPS[s]) as i:
                for off in range(2):
                    step(Step(s + off, i))
            s += 2 * LOOPS[s]
        else:
            step(Step(s))
            s += 1


PJOBS = (5, 3)


def p_job(it, k):
    return PJOBS[it.layer] * it.m + (PJOBS[0] * NB if it.layer else 0) + k


FJOBS = (13, 8)
SETUP_F = (0, 14)


def f_job(it, k):
    per = [(j + 1 - k % 2) // 2 for j in FJOBS]
    return per[it.layer] * it.m + (per[0] * NB if it.layer else 0) + SETUP_F[k % 2] + k // 2


def bank1(it):
    if it.layer == 0:
        return 3 + 9 * it.n
    return 3 + 9 * NB - 2 + 7 * it.m


def m_job(it, k):
    if k % 2 == 0:
        return 8 * it.n + k // 2 + (k // 2 >= 3)
    beside = it.layer == 0 and not (isinstance(it.n, int) and it.n == NB - 1)
    return bank1(it) + k // 2 + (((k >= 5) + (k >= 11)) if beside else 0)


def e_job(it, k):
    return 6 * it.n + k // 2


def mt_job(it, half):
    return 8 * it.n + 3 + 4 * half


def v_job(it):
    return bank1(it) - 1


def w_job(it, pair):
    if isinstance(it.n, int) and it.n == 0:
        return pair
    return bank1(it) - 9 + (2, 6)[pair]


TICKS = 48


def every(first, gap=4, count=12):
    return [first + gap * k for k in range(count)]


PE_P = ([-48, -45, -39, -25, -17], [-50, -48, -40])
ACT_P = ([-47, -45, -38, -25, -17], [-49, -47, -39])
DVE_P = ([None, -43, -32, -24, -13], [None, -43, -32])
PE_W = ([-31, -8], [])
ACT_W = ([-30, -7], [])
DVE_W = ([-31, -8], [])
POOL_MUL = ([-42, -32, -17, -10], [])
POOL_ADD = ([-42, -26, -17, -10], [])
ACT_K = ([-21, -7], [])
DVE_K = ([-19, 2], [])
ACT_SPLIT = ([], [-28])
DVE_SPLIT = ([], [-24])
PE_V = ([-1], [-2])
ACT_V = ([2], [0])
PE_M = ([1, 5, 9, 13, 17, 21, 25, 27, 33, 37, 41, 44], [1, 6, 9, 12, 17, 19, 26, 29, 33, 35, 41, 45])
DVE_M = ([1, 5, 9, 12, 15, 21, 24, 29, 33, 37, 41, 45], [2, 5, 8, 13, 17, 21, 25, 26, 35, 37, 41, 45])
DVE_PARTS = ([21, 46], [21, 46])
PE_MT = ([23, 47], [23, 47])
DVE_MT = ([23, 47], [23, 47])
PE_E = ([35, 38, 43, 47, 50, 54, 59, 62, 67, 71, 74, 79], [33, 39, 41, 45, 49, 55, 57, 60, 65, 71, 73, 76])
ACT_E = ([37, 41, 45, 49, 53, 56, 63, 65, 69, 73, 79, 81], [35, 40, 43, 48, 52, 56, 60, 62, 68, 72, 77, 80])
POOL_E = ([39, 43, 46, 51, 55, 58, 63, 66, 71, 77, 78, 85], [38, 43, 46, 50, 54, 58, 64, 66, 70, 74, 75, 82])
PE_PV = ([45, 49, 53, 57, 61, 65, 69, 73, 77, 81, 87, 89], [43, 48, 53, 56, 60, 62, 68, 74, 76, 80, 84, 88])
ACT_O = ([70, 92], [62, 83])
PE_F = ([91, 95, 100, 104, 113, 115, 119, 121, 126, 127, 128, 134, 135], [93, 94, 99, 103, 115, 118, 122, 128])
ACT_F = ([90, 97, 100, 104, 110, 115, 117, 123, 126, 127, 131, 132, 136], [89, 96, 97, 103, 115, 119, 123, 132])
DVE_F = ([90, 95, 97, 103, 106, 115, 119, 122, 125, 127, 129, 135, 136], [90, 95, 97, 104, 112, 114, 130, 131])
POOL_POW = ([102, 141], [111, 138])
DVE_NORM = ([106, 140], [110, 138])
POOL_XR = ([86], [95])
SP_MAX = ([3, 36], [15, 36])
SP_STACK = ([-24, -1], [-28, -8])
SP_X = ([-96], [-88])
SP_XF = ([65], [56])
SP_STORE = ([124], [130])
SELECTOR_TIMES = [8, 18, 26, 36]
SETUP_TIMES = [0, 1, 3, 5, 7, 9, 13, 22, 23, 26, 33, 38, 43, 46]


def due(st, tick, times):
    for layer in range(2):
        for k, t in enumerate(times[layer]):
            if t is not None and t % TICKS == tick:
                it = st.item(-(t // TICKS))
                if it.real and it.layer == layer:
                    yield it, k


TERMS = (((0, 0), (0, 1), (1, 0)),
         ((0, 0), (0, 1), (1, 0), (0, 2), (2, 0), (1, 1)))


def stacked_count(it):
    per = [2 * 16 * len(t) for t in TERMS]
    return per[0] * NB // 2 + per[1] * (it.half - NB // 2 + 1) if it.layer else per[0] * (it.half + 1)


LB_DVE = 24
W_DVE = 26
POOL_SETUP = 11
SETUP_STEP = 0


def until(eng, sem, count):
    if isinstance(count, int) and count <= 0:
        return
    eng.wait_ge(sem, count)


def build(nc, x, cst_d, W, out):
    x2d = nc.dram_tensor("x2_scratch", (NB * T, C), F32, kind="Internal").ap()
    xr_d = x.rearrange("b (n p) c -> b p n c", p=TILE)
    x2_d = x2d.rearrange("(b n p) c -> b p n c", b=NB, p=TILE)
    out_d = out.rearrange("b (n p) c -> b p n c", p=TILE)

    with ExitStack() as ctx:
        def sb(name, shape, dt=F32):
            return ctx.enter_context(nc.sbuf_tensor(name, shape, dt))

        def sem(name):
            return ctx.enter_context(nc.semaphore(name))

        ps = ctx.enter_context(nc.psum_tensor("ps", [128, 8, 512], F32))

        cst = sb("cst", [128, NC])
        cattn = sb("cattn", [128, 3, C])
        cproj = sb("cproj", [128, C])
        q2l = sb("q2l", [L, 2, HD])
        wqk = sb("wqk", [L, L])
        l2o = sb("l2o", [HD, L])
        lbias = sb("lbias", [L, 3])
        l2ob = sb("l2ob", [HD, 1])
        cattnb = sb("cattnb", [128, 3])
        rowb = sb("rowb", [1, 3, C])
        wgate = sb("wgate", [128, NE])
        wexp = sb("wexp", [128, NE, C])
        bexp = sb("bexp", [NE, C])
        w1l = sb("w1l", [128, 4, C])
        b1l = sb("b1l", [128, 3])
        w1n = sb("w1n", [128, NF * C])
        w2n = sb("w2n", [128, NF * C])
        b1h = sb("b1h", [128, NF])
        identb = sb("identb", [128, 128], BF16)
        maskb = sb("maskb", [128, 4, 128], BF16)
        triub = sb("triub", [128, 128], BF16)
        onesb = sb("onesb", [128, 128], BF16)
        neghalf = sb("neghalf", [128, 2])
        q2lrep = sb("q2lrep", [L, 2, NH, HD])
        wqkrep = sb("wqkrep", [L, 2, L // 2, 4])
        l2orep = sb("l2orep", [L, NH, HD])
        WL = sb("WL", [128, 2, NG * C])
        BDW = sb("BDW", [128, C])
        BDM = sb("BDM", [128, C])
        perm = sb("perm", [128, C])
        cprojT = sb("cprojT", [128, C])
        wv = sb("wv", [128, 2, C])
        wo = sb("wo", [128, 2, C])
        obias = sb("obias", [128, 2, C])
        qall = sb("qall", [128, 2, C])
        ball = sb("ball", [128, 2, NH])
        lball = sb("lball", [L, 2, NH])
        bsel = sb("bsel", [128, 2, NG, 4])
        lb = sb("lb", [128, 8])
        wqkbc = sb("wqkbc", [128, 1])
        ybc = sb("ybc", [128, 1])
        rep = sb("rep", [128, 3, C])
        wexpT = sb("wexpT", [128, NE, C])
        wq1 = sb("wq1", [128, 2, C])
        bq1 = sb("bq1", [128, 2])
        w1T = sb("w1T", [128, NF, C])
        w2T = sb("w2T", [128, NF, C])
        b2row = sb("b2row", [128, C])
        gam = sb("gam", [128, 8])
        xin = sb("xin", [128, 2, NT, C])
        xT = sb("xT", [128, 2, T])
        t1 = sb("t1", [128, 2, 2 * T])
        tb = sb("tb", [128, 2, 2 * T])
        t2 = sb("t2", [128, 2, 2 * T])
        rq = sb("rq", [128, NG * T])
        rk = sb("rk", [128, NG * T])
        parts = sb("parts", [128, 2, 4, NG * T], BF16)
        rest = sb("rest", [128, 2, T])
        parts1 = sb("parts1", [128, 2, 2, 3, T], BF16)
        QS = [[sb(f"QS{l}{p}", [128, NH, T], BF16) for p in range(2)] for l in range(2)]
        KS = [[sb(f"KS{l}{p}", [128, NH, T], BF16) for p in range(2)] for l in range(2)]
        nm = sb("nm", [128, 2, NT, NH])
        nmb = sb("nmb", [128, 2, NT, 2, 2, 8], BF16)
        mT = sb("mT", [MAXROWS, 2, 2, T], BF16)
        vaug = sb("vaug", [128, 2, NT, NH, OW])
        prob = sb("prob", [128, NP, 512])
        BD = prob[:, 0:2, :].rearrange("p k (g c) -> p k g c", g=NG)
        oT = sb("oT", [128, NG, T])
        rden = sb("rden", [128, NT, NH])
        on = sb("on", [128, NT, C])
        onT = sb("onT", [128, T])
        xf = sb("xf", [128, 2, NT, C])
        xr = sb("xr", [128, NT, C])
        y = sb("y", [128, NT, C])
        stats = sb("stats", [128, NT, 6])
        mv = sb("mv", [128, NT, 2])
        ve = sb("ve", [128, NT])
        rstd = sb("rstd", [128, NT])
        x1 = sb("x1", [128, NT, C])
        x1T = sb("x1T", [128, T])
        lmax = sb("lmax", [128, NT])
        lsh = sb("lsh", [128, NT, NE])
        lex = sb("lex", [128, NT, NE])
        lsum = sb("lsum", [128, NT])
        lrec = sb("lrec", [128, NT])
        pr = sb("pr", [128, NT, NE])
        pmax = sb("pmax", [128, NT])
        peq = sb("peq", [128, NT, NE])
        pk = sb("pk", [128, NT, NE])
        pkm = sb("pkm", [128, NT])
        oh = sb("oh", [128, NT, NE], BF16)
        seen = sb("seen", [128, NE], BF16)
        ohs = sb("ohs", [128, NE], BF16)
        kept = sb("kept", [128, NT, NE])
        gate = sb("gate", [128, NT, NE])
        gT = sb("gT", [NE, T])
        acc = sb("acc", [128, NT, C])
        hT = sb("hT", [128, NF, T])
        qtmp = hT.rearrange("p (k a) t -> p k (a t)", k=2)
        xo = sb("xo", [128, 2, NT, C])

        w_in = sem("w_in")
        w2_in = sem("w2_in")
        w_pool = sem("w_pool")
        w_pe = sem("w_pe")
        w_dve = sem("w_dve")
        w_act = sem("w_act")
        x_in = [sem(f"x_in{p}") for p in range(2)]
        xf_in = [sem(f"xf_in{p}") for p in range(2)]
        xo_stored = [sem(f"xo_stored{p}") for p in range(2)]
        p_full = sem("p_full")
        p_out = sem("p_out")
        swapped = sem("swapped")
        rope_mul = sem("rope_mul")
        rope_sum = sem("rope_sum")
        q_high = sem("q_high")
        k_high = sem("k_high")
        k_low = sem("k_low")
        split_a = sem("split_a")
        split_m = sem("split_m")
        split_l = sem("split_l")
        stacked = [[sem(f"stacked{h}{p}") for p in range(2)] for h in range(2)]
        s1_full = [sem(f"s1_full{b}") for b in range(2)]
        s1_out = [sem(f"s1_out{b}") for b in range(2)]
        nm_part = sem("nm_part")
        max_in = [[sem(f"max_in{h}{p}") for p in range(2)] for h in range(2)]
        s2_full = [sem(f"s2_full{b}") for b in range(2)]
        exp_done = sem("exp_done")
        clear_begun = sem("clear_begun")
        stats_seen = sem("stats_seen")
        causal = sem("causal")
        pv_done = sem("pv_done")
        o_out = sem("o_out")
        f_full = [sem(f"f_full{b}") for b in range(2)]
        f_out = [sem(f"f_out{b}") for b in range(2)]
        f_dve = sem("f_dve")
        var_ready = sem("var_ready")
        nm_high = sem("nm_high")
        w2_dve = sem("w2_dve")
        onehot_ready = sem("onehot_ready")
        gate_ready = sem("gate_ready")
        x1_ready = sem("x1_ready")
        xo_ready = sem("xo_ready")
        xr_done = sem("xr_done")
        rstd_done = sem("rstd_done")
        lexp_done = sem("lexp_done")

        block = ctx.enter_context(nc.Block())

        ident = cst[:, CI:CI + 128]
        hm = cst[:, CHM:CHM + NH]
        ones = cst[:, CONE:CONE + 128]

        NW, NW2 = 11, 22

        @block.sync
        def _(sp):
            def load(dst, src, s):
                sp.dma_start(dst, src).then_inc(s, 16)

            load(cst[:, :], cst_d, w_in)
            load(cattn[:, :, :], W["c_attn_w"].rearrange("(a p) c -> p a c", p=128), w_in)
            for n in range(3):
                load(cattnb[:, n:n + 1], W["c_attn_b"][n * C:(n + 1) * C].rearrange("(p a) -> p a", a=1), w_in)

            def other_weights():
                load(cproj[:, :], W["cproj_w"], w2_in)
                load(l2o[:, :], W["l2o_w"], w2_in)
                load(l2ob[:, :], W["l2o_b"].rearrange("(p a) -> p a", a=1), w2_in)
                load(rowb[:, 0, :], W["cproj_b"].rearrange("(a p) -> a p", a=1), w2_in)
                load(rowb[:, 1, :], W["bo"].rearrange("(a p) -> a p", a=1), w2_in)
                load(rowb[:, 2, :], W["b2"].rearrange("(a p) -> a p", a=1), w2_in)
                load(wgate[:, :], W["wg"], w2_in)
                load(wexp[:, :, :], W["W"].rearrange("e f h -> f e h"), w2_in)
                load(bexp[:, :], W["b"], w2_in)
                for n, name in enumerate(("Wq", "Wk", "Wv", "Wo")):
                    load(w1l[:, n, :], W[name], w2_in)
                for n, name in enumerate(("bq", "bk", "bv")):
                    load(b1l[:, n:n + 1], W[name].rearrange("(p a) -> p a", a=1), w2_in)
                load(w1n[:, :].rearrange("p (a c) -> p a c", a=NF), W["W1"].rearrange("(a p) c -> p a c", p=128), w2_in)
                load(w2n[:, :], W["W2"], w2_in)
                for n in range(NF):
                    load(b1h[:, n:n + 1], W["b1"][n * C:(n + 1) * C].rearrange("(p a) -> p a", a=1), w2_in)

            def value(v):
                return v if isinstance(v, int) else sp.snap(v)

            def load_x(it):
                row, mine = value(it.m), value(16 * (it.half - NB // 2) + 32)
                if it.before(2).real:
                    read = value(p_job(it.before(2), 0) + 1)
                    sp.wait_ge(p_full, read)
                if it.layer:
                    sp.wait_ge(xo_stored[it.par], mine)
                src = x2_d if it.layer else xr_d
                sp.dma_start(xin[:, it.par, :, :], src[row]).then_inc(x_in[it.par], 16)

            def load_xf(it):
                row = value(it.m)
                until(sp, xr_done, it.n)
                src = x2_d if it.layer else xr_d
                sp.dma_start(xf[:, it.par, :, :], src[row]).then_inc(xf_in[it.par], 16)

            def stack(it, half):
                rows = slice(64 * half, 64 * half + 64)
                heads = slice(8 * half, 8 * half + 8)
                read = value(e_job(it.before(2), 6 * half + 5) + 1)
                ready = value(2 * it.m + (2 if it.layer else half + 1))
                if it.before(2).real and half == 0:
                    sp.wait_ge(s2_full[1], read)
                done = stacked[half][it.par]
                if it.layer == 0:
                    sp.wait_ge(k_low, ready)
                    for r, (qp, kp) in enumerate(TERMS[0]):
                        for dst, part in ((QS[0], qp), (KS[0], 2 + kp)):
                            sp.dma_start(dst[it.par][L * r:L * r + L, heads, :],
                                         parts[:, it.par, part, 512 * half:512 * half + 512]).then_inc(done, 16)
                else:
                    sp.wait_ge(split_l, ready)
                    sp.wait_ge(w_pool, POOL_SETUP)
                    for r, (qp, kp) in enumerate(TERMS[1]):
                        for o, dst, part in ((0, QS[1], qp), (1, KS[1], kp)):
                            sp.dma_start(dst[it.par][HD * r:HD * r + HD, heads, :],
                                         parts1[rows, it.par, o, part, :]).then_inc(done, 16)

            def max_rows(it, half):
                sp.wait_ge(s1_out[0], mt_job(it, half) + 1)
                src = mT[:, it.par, half:half + 1, :].broadcast_to([MAXROWS, 8, T])
                sp.dma_start(QS[it.layer][it.par][MAXROW:STACKED, 8 * half:8 * half + 8, :], src)\
                    .then_inc(max_in[half][it.par], 16)

            def store(it):
                row, ready = value(it.m), value(it.n + 1)
                sp.wait_ge(xo_ready, ready)
                if it.layer == 0:
                    sp.dma_start(x2_d[row], xo[:, it.par, :, :]).then_inc(xo_stored[it.par], 16)
                else:
                    sp.dma_start(out_d[row], xo[:, it.par, :, :]).then_inc(xo_stored[it.par], 16)

            def step(st):
                for tick in range(TICKS):
                    for it, half in due(st, tick, SP_MAX):
                        max_rows(it, half)
                    for it, half in due(st, tick, SP_STACK):
                        stack(it, half)
                    for it, _ in due(st, tick, SP_X):
                        load_x(it)
                    for it, _ in due(st, tick, SP_XF):
                        load_xf(it)
                    for it, _ in due(st, tick, SP_STORE):
                        store(it)

            load_x(Item(0))
            other_weights()
            walk(sp, step)
            for p in range(2):
                sp.wait_ge(xo_stored[p], 16 * ITEMS // 2 + 16)

        @block.gpsimd
        def _(pool):
            g = nc.gpsimd
            g.memset(neghalf[:, :], -0.5).then_inc(w_pool, 1)
            g.memset(maskb[:, :, :], 0.0).then_inc(w_pool, 1)
            for p in range(2):
                g.memset(vaug[:, p, :, :, :], 0.0).then_inc(w_pool, 1)
            pool.wait_ge(w_pool, 4)
            g.affine_select(out=maskb[:, :, :], in_=maskb[:, :, :], compare_op=ALU.is_ge, fill=MASKED, base=0,
                            pattern=[[0, 4], [-1, 128]], channel_multiplier=1).then_inc(w_pool, 1)
            for p in range(2):
                g.memset(vaug[:, p, :, :, HD:HD + 1], 1.0).then_inc(w_pool, 1)
            for p in range(2):
                g.memset(QS[1][p][0:MAXROW, :, :], 0.0).then_inc(w_pool, 1)
                g.memset(KS[1][p][0:MAXROW, :, :], 0.0).then_inc(w_pool, 1)
            pool.wait_ge(w_in, 16 * NW)

            def rope_product(it, a):
                pool.wait_ge(swapped, 4 * it.m + a + 1)
                until(pool, rope_sum, 4 * it.m + a - 1)
                sin = cst[:, CSIN:CSIN + T].rearrange("p (a t) -> p a t", a=1).broadcast_to([128, 2, T])
                g.tensor_tensor(t2[:, a % 2, :].rearrange("p (a t) -> p a t", a=2),
                                tb[:, a % 2, :].rearrange("p (a t) -> p a t", a=2), sin, ALU.mult).then_inc(rope_mul, 1)

            def rope_total(it, a):
                pair, kind = a // 2, a % 2
                pool.wait_ge(p_out, p_job(it, 1 + a) + 1)
                pool.wait_ge(rope_mul, 4 * it.m + a + 1)
                if kind == 0 and it.before(1).real:
                    pool.wait_ge(s1_full[1], w_job(it.before(1), pair) + 1)
                if kind == 1:
                    until(pool, k_low, 2 * it.m + pair - 1)
                dst = (rq, rk)[kind][:, pair * 2 * T:(pair + 1) * 2 * T]
                g.tensor_tensor(dst, t1[:, a % 2, :], t2[:, a % 2, :], ALU.add).then_inc(rope_sum, 1)

            def clear(it, k):
                pool.wait_ge(exp_done, 12 * it.n + k + 1)
                pool.sem_inc(clear_begun, 1)
                heads = 2 if k % 3 < 2 else 4
                v = prob[:, (12 * it.par + k) % NP, :].rearrange("p (h t) -> p h t", h=heads)[:, :, 0:TILE]
                g.affine_select(out=v, in_=v, compare_op=ALU.is_ge, fill=0.0, base=0,
                                pattern=[[0, heads], [1, TILE]], channel_multiplier=-1).then_inc(causal, 1)

            def power(it, which):
                pool.wait_ge(var_ready, 2 * it.n + which + 1)
                g.tensor_tensor(rstd[:, :], ve[:, :], neghalf[:, :], ALU.pow).then_inc(rstd_done, 1)

            def residual(it):
                pool.wait_ge(f_out[1], SETUP_F[1])
                pool.wait_ge(xf_in[it.par], 16 * it.half + 16)
                if it.before(1).real:
                    pool.wait_ge(f_out[1], f_job(it.before(1), 3) + 1)
                ob = obias[:, it.layer:it.layer + 1, :].broadcast_to([128, NT, C])
                g.tensor_tensor(xr[:, :, :], xf[:, it.par, :, :], ob, ALU.add).then_inc(xr_done, 1)

            def step(st):
                for tick in range(TICKS):
                    for it, k in due(st, tick, POOL_E):
                        clear(it, k)
                    for it, a in due(st, tick, POOL_MUL):
                        rope_product(it, a)
                    for it, a in due(st, tick, POOL_ADD):
                        rope_total(it, a)
                    for it, _ in due(st, tick, POOL_XR):
                        residual(it)
                    for it, which in due(st, tick, POOL_POW):
                        power(it, which)

            walk(pool, step)

        @block.scalar
        def _(act):
            a_ = nc.scalar

            def loads():
                for dst, name in ((q2l[:, 0, :], "q2l_w"), (q2l[:, 1, :], "kv2l_w"), (wqk[:, :], "wqk_w")):
                    a_.dma_start(dst, W[name]).then_inc(w_in, 16)
                for dst, name in ((lbias[:, 0:1], "q2l_b"), (lbias[:, 1:2], "kv2l_b"), (lbias[:, 2:3], "wqk_b")):
                    a_.dma_start(dst, W[name].rearrange("(p a) -> p a", a=1)).then_inc(w_in, 16)

            def setup():
                for kind in range(2):
                    act.wait_ge(w_pe, 2 + kind)
                    a_.activation(WL[:, kind, :], ps[:, kind, :], ACT.Copy).then_inc(w_act, 1)
                act.wait_ge(w_pe, 5)
                a_.activation(wv[:, 0, :], ps[:, 5, 0:C], ACT.Copy).then_inc(w_act, 1)
                act.wait_ge(w_dve, W_DVE)

            def p_evac(it, k):
                act.wait_ge(p_full, p_job(it, k) + 1)
                if k == 0:
                    if it.before(2).real:
                        act.wait_ge(s1_full[1], v_job(it.before(2)) + 1)
                    a_.activation(xT[:, it.par, :], ps[:, PB, 0:T], ACT.Copy).then_inc(p_out, 1)
                elif it.layer == 0:
                    a = k - 1
                    pair, kind = a // 2, a % 2
                    until(act, rope_mul, 4 * it.m + a - 1)
                    for g in range(2):
                        col = kind * NG + 2 * pair + g
                        for src, dst in ((slice(0, 64), slice(64, 128)), (slice(64, 128), slice(0, 64))):
                            ins = a_.activation(tb[dst, a % 2, g * T:(g + 1) * T], ps[src, PB, g * T:(g + 1) * T],
                                                ACT.Identity, bias=lb[src, col:col + 1])
                    ins.then_inc(swapped, 1)
                else:
                    o = k - 1
                    if it.before(2).layer and o == 0:
                        for half in range(2):
                            parts_free(it, half)
                    a_.activation(parts1[:, it.par, o, 0, :], ps[:, PB, 0:T], ACT.Identity,
                                  bias=bq1[:, o:o + 1]).then_inc(split_a, 1)

            def q_parts(it, pair):
                act.wait_ge(s1_full[1], w_job(it, pair) + 1)
                parts_free(it, pair)
                a_.activation(parts[:, it.par, 0, pair * 512:(pair + 1) * 512], ps[:, S1[1], :], ACT.Identity,
                              bias=wqkbc[:, 0:1]).then_inc(q_high, 1)

            def parts_free(it, half):
                if it.before(2).real:
                    act.wait_ge(stacked[half][it.par], stacked_count(it.before(2)))

            def k_parts(it, pair):
                act.wait_ge(rope_sum, 4 * it.m + 2 * pair + 2)
                parts_free(it, pair)
                cols = slice(pair * 512, (pair + 1) * 512)
                a_.activation(parts[:, it.par, 2, cols], rk[:, cols], ACT.Copy).then_inc(k_high, 1)

            def split_middle(it):
                for o in range(2):
                    act.wait_ge(p_out, p_job(it, o + 1) + 1)
                    a_.activation(parts1[:, it.par, o, 1, :], rest[:, o, :], ACT.Copy).then_inc(split_m, 1)

            def values(it):
                act.wait_ge(s1_full[1], v_job(it) + 1)
                if it.before(2).real:
                    act.wait_ge(pv_done, 12 * it.before(2).n + 12)
                else:
                    act.wait_ge(w_pool, 7)
                a_.activation(vaug[:, it.par, :, :, 0:HD],
                              ps[:, S1[1], 0:T].rearrange("p (n h d) -> p n h d", n=NT, h=NH), ACT.Copy)\
                    .then_inc(s1_out[1], 1)

            def exp(it, k):
                act.wait_ge(s2_full[k % 2], e_job(it, k) + 1)
                if k % 2 == 0:
                    until(act, pv_done, 12 * it.n + k - NP + 2)
                a_.activation(prob[:, (12 * it.par + k) % NP, :], ps[:, S2[k % 2], :], ACT.Exp).then_inc(exp_done, 1)

            def o_evac(it, h):
                act.wait_ge(pv_done, 12 * it.n + 6 * h + 6)
                if h == 0 and it.before(1).real:
                    act.wait_ge(f_full[1], f_job(it.before(1), 1) + 1)
                a_.activation(oT[:, 2 * h:2 * h + 2, :].rearrange("p a t -> p (a t)"), ps[:, OB, :], ACT.Copy)\
                    .then_inc(o_out, 1)

            def f_evac(it, k):
                if k in (2, 4):
                    act.wait_ge(f_full[k % 2], f_job(it, k) + 1)
                    a_.activation((onT if k == 2 else x1T)[:, :], ps[:, FB[k % 2], 0:T], ACT.Copy).then_inc(f_out[k % 2], 1)
                elif it.layer == 0 and k == 5:
                    act.wait_ge(f_out[1], f_job(it, 5) + 1)
                    a_.activation(lex[:, :, :], lsh[:, :, :], ACT.Exp).then_inc(lexp_done, 1)
                elif it.layer == 0 and k == 7:
                    act.wait_ge(f_full[k % 2], f_job(it, k) + 1)
                    a_.activation(gT[:, :], ps[0:NE, FB[k % 2], 0:T], ACT.Copy).then_inc(f_out[k % 2], 1)
                elif it.layer == 1 and k in (5, 6):
                    act.wait_ge(f_full[k % 2], f_job(it, k) + 1)
                    for c in range(2):
                        ch = 2 * (k - 5) + c
                        ins = a_.activation(hT[:, ch, :], ps[:, FB[k % 2], c * T:(c + 1) * T], ACT.Relu, bias=b1h[:, ch:ch + 1])
                    ins.then_inc(f_out[k % 2], 1)

            def step(st):
                if st.base == FIRST:
                    loads()
                    setup()
                for tick in range(TICKS):
                    for it, k in due(st, tick, ACT_E):
                        exp(it, k)
                    for it, half in due(st, tick, ACT_O):
                        o_evac(it, half)
                    for it, k in due(st, tick, ACT_F):
                        f_evac(it, k)
                    for it, k in due(st, tick, ACT_P):
                        p_evac(it, k)
                    for it, pair in due(st, tick, ACT_W):
                        q_parts(it, pair)
                    for it, pair in due(st, tick, ACT_K):
                        k_parts(it, pair)
                    for it, _ in due(st, tick, ACT_SPLIT):
                        split_middle(it)
                    for it, _ in due(st, tick, ACT_V):
                        values(it)

            walk(act, step)

        @block.tensor
        def _(pe):
            mm, tr = nc.tensor.matmul, nc.tensor.transpose

            def setup():
                pe.wait_ge(w_in, 16 * NW)
                pe.wait_ge(w_dve, 4)
                for kind in range(2):
                    mm(ps[:, FB[1], L * kind:L * kind + L], q2lrep[:, kind, :, :].rearrange("p h d -> p (h d)"),
                       cst[0:L, CI:CI + L], start=True, stop=True)
                mm(ps[:, FB[1], 64:64 + L], wqkrep[:, :, :, :].rearrange("p a l b -> p (a l b)"),
                   cst[0:L, CI:CI + L], start=True, stop=True)
                mm(ps[:, FB[1], 96:97], cst[0:L, CE:CE + C], lbias[:, 2:3], start=True, stop=True).then_inc(w_pe, 1)
                for kind in range(2):
                    pe.wait_ge(w_dve, 4 + 6 * (kind + 1))
                    mm(ps[:, kind, :], cattn[:, kind, :], BD[:, kind, :, :].rearrange("p g c -> p (g c)"),
                       start=True, stop=True).then_inc(w_pe, 1)
                for kind in range(2):
                    dst = ps[:, 4, kind * NH:(kind + 1) * NH]
                    mm(dst, qall[:, kind, :], ball[:, kind, :], start=True, stop=False)
                    last = mm(dst, cst[0:L, CE:CE + C], lball[:, kind, :], start=False, stop=True)
                last.then_inc(w_pe, 1)
                tr(ps[:, 5, 0:C], cattn[:, 2, :], ident).then_inc(w_pe, 1)
                pe.wait_ge(w_act, 3)
                pe.wait_ge(w_dve, W_DVE)
                pe.wait_ge(w_pool, 5)

            def setup_f(j):
                if j == 0:
                    pe.wait_ge(w2_in, 16 * NW2)
                    pe.wait_ge(w2_dve, 4)
                else:
                    pe.wait_ge(f_out[1], j)
                bank = ps[:, FB[1], :]
                if j == 0:
                    last = tr(bank[:, 0:C], cproj[:, :], ident)
                elif j == 1:
                    last = tr(ps[0:L, FB[1], 0:HD], l2o[:, :], cst[0:HD, CI:CI + HD])
                elif j == 2:
                    last = mm(bank[:, 0:HD], l2orep[:, :, :].rearrange("p h e -> p (h e)"), q2l[:, 1, :],
                              start=True, stop=True)
                elif j == 3:
                    mm(bank[:, 0:1], l2orep[:, :, :].rearrange("p h e -> p (h e)"), lbias[:, 1:2], start=True, stop=False)
                    last = mm(bank[:, 0:1], cst[0:HD, CE8:CE8 + C], l2ob[:, :], start=False, stop=True)
                elif j == 4:
                    last = mm(bank[:, 0:C], BDM[:, :], cprojT[:, :], start=True, stop=True)
                elif j == 5:
                    mm(bank[:, 0:C], rep[:, 0, :], wo[:, 0, :], start=True, stop=False)
                    mm(bank[:, 0:C], rep[:, 1, :], cprojT[:, :], start=False, stop=False)
                    last = mm(bank[:, 0:C], cst[0:1, CONE:CONE + 128], rowb[:, 0, :], start=False, stop=True)
                elif j in (6, 7):
                    for e in range(4):
                        last = tr(bank[:, e * C:(e + 1) * C], wexp[:, 4 * (j - 6) + e, :], ident)
                elif j == 8:
                    last = mm(bank[:, 0:2], ones, gam[:, 0:2], start=True, stop=True)
                elif j in (9, 10):
                    pe.wait_ge(w2_dve, 11)
                    for a in range(NF):
                        last = tr(bank[:, a * C:(a + 1) * C], (w1n, w2n)[j - 9][:, a * C:(a + 1) * C], ident)
                elif j == 11:
                    for o in range(2):
                        last = mm(bank[:, o:o + 1], perm[:, :], b1l[:, o:o + 1], start=True, stop=True)
                elif j == 12:
                    mm(bank[:, 0:C], rep[:, 2, :], w1l[:, 3, :], start=True, stop=False)
                    last = mm(bank[:, 0:C], cst[0:1, CONE:CONE + 128], rowb[:, 1, :], start=False, stop=True)
                else:
                    last = mm(bank[:, 0:C], cst[0:1, CONE:CONE + 128], rowb[:, 2, :], start=True, stop=True)
                last.then_inc(f_full[1], 1)

            def projection(it, k):
                until(pe, p_out, p_job(it, k))
                bank = ps[:, PB, :]
                if k == 0:
                    pe.wait_ge(x_in[it.par], 16 * it.half + 16)
                    for n in range(NT):
                        last = tr(bank[:, n * TILE:(n + 1) * TILE], xin[:, it.par, n, :], ident)
                elif it.layer == 0:
                    pair, kind = (k - 1) // 2, (k - 1) % 2
                    for g in range(2):
                        last = mm(bank[:, g * T:(g + 1) * T], WL[:, kind, (2 * pair + g) * C:(2 * pair + g + 1) * C],
                                  xT[:, it.par, :], start=True, stop=True)
                else:
                    last = mm(bank[:, 0:T], wq1[:, k - 1, :], xT[:, it.par, :], start=True, stop=True)
                last.then_inc(p_full, 1)

            def query_product(it, pair):
                until(pe, s1_out[1], w_job(it, pair))
                pe.wait_ge(rope_sum, 4 * it.m + 2 * pair + 1)
                mm(ps[:, S1[1], :], BDW[:, :], rq[:, pair * 512:(pair + 1) * 512], start=True, stop=True)\
                    .then_inc(s1_full[1], 1)

            def values(it):
                until(pe, s1_out[1], v_job(it))
                pe.wait_ge(p_out, p_job(it, 0) + 1)
                w = w1l[:, 2, :] if it.layer else wv[:, 0, :]
                for n in range(NT):
                    last = mm(ps[:, S1[1], n * C:(n + 1) * C], xT[:, it.par, n * TILE:(n + 1) * TILE], w,
                              start=True, stop=True)
                last.then_inc(s1_full[1], 1)

            def scores_for_max(it, k):
                b, u, r = k % 2, k // 3, k % 3
                q, kk = QS[it.layer][it.par], KS[it.layer][it.par]
                if k in (0, 6):
                    pe.wait_ge(stacked[k // 6][it.par], stacked_count(it))
                until(pe, s1_out[b], m_job(it, k))
                bank = ps[:, S1[b], :]
                if r == 0:
                    for j in range(4):
                        mm(bank[:, j * TILE:(j + 1) * TILE], q[0:MAXROW, 4 * u + j, 0:TILE],
                           kk[0:MAXROW, 4 * u + j, 0:TILE], start=(j == 0), stop=False)
                    last = mm(bank, identb[:, :], maskb[:, :, :].rearrange("p h t -> p (h t)"), start=False, stop=True)
                else:
                    for j in range(2):
                        h = 4 * u + 2 * (r - 1) + j
                        mm(bank[:, j * T:(j + 1) * T], q[0:MAXROW, h, TILE:T], kk[0:MAXROW, h, :],
                           start=(j == 0), stop=False)
                    last = mm(bank.rearrange("p (h t) -> p h t", h=2)[:, :, TILE:T], identb[:, :], maskb[:, 0:2, :],
                              start=False, stop=True)
                last.then_inc(s1_full[b], 1)

            def transpose_max(it, half):
                pe.wait_ge(nm_part, 2 * it.n + half + 1)
                until(pe, s1_out[0], mt_job(it, half))
                bank = ps[0:MAXROWS, S1[0], :].bitcast(BF16)
                for n in range(NT):
                    last = tr(bank[:, n * TILE:(n + 1) * TILE],
                              nmb[:, it.par, n, half, :, :].rearrange("p a h -> p (a h)"), identb[:, :])
                last.then_inc(s1_full[0], 1)

            def scores_for_exp(it, k):
                b, u, r = k % 2, k // 3, k % 3
                q, kk = QS[it.layer][it.par], KS[it.layer][it.par]
                if k in (0, 6):
                    pe.wait_ge(max_in[k // 6][it.par], 16 * it.half + 16)
                    if isinstance(it.n, int) and it.n < 2:
                        pe.wait_ge(w_dve, W_DVE + 4)
                until(pe, exp_done, 12 * it.n + k - 1)
                bank = ps[:, S2[b], :]
                if r < 2:
                    for j in range(2):
                        h = 4 * u + 2 * r + j
                        last = mm(bank[:, j * T:(j + 1) * T], kk[0:STACKED, h, 0:TILE], q[0:STACKED, h, :],
                                  start=True, stop=True)
                else:
                    for j in range(4):
                        h = 4 * u + j
                        last = mm(bank[:, j * TILE:(j + 1) * TILE], kk[0:STACKED, h, TILE:T], q[0:STACKED, h, TILE:T],
                                  start=True, stop=True)
                last.then_inc(s2_full[b], 1)

            def times_values(it, k):
                u, r = k // 3, k % 3
                pe.wait_ge(causal, 12 * it.n + k + 1)
                if k == 0:
                    pe.wait_ge(s1_out[1], v_job(it) + 1)
                if k % 6 == 0:
                    until(pe, o_out, 2 * it.n + k // 6)
                base = (u % 2) * T
                for i in range(2 if r < 2 else 4):
                    j = 2 * r + i if r < 2 else i
                    rows = slice(32 * j, 32 * j + OW)
                    if r < 2:
                        last = mm(ps[rows, OB, base:base + T], vaug[:, it.par, 0, 4 * u + j, :],
                                  prob[:, (12 * it.par + k) % NP, i * T:(i + 1) * T], start=True, stop=False)
                    else:
                        last = mm(ps[rows, OB, base + TILE:base + T], vaug[:, it.par, 1, 4 * u + j, :],
                                  prob[:, (12 * it.par + k) % NP, i * TILE:(i + 1) * TILE], start=False, stop=True)
                last.then_inc(pv_done, 1)

            def f_product(it, k):
                if k < 3 or k > 9:
                    until(pe, f_out[k % 2], f_job(it, k))
                if k in (2, 3, 5) or (k == 8 or it.layer and k == 6):
                    pe.wait_ge(f_out[(k - 1) % 2], f_job(it, k - 1) + 1)
                if k == 7 and it.layer:
                    pe.wait_ge(f_out[1], f_job(it, 5) + 1)
                    pe.wait_ge(f_out[0], f_job(it, 6) + 1)
                bank = ps[:, FB[k % 2], :]
                if k < 2:
                    pe.wait_ge(o_out, 2 * it.n + 2)
                    for u in range(NG):
                        last = tr(bank[:, u * TILE:(u + 1) * TILE], oT[:, u, k * TILE:(k + 1) * TILE], ident)
                elif k == 2:
                    for n in range(NT):
                        last = tr(bank[:, n * TILE:(n + 1) * TILE], on[:, n, :], ident)
                elif k == 3:
                    w = w1l[:, 3, :] if it.layer else wo[:, 0, :]
                    for n in range(NT):
                        last = mm(bank[:, n * C:(n + 1) * C], onT[:, n * TILE:(n + 1) * TILE], w, start=True, stop=True)
                elif k == 4:
                    pe.wait_ge(x1_ready, it.n + 1)
                    for n in range(NT):
                        last = tr(bank[:, n * TILE:(n + 1) * TILE], x1[:, n, :], ident)
                elif it.layer == 0:
                    last = moe(it, k, bank)
                else:
                    last = mlp(k, bank)
                last.then_inc(f_full[k % 2], 1)

            def moe(it, k, bank):
                if k == 5:
                    for n in range(NT):
                        last = mm(bank[:, n * NE:(n + 1) * NE], x1T[:, n * TILE:(n + 1) * TILE], wgate[:, :],
                                  start=True, stop=True)
                elif k == 6:
                    pe.wait_ge(onehot_ready, it.m + 1)
                    for n in range(NT):
                        dst = bank[:, n * NE:(n + 1) * NE]
                        mm(dst, triub[:, :], oh[:, n, :], start=True, stop=False)
                        if n:
                            mm(dst, onesb[:, :], oh[:, 0, :], start=False, stop=False)
                        last = mm(dst, onesb[:, :], seen[:, :], start=False, stop=True)
                elif k == 7:
                    pe.wait_ge(gate_ready, it.m + 1)
                    for n in range(NT):
                        last = tr(ps[0:NE, FB[1], n * TILE:(n + 1) * TILE], gate[:, n, :], ident)
                elif k == 8:
                    for n in range(NT):
                        last = mm(bank[:, n * C:(n + 1) * C], gT[:, n * TILE:(n + 1) * TILE], bexp[:, :],
                                  start=True, stop=True)
                else:
                    e = 2 * (k - 9)
                    for n in range(NT):
                        last = mm(bank[:, n * 2 * C:(n + 1) * 2 * C], x1T[:, n * TILE:(n + 1) * TILE],
                                  wexpT[:, e:e + 2, :].rearrange("p e c -> p (e c)"), start=True, stop=True)
                return last

            def mlp(k, bank):
                if k in (5, 6):
                    for c in range(2):
                        last = mm(bank[:, c * T:(c + 1) * T], w1T[:, 2 * (k - 5) + c, :], x1T[:, :], start=True, stop=True)
                else:
                    for n in range(NT):
                        for c in range(NF):
                            last = mm(bank[:, n * C:(n + 1) * C], hT[:, c, n * TILE:(n + 1) * TILE], w2T[:, c, :],
                                      start=(c == 0), stop=(c == NF - 1))
                return last

            def step(st):
                if st.base == FIRST:
                    setup()
                for tick in range(TICKS):
                    for it, k in due(st, tick, PE_F):
                        f_product(it, k)
                    for it, k in due(st, tick, PE_M):
                        scores_for_max(it, k)
                    for it, k in due(st, tick, PE_E):
                        scores_for_exp(it, k)
                    for it, k in due(st, tick, PE_PV):
                        times_values(it, k)
                    for it, k in due(st, tick, PE_P):
                        projection(it, k)
                    for it, pair in due(st, tick, PE_W):
                        query_product(it, pair)
                    if st.base == SETUP_STEP and tick in SETUP_TIMES:
                        setup_f(SETUP_TIMES.index(tick))
                    for it, _ in due(st, tick, PE_V):
                        values(it)
                    for it, half in due(st, tick, PE_MT):
                        transpose_max(it, half)

            walk(pe, step)

        @block.vector
        def _(dve):
            v = nc.vector

            def setup():
                for p in range(2):
                    dve.sem_inc(xo_stored[p], 16)
                dve.wait_ge(w_in, 16 * NW)
                v.tensor_copy(q2lrep[:, :, :, :],
                              q2l[:, :, :].rearrange("p k (a d) -> p k a d", a=1).broadcast_to([L, 2, NH, HD]))\
                    .then_inc(w_dve, 1)
                v.tensor_copy(wqkrep[:, :, :, :],
                              wqk[:, :].rearrange("p (l a b) -> p a l b", a=2, b=1).broadcast_to([L, 2, L // 2, 4]))\
                    .then_inc(w_dve, 1)
                v.tensor_copy(lball[:, :, :], lbias[:, 0:2].rearrange("p (k a) -> p k a", a=1).broadcast_to([L, 2, NH]))\
                    .then_inc(w_dve, 1)
                v.tensor_copy(ball[:, :, :], cattnb[:, 0:2].rearrange("p (k a) -> p k a", a=1)
                              .broadcast_to([128, 2, NH])).then_inc(w_dve, 1)
                dve.wait_ge(w_dve, 4)
                dve.wait_ge(w_pe, 1)
                shape = [128, 2, L // 2, 4]
                for kind in range(2):
                    src = ps[:, FB[1], L * kind:L * kind + L].rearrange("p (l a b) -> p a l b", a=2, b=1)
                    for g in range(NG):
                        own = hm.rearrange("p (h j b) -> p h j b", h=2, j=4)[:, g // 2, :, g % 2]
                        own = own.rearrange("p (a l j) -> p a l j", a=1, l=1)
                        v.tensor_tensor(BD[:, kind, g, :].rearrange("p (a l b) -> p a l b", a=2, b=4),
                                        src.broadcast_to(shape), own.broadcast_to(shape), ALU.mult).then_inc(w_dve, 1)
                    v.tensor_copy(qall[:, kind, :].rearrange("p (a l b) -> p a l b", a=2, b=4),
                                  src.broadcast_to(shape)).then_inc(w_dve, 1)
                    v.tensor_tensor(ball[:, kind, :], ball[:, kind, :], hm, ALU.mult).then_inc(w_dve, 1)
                src = ps[:, FB[1], 64:64 + L].rearrange("p (l a b) -> p a l b", a=2, b=1).broadcast_to(shape)
                own = cst[:, CJM:CJM + 4].rearrange("p (a l j) -> p a l j", a=1, l=1).broadcast_to(shape)
                v.tensor_tensor(BDW[:, :].rearrange("p (a l b) -> p a l b", a=2, b=4), src, own, ALU.mult)\
                    .then_inc(w_dve, 1)
                v.tensor_scalar(wqkbc[:, :], ps[:, FB[1], 96:97], float(L) ** -0.5, None, ALU.mult).then_inc(w_dve, 1)
                v.tensor_copy(identb[:, :], ident).then_inc(w_dve, 1)
                v.tensor_copy(triub[:, :], cst[:, CU:CU + 128]).then_inc(w_dve, 1)
                v.tensor_copy(onesb[:, :], ones).then_inc(w_dve, 1)
                v.memset(seen[:, :], 0.0).then_inc(w_dve, 1)
                dve.wait_ge(w_pe, 4)
                own = cst[:, CJ:CJ + 4].rearrange("p (k a j b) -> p k a j b", k=1, a=1, b=1)
                for kind in range(2):
                    v.tensor_tensor(bsel[:, kind, :, :].rearrange("p (a b) j -> p a j b", a=2),
                                    ps[:, 4, kind * NH:(kind + 1) * NH].rearrange("p (a j b) -> p a j b", a=2, j=4),
                                    own[:, 0].broadcast_to([128, 2, 4, 2]), ALU.mult).then_inc(w_dve, 1)
                dve.wait_ge(w_dve, LB_DVE)
                v.tensor_reduce(lb[:, :], bsel[:, :, :, :].rearrange("p k g j -> p (k g) j"), AX.X, ALU.add)\
                    .then_inc(w_dve, 1)
                v.tensor_copy(perm[:, :].rearrange("p (a d b) -> p a d b", a=2, d=HD),
                              ident.rearrange("p (a b d) -> p a d b", a=2, d=HD)).then_inc(w_dve, 1)

            def selector(k):
                sel = cst[MAXROW:STACKED, CSEL:CSEL + NH].rearrange("p (h a) -> p h a", a=1).broadcast_to([MAXROWS, NH, T])
                v.tensor_copy(KS[k // 2][k % 2][MAXROW:STACKED, :, :], sel).then_inc(w_dve, 1)

            def setup_2():
                dve.wait_ge(w2_in, 16 * NW2)
                v.tensor_copy(rep[:, 0, :], cattnb[:, 2:3].broadcast_to([128, C])).then_inc(w2_dve, 1)
                v.tensor_copy(rep[:, 2, :], b1l[:, 2:3].broadcast_to([128, C])).then_inc(w2_dve, 1)
                v.tensor_reduce(gam[:, 0:1], w1n[:, :], AX.X, ALU.add, apply_absolute_value=True).then_inc(w2_dve, 1)
                v.tensor_reduce(gam[:, 1:2], w2n[:, :], AX.X, ALU.add, apply_absolute_value=True).then_inc(w2_dve, 1)
                for o in range(2):
                    v.tensor_scalar(wq1[:, o, :].rearrange("p (a d b) -> p a d b", a=2, d=HD),
                                    w1l[:, o, :].rearrange("p (a b d) -> p a d b", a=2, d=HD),
                                    (float(HD) ** -0.5, 1.0)[o], None, ALU.mult).then_inc(w2_dve, 1)

            def setup_f(j):
                dve.wait_ge(f_full[1], j + 1)
                bank = ps[:, FB[1], :]
                if j == 0:
                    last = v.tensor_copy(cprojT[:, :], bank[:, 0:C])
                elif j == 1:
                    last = v.tensor_copy(l2orep[:, :, :], ps[0:L, FB[1], 0:HD].rearrange("p (a e) -> p a e", a=1)
                                         .broadcast_to([L, NH, HD]))
                elif j == 2:
                    last = v.tensor_tensor(BDM[:, :].rearrange("p (h d) -> p h d", h=NH),
                                           bank[:, 0:HD].rearrange("p (a d) -> p a d", a=1).broadcast_to([128, NH, HD]),
                                           hm.rearrange("p (h a) -> p h a", a=1).broadcast_to([128, NH, HD]), ALU.mult)
                elif j == 3:
                    last = v.tensor_copy(rep[:, 1, :], bank[:, 0:1].broadcast_to([128, C]))
                elif j == 4:
                    last = v.tensor_copy(wo[:, 0, :], bank[:, 0:C])
                elif j == 5:
                    last = v.tensor_copy(obias[:, 0, :], bank[:, 0:C])
                elif j in (6, 7):
                    last = v.tensor_copy(wexpT[:, 4 * (j - 6):4 * (j - 6) + 4, :].rearrange("p e c -> p (e c)"), bank)
                elif j == 8:
                    last = v.tensor_scalar(gam[:, 2:4], bank[:, 0:2], 1.0 / (NF * C * C), EPS, ALU.mult, ALU.add)
                elif j in (9, 10):
                    last = v.tensor_copy((w1T, w2T)[j - 9][:, :, :].rearrange("p a c -> p (a c)"), bank)
                elif j == 11:
                    v.tensor_scalar(bq1[:, 0:1], bank[:, 0:1], float(HD) ** -0.5, None, ALU.mult)
                    last = v.tensor_copy(bq1[:, 1:2], bank[:, 1:2])
                elif j == 12:
                    last = v.tensor_copy(obias[:, 1, :], bank[:, 0:C])
                else:
                    last = v.tensor_copy(b2row[:, :], bank[:, 0:C])
                last.then_inc(f_out[1], 1)
                if j == 8:
                    dve.wait_ge(f_out[1], 9)
                    v.tensor_scalar(gam[:, 4:6], gam[:, 2:4], 0.5, None, ALU.mult)
                    v.tensor_scalar(gam[:, 6:8], gam[:, 2:4], -0.5, None, ALU.mult).then_inc(w2_dve, 1)
                    dve.wait_ge(w2_dve, 7)
                    for n, w in enumerate((w1n, w2n)):
                        v.tensor_scalar(qtmp[:, n, :], w[:, :], gam[:, 6 + n:7 + n], None, ALU.is_lt).then_inc(w2_dve, 1)
                    dve.wait_ge(w2_dve, 9)
                    for n, w in enumerate((w1n, w2n)):
                        v.scalar_tensor_tensor(out=w[:, :], in0=w[:, :], scalar=gam[:, 4 + n:5 + n],
                                               in1=qtmp[:, n, :], op0=ALU.is_gt, op1=ALU.subtract).then_inc(w2_dve, 1)

            def p_evac(it, k):
                if it.layer == 0:
                    a = k - 1
                    pair, kind = a // 2, a % 2
                    dve.wait_ge(swapped, 4 * it.m + a + 1)
                    until(dve, rope_sum, 4 * it.m + a - 1)
                    for g in range(2):
                        col = kind * NG + 2 * pair + g
                        last = v.scalar_tensor_tensor(out=t1[:, a % 2, g * T:(g + 1) * T],
                                                      in0=ps[:, PB, g * T:(g + 1) * T], scalar=lb[:, col:col + 1],
                                                      in1=cst[:, CCOS:CCOS + T], op0=ALU.add, op1=ALU.mult)
                    last.then_inc(p_out, 1)
                else:
                    o = k - 1
                    dve.wait_ge(split_a, 2 * it.m + o + 1)
                    until(dve, split_l, 2 * it.m)
                    v.scalar_tensor_tensor(out=rest[:, o, :], in0=ps[:, PB, 0:T], scalar=bq1[:, o:o + 1],
                                           in1=parts1[:, it.par, o, 0, :], op0=ALU.add, op1=ALU.subtract)\
                        .then_inc(p_out, 1)

            def q_parts(it, pair):
                dve.wait_ge(q_high, 2 * it.m + pair + 1)
                cols = slice(pair * 512, (pair + 1) * 512)
                v.scalar_tensor_tensor(out=parts[:, it.par, 1, cols], in0=ps[:, S1[1], :], scalar=wqkbc[:, 0:1],
                                       in1=parts[:, it.par, 0, cols], op0=ALU.add, op1=ALU.subtract)\
                    .then_inc(s1_out[1], 1)

            def k_parts(it, pair):
                dve.wait_ge(k_high, 2 * it.m + pair + 1)
                cols = slice(pair * 512, (pair + 1) * 512)
                v.tensor_tensor(parts[:, it.par, 3, cols], rk[:, cols], parts[:, it.par, 2, cols], ALU.subtract)\
                    .then_inc(k_low, 1)

            def split_low(it):
                for o in range(2):
                    dve.wait_ge(split_m, 2 * it.m + o + 1)
                    v.tensor_tensor(parts1[:, it.par, o, 2, :], rest[:, o, :], parts1[:, it.par, o, 1, :], ALU.subtract)\
                        .then_inc(split_l, 1)

            def row_max(it, k):
                b, u, r = k % 2, k // 3, k % 3
                dve.wait_ge(s1_full[b], m_job(it, k) + 1)
                if r == 0:
                    v.tensor_reduce(nm[:, it.par, 0, 4 * u:4 * u + 4], ps[:, S1[b], :].rearrange("p (h t) -> p h t", h=4),
                                    AX.X, ALU.max, negate=True).then_inc(s1_out[b], 1)
                else:
                    h = 4 * u + 2 * (r - 1)
                    v.tensor_reduce(nm[:, it.par, 1, h:h + 2], ps[:, S1[b], :].rearrange("p (h t) -> p h t", h=2),
                                    AX.X, ALU.max, negate=True).then_inc(s1_out[b], 1)

            def max_parts(it, half):
                src = nm[:, it.par, :, 8 * half:8 * half + 8]
                dve.wait_ge(s1_out[1], m_job(it, 6 * half + 5) + 1)
                dve.wait_ge(s1_out[0], m_job(it, 6 * half + 4) + 1)
                v.tensor_copy(nmb[:, it.par, :, half, 0, :], src).then_inc(nm_high, 1)
                dve.wait_ge(nm_high, 2 * it.n + half + 1)
                v.tensor_tensor(nmb[:, it.par, :, half, 1, :], src, nmb[:, it.par, :, half, 0, :], ALU.subtract)\
                    .then_inc(nm_part, 1)

            def max_evac(it, half):
                dve.wait_ge(s1_full[0], mt_job(it, half) + 1)
                v.tensor_copy(mT[:, it.par, half, :], ps[0:MAXROWS, S1[0], :].bitcast(BF16)[:, 0:T]).then_inc(s1_out[0], 1)

            def f_chain(it, start):
                count = [start]

                def link(ins):
                    count[0] += 1
                    ins.then_inc(f_dve, 1)
                    dve.wait_ge(f_dve, count[0])
                return link

            def statistics(src, link):
                v.bn_stats(stats[:, 0, :], src[:, 0, :])
                link(v.bn_stats(stats[:, 1, :], src[:, 1, :]))
                dve.sem_inc(stats_seen, 1)
                v.bn_aggr(mv[:, 0, :], stats[:, 0, :])
                link(v.bn_aggr(mv[:, 1, :], stats[:, 1, :]))
                v.tensor_scalar(ve[:, :], mv[:, :, 1], EPS, None, ALU.add).then_inc(var_ready, 1)

            def normalise(it, which):
                dve.wait_ge(rstd_done, 2 * it.n + which + 1)
                src = y if which == 0 or it.layer else acc
                if which == 0:
                    dst, signal = x1, x1_ready
                else:
                    dst, signal = xo[:, it.par, :, :], xo_ready
                    dve.wait_ge(xo_stored[it.par], 16 * it.half + 16)
                for n in range(NT):
                    last = v.tensor_scalar(dst[:, n, :], src[:, n, :], mv[:, n, 0:1], rstd[:, n:n + 1],
                                           ALU.subtract, ALU.mult)
                last.then_inc(signal, 1)

            def f_step(it, k):
                bank = ps[:, FB[k % 2], :]
                if k in (0, 1, 3) or (it.layer == 0 and k in (5, 6, 8, 9, 10, 11, 12)) or (it.layer == 1 and k == 7):
                    dve.wait_ge(f_full[k % 2], f_job(it, k) + 1)
                if k < 2:
                    link = f_chain(it, k)
                    heads = bank.rearrange("p (h w) -> p h w", w=OW)
                    link(v.reciprocal(rden[:, k, :], heads[:, :, HD]))
                    v.tensor_tensor(on[:, k, :].rearrange("p (h d) -> p h d", d=HD), heads[:, :, 0:HD],
                                    rden[:, k, :].rearrange("p (h a) -> p h a", a=1).broadcast_to([128, NH, HD]), ALU.mult)\
                        .then_inc(f_out[k % 2], 1)
                elif k == 3:
                    dve.wait_ge(xr_done, it.n + 1)
                    v.tensor_tensor(y[:, :, :].rearrange("p n c -> p (n c)"), bank[:, 0:T],
                                    xr[:, :, :].rearrange("p n c -> p (n c)"), ALU.add).then_inc(f_out[k % 2], 1)
                    dve.wait_ge(f_out[k % 2], f_job(it, 3) + 1)
                    statistics(y, f_chain(it, 2))
                elif it.layer == 0:
                    moe_step(it, k, bank)
                elif k == 4:
                    dve.wait_ge(x1_ready, it.n + 1)
                    link = f_chain(it, 4)
                    link(v.tensor_tensor(acc[:, :, :], x1[:, :, :],
                                         b2row[:, :].rearrange("p (a c) -> p a c", a=1).broadcast_to([128, NT, C]), ALU.add))
                elif k == 7:
                    v.tensor_tensor(y[:, :, :].rearrange("p n c -> p (n c)"), bank[:, 0:T],
                                    acc[:, :, :].rearrange("p n c -> p (n c)"), ALU.add).then_inc(f_out[k % 2], 1)
                    dve.wait_ge(f_out[k % 2], f_job(it, 7) + 1)
                    statistics(y, f_chain(it, 5))
                    dve.sem_clear(f_dve)

            def moe_step(it, k, bank):
                two = [128, NT, NE]

                def wide(ap):
                    return ap.rearrange("p (n a) -> p n a", a=1).broadcast_to(two)

                if k == 5:
                    logits = bank[:, 0:NT * NE].rearrange("p (n e) -> p n e", e=NE)
                    link = f_chain(it, 4)
                    link(v.tensor_reduce(lmax[:, :], logits, AX.X, ALU.max))
                    v.tensor_tensor(lsh[:, :, :], logits, wide(lmax[:, :]), ALU.subtract).then_inc(f_out[k % 2], 1)
                    dve.wait_ge(lexp_done, it.m + 1)
                    link(v.tensor_reduce(lsum[:, :], lex[:, :, :], AX.X, ALU.add))
                    link(v.reciprocal(lrec[:, :], lsum[:, :]))
                    link(v.tensor_tensor(pr[:, :, :], lex[:, :, :], wide(lrec[:, :]), ALU.mult))
                    link(v.tensor_reduce(pmax[:, :], pr[:, :, :], AX.X, ALU.max))
                    link(v.tensor_tensor(peq[:, :, :], pr[:, :, :], wide(pmax[:, :]), ALU.is_equal))
                    order = cst[:, CW:CW + NE].rearrange("p (a e) -> p a e", a=1).broadcast_to(two)
                    link(v.tensor_tensor(pk[:, :, :], peq[:, :, :], order, ALU.mult))
                    link(v.tensor_reduce(pkm[:, :], pk[:, :, :], AX.X, ALU.max))
                    v.tensor_tensor(oh[:, :, :], pk[:, :, :], wide(pkm[:, :]), ALU.is_equal).then_inc(onehot_ready, 1)
                elif k == 6:
                    link = f_chain(it, 12)
                    before = bank[:, 0:NT * NE].rearrange("p (n e) -> p n e", e=NE)
                    v.scalar_tensor_tensor(out=kept[:, :, :], in0=before, scalar=float(CAP), in1=oh[:, :, :],
                                           op0=ALU.is_lt, op1=ALU.mult).then_inc(f_out[k % 2], 1)
                    dve.wait_ge(f_out[k % 2], f_job(it, 6) + 1)
                    v.tensor_tensor(gate[:, :, :], kept[:, :, :], wide(pmax[:, :]), ALU.mult).then_inc(gate_ready, 1)
                    link(v.tensor_tensor(ohs[:, :], oh[:, 0, :], oh[:, 1, :], ALU.add))
                    link(v.tensor_tensor(seen[:, :], seen[:, :], ohs[:, :], ALU.add))
                elif k == 8:
                    dve.wait_ge(x1_ready, it.n + 1)
                    v.tensor_tensor(acc[:, :, :].rearrange("p n c -> p (n c)"), bank[:, 0:T],
                                    x1[:, :, :].rearrange("p n c -> p (n c)"), ALU.add).then_inc(f_out[k % 2], 1)
                    dve.wait_ge(f_out[k % 2], f_job(it, 8) + 1)
                elif k >= 9:
                    start = 14 + 3 * (k - 9)
                    for j in range(2 * NT):
                        e, n = j // NT, j % NT
                        if j < 2 and k > 9:
                            if j == 0:
                                dve.wait_ge(f_dve, start)
                            else:
                                dve.wait_ge(f_out[(k - 1) % 2], f_job(it, k - 1) + 1)
                        if j >= 2:
                            dve.wait_ge(f_dve, start + j - 1)
                        ins = v.scalar_tensor_tensor(out=acc[:, n, :],
                                                     in0=bank[:, (2 * n + e) * C:(2 * n + e + 1) * C],
                                                     scalar=gate[:, n, 2 * (k - 9) + e:2 * (k - 9) + e + 1],
                                                     in1=acc[:, n, :], op0=ALU.mult, op1=ALU.add)
                        ins.then_inc(f_dve if j < 3 else f_out[k % 2], 1)
                    if k == 12:
                        dve.wait_ge(f_dve, 26)
                        dve.wait_ge(f_out[0], f_job(it, 12) + 1)
                        statistics(acc, f_chain(it, 26))
                        dve.sem_clear(f_dve)

            def step(st):
                if st.base == FIRST:
                    setup()
                if st.base == SETUP_STEP:
                    setup_2()
                for tick in range(TICKS):
                    for it, which in due(st, tick, DVE_NORM):
                        normalise(it, which)
                    for it, k in due(st, tick, DVE_F):
                        f_step(it, k)
                    for it, k in due(st, tick, DVE_M):
                        row_max(it, k)
                    for it, half in due(st, tick, DVE_PARTS):
                        max_parts(it, half)
                    for it, k in due(st, tick, DVE_P):
                        p_evac(it, k)
                    for it, pair in due(st, tick, DVE_W):
                        q_parts(it, pair)
                    for it, pair in due(st, tick, DVE_K):
                        k_parts(it, pair)
                    for it, _ in due(st, tick, DVE_SPLIT):
                        split_low(it)
                    if st.base == SETUP_STEP and tick in SETUP_TIMES:
                        setup_f(SETUP_TIMES.index(tick))
                    if st.base == FIRST and tick in SELECTOR_TIMES:
                        selector(SELECTOR_TIMES.index(tick))
                    for it, half in due(st, tick, DVE_MT):
                        max_evac(it, half)

            walk(dve, step)


_W = (("c_attn_w", "L0_attn_c_attn_w"), ("c_attn_b", "L0_attn_c_attn_b"), ("q2l_w", "L0_attn_q2l_w"),
      ("q2l_b", "L0_attn_q2l_b"), ("kv2l_w", "L0_attn_kv2l_w"), ("kv2l_b", "L0_attn_kv2l_b"),
      ("l2o_w", "L0_attn_l2o_w"), ("l2o_b", "L0_attn_l2o_b"), ("wqk_w", "L0_attn_wqk_w"),
      ("wqk_b", "L0_attn_wqk_b"), ("cproj_w", "L0_attn_cproj_w"), ("cproj_b", "L0_attn_cproj_b"),
      ("wg", "L0_ffn_wg"), ("W", "L0_ffn_W"), ("b", "L0_ffn_b"), ("Wq", "L1_attn_Wq"), ("bq", "L1_attn_bq"),
      ("Wk", "L1_attn_Wk"), ("bk", "L1_attn_bk"), ("Wv", "L1_attn_Wv"), ("bv", "L1_attn_bv"),
      ("Wo", "L1_attn_Wo"), ("bo", "L1_attn_bo"), ("W1", "L1_ffn_W1"), ("b1", "L1_ffn_b1"),
      ("W2", "L1_ffn_W2"), ("b2", "L1_ffn_b2"))


def kernel(**inputs):
    import numpy as np
    import concourse.bacc as bacc
    from concourse.bass_utils import run_bass_kernel_spmd

    nc = bacc.Bacc("TRN2", target_bir_lowering=False, num_devices=1)
    arrays = {}

    def dram(name, a):
        a = np.ascontiguousarray(a)
        arrays[name] = a
        return nc.dram_tensor(name, a.shape, mybir.dt.from_np(a.dtype), kind="ExternalInput").ap()

    x = dram("x", inputs["L0_attn_x"])
    c = dram("shape_constants", constants())
    w = {short: dram(long, inputs[long]) for short, long in _W}
    out = nc.dram_tensor("out", (NB, T, C), F32, kind="ExternalOutput").ap()
    build(nc, x, c, w, out)
    r = run_bass_kernel_spmd(nc, [arrays], core_ids=[0])
    return r.results[0]["out"]
```
